# Optimizing a Trainium2 kernel written in Bass

```python
import numpy as np
import jax
import jax.numpy as jnp

def _softmax(x, axis=-1):
    return jax.nn.softmax(x, axis=axis)

def _gelu(x):
    return jax.nn.gelu(x, approximate=True)

def _silu(x):
    return jax.nn.silu(x)

def _sigmoid(x):
    return jax.nn.sigmoid(x)

def _layernorm(x, axis=-1, eps=1e-05):
    m = jnp.mean(x, axis=axis, keepdims=True)
    v = jnp.var(x, axis=axis, keepdims=True)
    return (x - m) / jnp.sqrt(v + eps)

def _scatter_add(tgt, idx, src, axis=0):
    return tgt.at[idx].add(src)

def _segment_sum(src, seg, n):
    return jax.ops.segment_sum(src, seg, n)
kernel_name = 'mk_macaron_d2_jaxref_r8_e49966'

def setup_inputs(seed: int=0):
    np.random.seed(seed)
    _w = jnp.asarray

    def _L0_attn_setup():
        import jax, jax.numpy as jnp
        import numpy as np
        import math
        B, T, D = (2, 256, 128)
        N_HEADS = 16
        D_HEAD = D // N_HEADS

        def _rope_tables(t, d_head, dtype=jnp.float32):
            theta = 1.0 / 10000.0 ** (jnp.arange(0, d_head, 2, dtype=jnp.float32) / d_head)
            angles = jnp.outer(jnp.arange(t, dtype=jnp.float32), theta)
            angles = jnp.concatenate([angles, angles], axis=-1)
            return (jnp.cos(angles).astype(dtype), jnp.sin(angles).astype(dtype))

        def _rotate_half(x):
            half = x.shape[-1] // 2
            return jnp.concatenate([-x[..., half:], x[..., :half]], axis=-1)

        def _apply_rope(x, cos, sin):
            return x * cos[None, None] + _rotate_half(x) * sin[None, None]
        key = jax.random.key(seed)
        k1, k2, k3, k4 = jax.random.split(key, 4)
        s_in = 1.0 / math.sqrt(D)
        return {'x': jax.random.normal(k1, (B, T, D), dtype=jnp.float32), 'w_qkv': jax.random.normal(k2, (D, 3 * D), dtype=jnp.float32) * s_in, 'w_out': jax.random.normal(k3, (D, D), dtype=jnp.float32) * s_in, 'b_out': jax.random.normal(k4, (D,), dtype=jnp.float32) * 0.01}
    _L0_attn_in = _L0_attn_setup()

    def _L0_ffn_setup():
        import jax, jax.numpy as jnp
        import numpy as np
        TOP_K = 2
        key = jax.random.key(seed)
        k0, k1, k2, k3, k4 = jax.random.split(key, 5)
        B, S, D, H, E = (4, 256, 128, 256, 8)
        x = jax.random.normal(k0, (B, S, D), dtype=jnp.float32)
        router_w = jax.random.normal(k1, (E, D), dtype=jnp.float32) * D ** (-0.5)
        w_gate = jax.random.normal(k2, (E, D, H), dtype=jnp.float32) * D ** (-0.5)
        w_up = jax.random.normal(k3, (E, D, H), dtype=jnp.float32) * D ** (-0.5)
        w_down = jax.random.normal(k4, (E, H, D), dtype=jnp.float32) * H ** (-0.5)
        return {'x': x, 'router_w': router_w, 'w_gate': w_gate, 'w_up': w_up, 'w_down': w_down}
    _L0_ffn_in = _L0_ffn_setup()

    def _L1_attn_setup():
        import jax, jax.numpy as jnp
        import numpy as np
        import math
        DK = 128
        key = jax.random.key(seed)
        k1, k2 = jax.random.split(key)
        x = jax.random.normal(k1, (4, 256, 128), dtype=jnp.float32)
        W = jax.random.normal(k2, (128, 3 * DK), dtype=jnp.float32) * (1.0 / math.sqrt(128))
        b = jnp.zeros((3 * DK,), dtype=jnp.float32)
        return {'x': x, 'W': W, 'b': b}
    _L1_attn_in = _L1_attn_setup()

    def _L1_ffn_setup():
        import jax, jax.numpy as jnp
        import numpy as np
        D_MODEL, D_FF, RANK = (128, 512, 32)
        B, S = (4, 512)
        key = jax.random.key(seed)
        ks = jax.random.split(key, 7)
        return {'x': jax.random.normal(ks[0], (B, S, D_MODEL), dtype=jnp.float32), 'U1': jax.random.normal(ks[1], (D_MODEL, RANK), dtype=jnp.float32) * 0.02, 'V1': jax.random.normal(ks[2], (RANK, D_FF), dtype=jnp.float32) * 0.02, 'b1': jnp.zeros((D_FF,), dtype=jnp.float32), 'U2': jax.random.normal(ks[3], (D_FF, RANK), dtype=jnp.float32) * 0.02, 'V2': jax.random.normal(ks[4], (RANK, D_MODEL), dtype=jnp.float32) * 0.02, 'b2': jnp.zeros((D_MODEL,), dtype=jnp.float32)}
    _L1_ffn_in = _L1_ffn_setup()
    _d = {'L0_attn_x': _L0_attn_in['x'], 'L0_attn_w_qkv': _L0_attn_in['w_qkv'], 'L0_attn_w_out': _L0_attn_in['w_out'], 'L0_attn_b_out': _L0_attn_in['b_out'], 'L0_ffn_router_w': _L0_ffn_in['router_w'], 'L0_ffn_w_gate': _L0_ffn_in['w_gate'], 'L0_ffn_w_up': _L0_ffn_in['w_up'], 'L0_ffn_w_down': _L0_ffn_in['w_down'], 'L1_attn_W': _L1_attn_in['W'], 'L1_attn_b': _L1_attn_in['b'], 'L1_ffn_U1': _L1_ffn_in['U1'], 'L1_ffn_V1': _L1_ffn_in['V1'], 'L1_ffn_b1': _L1_ffn_in['b1'], 'L1_ffn_U2': _L1_ffn_in['U2'], 'L1_ffn_V2': _L1_ffn_in['V2'], 'L1_ffn_b2': _L1_ffn_in['b2']}
    _x0 = _d['L0_attn_x']
    _d['L0_attn_x'] = jax.random.normal(jax.random.fold_in(jax.random.key(seed), 1), (8, 512, 128), dtype=_x0.dtype)
    del _x0
    return _d

def reference(L0_attn_x, L0_attn_w_qkv, L0_attn_w_out, L0_attn_b_out, L0_ffn_router_w, L0_ffn_w_gate, L0_ffn_w_up, L0_ffn_w_down, L1_attn_W, L1_attn_b, L1_ffn_U1, L1_ffn_V1, L1_ffn_b1, L1_ffn_U2, L1_ffn_V2, L1_ffn_b2):

    def _L0_attn_ref(x, w_qkv, w_out, b_out):
        import jax, jax.numpy as jnp
        import numpy as np
        import math
        B, T, D = (2, 256, 128)
        N_HEADS = 16
        D_HEAD = D // N_HEADS

        def _rope_tables(t, d_head, dtype=jnp.float32):
            theta = 1.0 / 10000.0 ** (jnp.arange(0, d_head, 2, dtype=jnp.float32) / d_head)
            angles = jnp.outer(jnp.arange(t, dtype=jnp.float32), theta)
            angles = jnp.concatenate([angles, angles], axis=-1)
            return (jnp.cos(angles).astype(dtype), jnp.sin(angles).astype(dtype))

        def _rotate_half(x):
            half = x.shape[-1] // 2
            return jnp.concatenate([-x[..., half:], x[..., :half]], axis=-1)

        def _apply_rope(x, cos, sin):
            return x * cos[None, None] + _rotate_half(x) * sin[None, None]
        b, t, d = x.shape
        qkv = x @ w_qkv
        qkv = qkv.reshape(b, t, 3, N_HEADS, D_HEAD)
        q = jnp.transpose(qkv[:, :, 0], (0, 2, 1, 3))
        k = jnp.transpose(qkv[:, :, 1], (0, 2, 1, 3))
        v = jnp.transpose(qkv[:, :, 2], (0, 2, 1, 3))
        cos, sin = _rope_tables(t, D_HEAD, x.dtype)
        q = _apply_rope(q, cos, sin)
        k = _apply_rope(k, cos, sin)
        scores = jnp.einsum('bhqd,bhkd->bhqk', q, k) / math.sqrt(D_HEAD)
        probs = jax.nn.softmax(scores, axis=-1)
        out = jnp.einsum('bhqk,bhkd->bhqd', probs, v)
        out = jnp.transpose(out, (0, 2, 1, 3)).reshape(b, t, d)
        return out @ w_out + b_out

    def _L0_ffn_ref(x, router_w, w_gate, w_up, w_down):
        import jax, jax.numpy as jnp
        import numpy as np
        TOP_K = 2
        B, S, D = x.shape
        E = router_w.shape[0]
        xt = x.reshape(-1, D)
        logits = xt @ router_w.T
        topk_vals, topk_idx = jax.lax.top_k(logits, TOP_K)
        g = jax.nn.sigmoid(topk_vals)
        g = g / (g.sum(axis=-1, keepdims=True) + 1e-10)
        out = jnp.zeros_like(xt)
        for e in range(E):
            ge = jnp.sum(jnp.where(topk_idx == e, g, jnp.zeros_like(g)), axis=-1)
            h = jax.nn.silu(xt @ w_gate[e]) * (xt @ w_up[e])
            out = out + ge[:, None] * (h @ w_down[e])
        return out.reshape(B, S, D)

    def _L1_attn_ref(x, W, b):
        import jax, jax.numpy as jnp
        import numpy as np
        import math
        DK = 128
        qkv = jnp.einsum('btc,cd->btd', x, W) + b
        q, k, v = jnp.split(qkv, 3, axis=-1)
        scale = 1.0 / math.sqrt(DK)
        weights = jnp.einsum('btc,bTc->btT', q, k) * scale
        T = weights.shape[-1]
        mask = jnp.tril(jnp.ones((T, T), dtype=jnp.float32))
        logits = jnp.where(mask == 0, jnp.float32(-9000000000000000.0), weights)
        attention = jax.nn.softmax(logits, axis=-1)
        values = jnp.einsum('btT,bTc->btc', attention, v)
        return values

    def _L1_ffn_ref(x, U1, V1, b1, U2, V2, b2):
        import jax, jax.numpy as jnp
        import numpy as np
        D_MODEL, D_FF, RANK = (128, 512, 32)
        B, S = (4, 512)
        P = jnp.einsum('bsd,dr->bsr', x, U1)
        H = jax.nn.gelu(jnp.einsum('bsr,rf->bsf', P, V1) + b1)
        Q = jnp.einsum('bsf,fr->bsr', H, U2)
        return jnp.einsum('bsr,rd->bsd', Q, V2) + b2
    x = L0_attn_x
    x = x + 0.5 * _L0_ffn_ref(_layernorm(x, axis=-1), L0_ffn_router_w, L0_ffn_w_gate, L0_ffn_w_up, L0_ffn_w_down)
    x = x + _L0_attn_ref(_layernorm(x, axis=-1), L0_attn_w_qkv, L0_attn_w_out, L0_attn_b_out)
    x = x + 0.5 * _L0_ffn_ref(_layernorm(x, axis=-1), L0_ffn_router_w, L0_ffn_w_gate, L0_ffn_w_up, L0_ffn_w_down)
    x = x + 0.5 * _L1_ffn_ref(_layernorm(x, axis=-1), L1_ffn_U1, L1_ffn_V1, L1_ffn_b1, L1_ffn_U2, L1_ffn_V2, L1_ffn_b2)
    x = x + _L1_attn_ref(_layernorm(x, axis=-1), L1_attn_W, L1_attn_b)
    x = x + 0.5 * _L1_ffn_ref(_layernorm(x, axis=-1), L1_ffn_U1, L1_ffn_V1, L1_ffn_b1, L1_ffn_U2, L1_ffn_V2, L1_ffn_b2)
    return x

_drawn_inputs = setup_inputs


def setup_inputs(seed=0):
    import zlib

    import numpy as np

    out = dict(_drawn_inputs(seed))
    spreads = {'L1_attn_b': (0.0, 0.1), 'L1_ffn_b1': (0.0, 0.8), 'L1_ffn_b2': (0.0, 0.1)}
    factors = {'L0_attn_b_out': 2.739,
     'L1_ffn_U1': 8.0,
     'L1_ffn_V1': 8.0,
     'L1_ffn_U2': 8.0,
     'L1_ffn_V2': 8.0}
    for name, (base, spread) in spreads.items():
        noise = np.random.default_rng([zlib.crc32(name.encode()), seed]).standard_normal(out[name].shape)
        drawn = base * np.exp(spread * noise) if base else spread * noise
        out[name] = jnp.asarray(drawn.astype(out[name].dtype))
    for name, factor in factors.items():
        out[name] = (out[name] * factor).astype(out[name].dtype)
    return out
```

```python
from contextlib import ExitStack

import concourse.bass as bass
from concourse import mybir

F32 = mybir.dt.float32
F32R = mybir.dt.float32r
I32 = mybir.dt.int32
U32 = mybir.dt.uint32
ALU = mybir.AluOpType
ACT = mybir.ActivationFunctionType
AX_X = mybir.AxisListType.X

P = 128
B, T, D = 8, 512, 128
NT = T // P
EPS = 1e-5


class Norm:

    def __init__(self, nc, ctx, name, src, const, xt_ps):
        self.nc, self.src, self.const, self.xt_ps = nc, src, const, xt_ps
        sb = lambda n, s, d=F32: ctx.enter_context(nc.sbuf_tensor(f"{name}_{n}", s, d))
        sem = lambda n: ctx.enter_context(nc.semaphore(f"{name}_{n}"))
        self.x = [sb(f"x{k}", [P, NT, D]) for k in range(2)]
        self.xn = [sb(f"xn{k}", [P, NT, D]) for k in range(2)]
        self.stats = [sb(f"stats{k}", [P, NT, 6]) for k in range(2)]
        self.mv = [sb(f"mv{k}", [P, NT, 2]) for k in range(2)]
        self.var = [sb(f"var{k}", [P, NT]) for k in range(2)]
        self.rstd = [sb(f"rstd{k}", [P, NT]) for k in range(2)]
        self.x_loaded = [sem(f"x_loaded{k}") for k in range(2)]
        self.stats_done = sem("stats_done")
        self.aggregating = sem("aggregating")
        self.var_done = sem("var_done")
        self.eps_added = sem("eps_added")
        self.rstd_done = sem("rstd_done")
        self.xn_done = [sem(f"xn_done{k}") for k in range(2)]
        self.xt_done = [sem(f"xt_done{k}") for k in range(2)]

    def load(self, sp, at, x_free):
        u, pair, par = at.u, at.pair, at.par
        sp.wait_ge(x_free[par], pair)
        src = self.src.rearrange("b (i p) d -> b p i d", p=P)
        sp.dma_start(self.x[par][:], src[u]).then_inc(self.x_loaded[par], 16)

    def statistics(self, dve, at):
        nc, u, pair, par = self.nc, at.u, at.pair, at.par
        dve.wait_ge(self.x_loaded[par], 16 * (pair + 1))
        for i in range(NT):
            last = nc.vector.bn_stats(self.stats[par][:, i, :], self.x[par][:, i, :])
        last.then_inc(self.stats_done, 1)
        dve.wait_ge(self.stats_done, u + 1)
        dve.sem_inc(self.aggregating, 1)
        for i in range(NT):
            last = nc.vector.bn_aggr(self.mv[par][:, i, :], self.stats[par][:, i, :])
        last.then_inc(self.var_done, 1)

    def root(self, pool, at):
        nc, u, pair, par = self.nc, at.u, at.pair, at.par
        pool.wait_ge(self.var_done, u + 1)
        nc.gpsimd.tensor_tensor(self.var[par][:], self.mv[par][:, :, 1], self.const["eps"][:, 0:NT],
                                ALU.add).then_inc(self.eps_added, 1)
        pool.wait_ge(self.eps_added, u + 1)
        nc.gpsimd.tensor_tensor(self.rstd[par][:], self.var[par][:], self.const["minus_half"][:, 0:NT],
                                ALU.pow).then_inc(self.rstd_done, 1)

    def normalise(self, dve, at):
        nc, u, pair, par = self.nc, at.u, at.pair, at.par
        dve.wait_ge(self.rstd_done, u + 1)
        dve.wait_ge(self.xt_done[par], pair)
        for i in range(NT):
            last = nc.vector.tensor_scalar(self.xn[par][:, i, :], self.x[par][:, i, :],
                                           self.mv[par][:, i, 0:1], self.rstd[par][:, i:i + 1],
                                           ALU.subtract, ALU.mult)
        last.then_inc(self.xn_done[par], 1)

    def transpose(self, pe, at):
        nc, u, pair, par = self.nc, at.u, at.pair, at.par
        pe.wait_ge(self.xn_done[par], pair + 1)
        for i in range(NT):
            last = nc.tensor.transpose(self.xt_ps[:, i * P:(i + 1) * P], self.xn[par][:, i, :],
                                       self.const["ident"][:])
        last.then_inc(self.xt_done[par], 1)


class Unit:

    def __init__(self, pair, par, n, ways=2):
        self.pair, self.par, self.n, self.ways, self.u = pair, par, n, ways, pair * ways + par

    def after(self, k):
        pair, par = self.pair + (self.par + k) // self.ways, (self.par + k) % self.ways
        if isinstance(pair, int) and not 0 <= pair < self.n // self.ways:
            return None
        return Unit(pair, par, self.n, self.ways)


def skewed(engine, iteration, lead, lag=0, n=B, ways=2):
    first, last = max((lag + ways - 1) // ways, 1), (n - lead) // ways
    for t in range(-lead, ways * first):
        iteration(Unit(t // ways, t % ways, n, ways))
    with engine.Fori(first, last) as pair:
        for k in range(ways):
            iteration(Unit(pair, k, n, ways))
    for t in range(ways * last, n + lag):
        iteration(Unit(t // ways, t % ways, n, ways))



def clear_semaphores(nc):
    given_back = sorted(nc.released_uncleared_semaphores)
    with nc.Block() as block:
        @block.gpsimd
        def _(pool):
            first = given_back[0]
            for number, following in zip(given_back, given_back[1:] + [None]):
                if following != number + 1:
                    pool.sem_clear(range(first, number + 1))
                    first = following


def make_constants(nc, ctx):
    sb = lambda n, s, d=F32: ctx.enter_context(nc.sbuf_tensor(n, s, d))
    const = dict(eps=sb("eps", [P, 8]), minus_half=sb("minus_half", [P, 8]), ident=sb("ident", [P, P]))
    zeroed = ctx.enter_context(nc.semaphore("ident_zeroed"))
    with nc.Block() as block:
        @block.gpsimd
        def _(pool):
            nc.gpsimd.memset(const["eps"][:], EPS)
            nc.gpsimd.memset(const["minus_half"][:], -0.5)
            nc.gpsimd.memset(const["ident"][:], 0.0).then_inc(zeroed, 1)
            pool.wait_ge(zeroed, 1)
            nc.gpsimd.affine_select(out=const["ident"][:], in_=const["ident"][:], compare_op=ALU.not_equal,
                                    fill=1.0, base=0, pattern=[[-1, P]], channel_multiplier=1)
    return const


R = 32
FF = 512
FC = FF // P


def load_ffn_weights(nc, ctx, U1, V1, b1, U2, V2, b2):
    sb = lambda n, s, d=F32: ctx.enter_context(nc.sbuf_tensor(f"ffn_{n}", s, d))
    w = dict(u1=sb("u1", [P, 4, R]), v1=sb("v1", [P, FF]), v1_hi=sb("v1_hi", [P, FF], F32R),
             v1_stack=sb("v1_stack", [P, FF], F32R), b1=sb("b1", [P, FC]), u2=sb("u2", [P, FC, R]),
             v2=sb("v2", [P, D]), v2_half=sb("v2_half", [P, D]), b2=sb("b2", [P, D]),
             b2_half=sb("b2_half", [P, D]))
    loaded = ctx.enter_context(nc.semaphore("ffn_weights_loaded"))
    split = ctx.enter_context(nc.semaphore("ffn_v1_split"))
    with nc.Block() as block:
        @block.sync
        def _(sp):
            for g in range(4):
                sp.dma_start(w["u1"][:, g, :], U1).then_inc(loaded, 16)
                sp.dma_start(w["v1"][g * R:(g + 1) * R, :], V1).then_inc(loaded, 16)
                sp.dma_start(w["v2"][g * R:(g + 1) * R, :], V2).then_inc(loaded, 16)
            sp.dma_start(w["b1"][:], b1.rearrange("(c p) -> p c", p=P),
                         allow_slow_non_contiguous=True).then_inc(loaded, 16)
            sp.dma_start(w["u2"][:], U2.rearrange("(c p) r -> p c r", p=P)).then_inc(loaded, 16)
            sp.dma_start(w["b2"][:], b2.partition_broadcast(P)).then_inc(loaded, 16)

        @block.vector
        def _(dve):
            dve.wait_ge(loaded, 15 * 16)
            nc.vector.tensor_scalar_mul(w["v2_half"][:], w["v2"][:], 0.5)
            nc.vector.tensor_scalar_mul(w["b2_half"][:], w["b2"][:], 0.5)
            nc.vector.tensor_copy(w["v1_hi"][:], w["v1"][:]).then_inc(split, 1)
            dve.wait_ge(split, 1)
            for g in (0, 2):
                rows = slice(g * R, (g + 1) * R)
                nc.vector.tensor_copy(w["v1_stack"][rows, :], w["v1"][rows, :])
            for g in (1, 3):
                rows = slice(g * R, (g + 1) * R)
                nc.vector.tensor_tensor(w["v1_stack"][rows, :], w["v1"][rows, :],
                                        w["v1_hi"][rows, :].bitcast(F32), ALU.subtract)
    return w


def ffn_stage(nc, name, src, dst, const, w):
    with ExitStack() as ctx:
        sb = lambda n, s, d=F32: ctx.enter_context(nc.sbuf_tensor(f"{name}_{n}", s, d))
        ps = lambda n, s: ctx.enter_context(nc.psum_tensor(f"{name}_{n}", s, F32))
        sem = lambda n: ctx.enter_context(nc.semaphore(f"{name}_{n}"))
        xt_ps = ps("xt_ps", [P, T])
        norm = Norm(nc, ctx, name, src, const, xt_ps)
        xt = [sb(f"xt{k}", [P, T]) for k in range(2)]
        xb = [sb(f"xb{k}", [P, NT, D]) for k in range(2)]
        rank = [sb(f"rank{k}", [P, T], F32R) for k in range(2)]
        hid = [sb(f"hid{c}", [P, T]) for c in range(FC)]
        low = [sb(f"low{k}", [P, T]) for k in range(2)]
        y = [sb(f"y{k}", [P, NT, D]) for k in range(2)]
        rank_ps = ps("rank_ps", [P, T])
        hid_ps = [ps(f"hid_ps{k}", [P, T]) for k in range(3)]
        low_ps = ps("low_ps", [P, T])
        out_ps = [ps(f"out_ps{k}", [P, NT, D]) for k in range(2)]
        xt_copied, rank_done, rank_hi, rank_lo = [sem(n) for n in ("xt_copied", "rank_done", "rank_hi", "rank_lo")]
        hid_done, gelu_done, low_done, low_copied = [sem(n) for n in ("hid_done", "gelu_done", "low_done", "low_copied")]
        out_done = sem("out_done")
        xb_done = [sem(f"xb_done{k}") for k in range(2)]
        y_done = [sem(f"y_done{k}") for k in range(2)]
        y_stored = [sem(f"y_stored{k}") for k in range(2)]

        dst_v = dst.rearrange("b (i p) d -> b p i d", p=P)
        with nc.Block() as block:
            @block.sync
            def _(sp):
                def iteration(t):
                    if at := t.after(3):
                        norm.load(sp, at, xb_done)
                    if at := t.after(0):
                        sp.wait_ge(y_done[at.par], at.pair + 1)
                        sp.dma_start(dst_v[at.u], y[at.par][:]).then_inc(y_stored[at.par], 16)

                skewed(sp, iteration, lead=3)
                for par in range(2):
                    sp.wait_ge(y_stored[par], 16 * (B // 2))

            @block.gpsimd
            def _(pool):
                def iteration(t):
                    if at := t.after(2):
                        norm.root(pool, at)
                        pool.wait_ge(norm.xn_done[at.par], at.pair + 1)
                        pool.wait_ge(y_done[at.par], at.pair)
                        nc.gpsimd.tensor_tensor(xb[at.par][:], norm.x[at.par][:],
                                                w["b2_half"][:].unsqueeze(1).to_broadcast([P, NT, D]),
                                                ALU.add).then_inc(xb_done[at.par], 1)

                skewed(pool, iteration, lead=2)

            @block.tensor
            def _(pe):
                def iteration(t):
                    if at := t.after(0):
                        pe.wait_ge(rank_lo, at.u + 1)
                        for c in range(FC):
                            pe.wait_ge(gelu_done, at.u * FC + max(c - 1, 0))
                            nc.tensor.matmul(hid_ps[c % 2][:], w["v1_stack"][:, c * P:(c + 1) * P],
                                             rank[at.par][:], start=True, stop=True).then_inc(hid_done, 1)
                    if at := t.after(1):
                        pe.wait_ge(xt_copied, at.u + 1)
                        nc.tensor.matmul(rank_ps[:], w["u1"][:].rearrange("p g r -> p (g r)"), xt[at.par][:],
                                         start=True, stop=True).then_inc(rank_done, 1)
                    if at := t.after(0):
                        pe.wait_ge(gelu_done, (at.u + 1) * FC)
                        for c in range(FC):
                            last = nc.tensor.matmul(low_ps[c * R:(c + 1) * R, :], w["u2"][:, c, :], hid[c][:],
                                                    start=True, stop=True)
                        last.then_inc(low_done, 1)
                        pe.wait_ge(low_copied, at.u + 1)
                        pe.wait_ge(y_done[at.par], at.pair)
                        for i in range(NT):
                            last = nc.tensor.matmul(out_ps[at.par][:, i, :], low[at.par][:, i * P:(i + 1) * P],
                                                    w["v2_half"][:], start=True, stop=True)
                        last.then_inc(out_done, 1)
                    if at := t.after(2):
                        norm.transpose(pe, at)

                skewed(pe, iteration, lead=2)

            @block.scalar
            def _(act):
                def iteration(t):
                    def gelu(at, c):
                        act.wait_ge(hid_done, at.u * FC + c + 1)
                        act.wait_ge(low_done, at.u)
                        nc.scalar.activation(hid[c][:], hid_ps[c % 2][:], ACT.Gelu_apprx_tanh,
                                             bias=w["b1"][:, c:c + 1]).then_inc(gelu_done, 1)

                    if at := t.after(0):
                        for c in range(FC):
                            gelu(at, c)
                    if at := t.after(1):
                        act.wait_ge(rank_done, at.u + 1)
                        nc.scalar.copy(rank[at.par][:], rank_ps[:]).then_inc(rank_hi, 1)
                    if at := t.after(0):
                        act.wait_ge(low_done, at.u + 1)
                        nc.scalar.copy(low[at.par][:], low_ps[:]).then_inc(low_copied, 1)
                    if at := t.after(2):
                        act.wait_ge(norm.xt_done[at.par], at.pair + 1)
                        nc.scalar.copy(xt[at.par][:], xt_ps[:]).then_inc(xt_copied, 1)

                skewed(act, iteration, lead=2)

            @block.vector
            def _(dve):
                def iteration(t):
                    if at := t.after(2):
                        norm.statistics(dve, at)
                    if at := t.after(1):
                        dve.wait_ge(rank_hi, at.u + 1)
                        nc.vector.tensor_tensor(rank[at.par][64:P, :], rank_ps[64:P, :],
                                                rank[at.par][64:P, :].bitcast(F32),
                                                ALU.subtract).then_inc(rank_lo, 1)
                    if at := t.after(2):
                        norm.normalise(dve, at)
                    if at := t.after(0):
                        dve.wait_ge(out_done, at.u + 1)
                        dve.wait_ge(xb_done[at.par], at.pair + 1)
                        dve.wait_ge(y_stored[at.par], 16 * at.pair)
                        nc.vector.tensor_tensor(y[at.par][:], out_ps[at.par][:], xb[at.par][:],
                                                ALU.add).then_inc(y_done[at.par], 1)

                skewed(dve, iteration, lead=2)


MASKED = -9000000000000000.0


def load_causal_weights(nc, ctx, W, bias):
    sb = lambda n, s, d=F32: ctx.enter_context(nc.sbuf_tensor(f"causal_{n}", s, d))
    w = dict(w=sb("w", [P, 3 * D]), bias=sb("bias", [P, 3]), bq=sb("bq", [P, 1]), bv=sb("bv", [P, D]),
             mask=sb("mask", [P, P]))
    loaded = ctx.enter_context(nc.semaphore("causal_weights_loaded"))
    zeroed = ctx.enter_context(nc.semaphore("causal_mask_zeroed"))
    with nc.Block() as block:
        @block.sync
        def _(sp):
            sp.dma_start(w["w"][:], W).then_inc(loaded, 16)
            sp.dma_start(w["bias"][:], bias.rearrange("(c p) -> p c", p=P),
                         allow_slow_non_contiguous=True).then_inc(loaded, 16)
            sp.dma_start(w["bv"][:], bias[2 * D:3 * D].partition_broadcast(P)).then_inc(loaded, 16)

        @block.vector
        def _(dve):
            dve.wait_ge(loaded, 3 * 16)
            nc.vector.tensor_scalar_mul(w["bq"][:], w["bias"][:, 0:1], float(D) ** -0.5)

        @block.gpsimd
        def _(pool):
            nc.gpsimd.memset(w["mask"][:], 0.0).then_inc(zeroed, 1)
            pool.wait_ge(zeroed, 1)
            nc.gpsimd.affine_select(out=w["mask"][:], in_=w["mask"][:], compare_op=ALU.is_ge, fill=MASKED,
                                    base=0, pattern=[[-1, P]], channel_multiplier=1)
    return w


def causal_stage(nc, name, src, dst, const, w):
    SCALE = float(D) ** -0.5
    with ExitStack() as ctx:
        sb = lambda n, s, d=F32: ctx.enter_context(nc.sbuf_tensor(f"{name}_{n}", s, d))
        ps = lambda n, s: ctx.enter_context(nc.psum_tensor(f"{name}_{n}", s, F32))
        sem = lambda n: ctx.enter_context(nc.semaphore(f"{name}_{n}"))
        xt_ps = ps("xt_ps", [P, T])
        norm = Norm(nc, ctx, name, src, const, xt_ps)
        xt = [sb(f"xt{k}", [P, T]) for k in range(2)]
        res = [sb(f"res{k}", [P, NT, D]) for k in range(2)]
        q = [sb(f"q{k}", [P, T]) for k in range(2)]
        k_ = [sb(f"k{k}", [P, T]) for k in range(2)]
        v = [sb(f"v{k}", [P, NT, D]) for k in range(2)]
        neg_max = [sb(f"neg_max{k}", [P, NT]) for k in range(2)]
        row_sum = [sb(f"row_sum{k}", [P, NT]) for k in range(2)]
        inv_sum = [sb(f"inv_sum{k}", [P, NT]) for k in range(2)]
        prob = [sb(f"prob{i}", [P, T]) for i in range(NT)]
        prob_t = [sb(f"prob_t{k}", [P, NT, P]) for k in range(2)]
        y = [sb(f"y{k}", [P, NT, D]) for k in range(2)]
        qv_ps, k_ps = ps("qv_ps", [P, T]), ps("k_ps", [P, T])
        score_ps = [ps(f"score_ps{k}", [P, T]) for k in range(2)]
        prob_t_ps = [ps(f"prob_t_ps{k}", [P, NT, P]) for k in range(2)]
        out_ps = ps("out_ps", [P, NT, D])
        (xt_copied, q_done, k_done, v_done, q_copied, k_copied, v_copied, res_done, score_done, mask_added,
         max_done, exp_done, prob_t_done, prob_t_copied, value_done, inv_done) = [
            sem(n) for n in ("xt_copied", "q_done", "k_done", "v_done", "q_copied", "k_copied", "v_copied",
                             "res_done", "score_done", "mask_added", "max_done", "exp_done", "prob_t_done",
                             "prob_t_copied", "value_done", "inv_done")]
        copying = sem("copying")
        res_copied = [sem(f"res_copied{k}") for k in range(2)]
        y_done = [sem(f"y_done{k}") for k in range(2)]
        y_stored = [sem(f"y_stored{k}") for k in range(2)]
        dst_v = dst.rearrange("b (i p) d -> b p i d", p=P)

        with nc.Block() as block:
            @block.sync
            def _(sp):
                def iteration(t):
                    if at := t.after(3):
                        norm.load(sp, at, res_copied)
                    if at := t.after(0):
                        sp.wait_ge(y_done[at.par], at.pair + 1)
                        sp.dma_start(dst_v[at.u], y[at.par][:]).then_inc(y_stored[at.par], 16)

                skewed(sp, iteration, lead=3)
                for par in range(2):
                    sp.wait_ge(y_stored[par], 16 * (B // 2))

            @block.gpsimd
            def _(pool):
                def iteration(t):
                    if at := t.after(2):
                        norm.root(pool, at)
                        pool.wait_ge(norm.xn_done[at.par], at.pair + 1)
                        pool.wait_ge(y_done[at.par], at.pair)
                        pool.sem_inc(copying, 1)
                        nc.gpsimd.tensor_copy(res[at.par][:], norm.x[at.par][:]).then_inc(res_copied[at.par], 1)

                skewed(pool, iteration, lead=2)

            @block.tensor
            def _(pe):
                def score(at, i):
                    pe.wait_ge(exp_done, at.u * NT + max(i - 1, 0))
                    n = (i + 1) * P
                    nc.tensor.matmul(score_ps[i % 2][:, 0:n], q[at.par][:, i * P:n], k_[at.par][:, 0:n],
                                     start=True, stop=True).then_inc(score_done, 1)

                def prob_transpose(at, i):
                    pe.wait_ge(exp_done, at.u * NT + i + 1)
                    pe.wait_ge(prob_t_copied, at.u * NT + max(i - 1, 0))
                    for j in range(i + 1):
                        last = nc.tensor.transpose(prob_t_ps[i % 2][:, j, :], prob[i][:, j * P:(j + 1) * P],
                                                   const["ident"][:])
                    last.then_inc(prob_t_done, 1)

                def values(at, i):
                    pe.wait_ge(prob_t_copied, at.u * NT + i + 1)
                    for j in range(i + 1):
                        last = nc.tensor.matmul(out_ps[:, i, :], prob_t[i % 2][:, j, :], v[at.par][:, j, :],
                                                start=(j == 0), stop=(j == i))
                    last.then_inc(value_done, 1)

                def iteration(t):
                    now, nxt = t.after(0), t.after(1)
                    if now:
                        pe.wait_ge(q_copied, now.u + 1)
                        pe.wait_ge(k_copied, now.u + 1)
                        score(now, 0)
                        score(now, 1)
                    if nxt:
                        pe.wait_ge(xt_copied, nxt.u + 1)
                        pe.wait_ge(v_copied, nxt.u)
                        nc.tensor.matmul(qv_ps[:], w["w"][:, 0:D], xt[nxt.par][:], start=True,
                                         stop=True).then_inc(q_done, 1)
                    if now:
                        score(now, 2)
                    if nxt:
                        pe.wait_ge(k_copied, nxt.u)
                        nc.tensor.matmul(k_ps[:], w["w"][:, D:2 * D], xt[nxt.par][:], start=True,
                                         stop=True).then_inc(k_done, 1)
                    if now:
                        score(now, 3)
                    if nxt:
                        pe.wait_ge(q_copied, nxt.u + 1)
                        for i in range(NT):
                            last = nc.tensor.matmul(qv_ps[:, i * P:(i + 1) * P], xt[nxt.par][:, i * P:(i + 1) * P],
                                                    w["w"][:, 2 * D:3 * D], start=True, stop=True)
                        last.then_inc(v_done, 1)
                    if now:
                        prob_transpose(now, 0)
                        prob_transpose(now, 1)
                        pe.wait_ge(v_copied, now.u + 1)
                        pe.wait_ge(y_done[1 - now.par], now.pair + now.par)
                        values(now, 0)
                        prob_transpose(now, 2)
                        values(now, 1)
                        prob_transpose(now, 3)
                        values(now, 2)
                        values(now, 3)
                    if ahead := t.after(2):
                        norm.transpose(pe, ahead)

                skewed(pe, iteration, lead=2)

            @block.scalar
            def _(act):
                def exponential(at, i):
                    n = (i + 1) * P
                    act.wait_ge(max_done, at.u * NT + i + 1)
                    act.wait_ge(prob_t_done, at.u * NT)
                    nc.scalar.activation(prob[i][:, 0:n], score_ps[i % 2][:, 0:n], ACT.Exp,
                                         bias=neg_max[at.par][:, i:i + 1],
                                         accum_out=row_sum[at.par][:, i:i + 1]).then_inc(exp_done, 1)

                def iteration(t):
                    now, nxt = t.after(0), t.after(1)
                    if now:
                        exponential(now, 0)
                        exponential(now, 1)
                    if nxt:
                        act.wait_ge(q_done, nxt.u + 1)
                        nc.scalar.activation(q[nxt.par][:], qv_ps[:], ACT.Identity, bias=w["bq"][:, 0:1],
                                             scale=SCALE).then_inc(q_copied, 1)
                    if now:
                        exponential(now, 2)
                        exponential(now, 3)
                        for i in (0, 1, 2, 3):
                            act.wait_ge(prob_t_done, now.u * NT + i + 1)
                            act.wait_ge(value_done, now.u * NT + max(i - 1, 0))
                            nc.scalar.copy(prob_t[i % 2][:, 0:i + 1, :],
                                           prob_t_ps[i % 2][:, 0:i + 1, :]).then_inc(prob_t_copied, 1)
                    if ahead := t.after(2):
                        act.wait_ge(norm.xt_done[ahead.par], ahead.pair + 1)
                        nc.scalar.copy(xt[ahead.par][:], xt_ps[:]).then_inc(xt_copied, 1)

                skewed(act, iteration, lead=2)

            @block.vector
            def _(dve):
                def row_max(at, i):
                    n = (i + 1) * P
                    dve.wait_ge(score_done, at.u * NT + i + 1)
                    nc.vector.tensor_tensor(score_ps[i % 2][:, i * P:n], score_ps[i % 2][:, i * P:n],
                                            w["mask"][:], ALU.add).then_inc(mask_added, 1)
                    dve.wait_ge(mask_added, at.u * NT + i + 1)
                    nc.vector.tensor_reduce(neg_max[at.par][:, i:i + 1], score_ps[i % 2][:, 0:n], AX_X, ALU.max,
                                            negate=True).then_inc(max_done, 1)

                def iteration(t):
                    now, nxt, ahead = t.after(0), t.after(1), t.after(2)
                    if now:
                        row_max(now, 0)
                        row_max(now, 1)
                    if ahead:
                        norm.statistics(dve, ahead)
                    if now:
                        row_max(now, 2)
                    if nxt:
                        dve.wait_ge(k_done, nxt.u + 1)
                        nc.vector.tensor_scalar(k_[nxt.par][:], k_ps[:], w["bias"][:, 1:2], None,
                                                ALU.add).then_inc(k_copied, 1)
                    if now:
                        row_max(now, 3)
                    if nxt:
                        dve.wait_ge(v_done, nxt.u + 1)
                        nc.vector.tensor_tensor(v[nxt.par][:], qv_ps[:].rearrange("p (i d) -> p i d", i=NT),
                                                w["bv"][:].unsqueeze(1).to_broadcast([P, NT, D]),
                                                ALU.add).then_inc(v_copied, 1)
                    if ahead:
                        norm.normalise(dve, ahead)
                    if now:
                        dve.wait_ge(exp_done, (now.u + 1) * NT)
                        nc.vector.reciprocal(inv_sum[now.par][:], row_sum[now.par][:]).then_inc(inv_done, 1)
                        dve.wait_ge(inv_done, now.u + 1)
                        dve.wait_ge(value_done, (now.u + 1) * NT)
                        dve.wait_ge(res_copied[now.par], now.pair + 1)
                        dve.wait_ge(y_stored[now.par], 16 * now.pair)
                        for i in range(NT):
                            last = nc.vector.scalar_tensor_tensor(
                                y[now.par][:, i, :], out_ps[:, i, :], inv_sum[now.par][:, i:i + 1],
                                res[now.par][:, i, :], ALU.mult, ALU.add)
                        last.then_inc(y_done[now.par], 1)

                skewed(dve, iteration, lead=2)


H = 16
DH = D // H
SLOTS = H // 2
PARTS = 4
MAX_ROW = PARTS * DH
KROWS = 64
HALF = SLOTS // 2


def load_heads_weights(nc, ctx, wqk, wv, wo, bo, cos, sin):
    sb = lambda n, s, d=F32: ctx.enter_context(nc.sbuf_tensor(f"heads_{n}", s, d))
    w = dict(qk=sb("qk", [P, 2, D]), rot=sb("rot", [P, 2, D]), v=sb("v", [P, D]), o=sb("o", [P, D]),
             bo=sb("bo", [P, D]), cos=sb("cos", [P, T]), sin=sb("sin", [P, T]))
    loaded = ctx.enter_context(nc.semaphore("heads_weights_loaded"))
    with nc.Block() as block:
        @block.sync
        def _(sp):
            sp.dma_start(w["qk"][:], wqk).then_inc(loaded, 16)
            for n in range(2):
                rot = w["rot"][:, n, :].rearrange("p (a e c) -> p a e c", e=2, c=DH // 2 * SLOTS)
                plain = wqk[:, n, :].rearrange("p (a e c) -> p a e c", e=2, c=DH // 2 * SLOTS)
                for e in range(2):
                    sp.dma_start(rot[:, :, e, :], plain[:, :, 1 - e, :]).then_inc(loaded, 16)
            sp.dma_start(w["v"][:], wv).then_inc(loaded, 16)
            sp.dma_start(w["o"][:], wo).then_inc(loaded, 16)
            sp.dma_start(w["bo"][:], bo.partition_broadcast(P)).then_inc(loaded, 16)
            sp.dma_start(w["cos"][:], cos).then_inc(loaded, 16)
            sp.dma_start(w["sin"][:], sin).then_inc(loaded, 16)
            sp.wait_ge(loaded, 10 * 16)
    return w


def heads_stage(nc, name, src, dst, const, w):
    STEPS = H * NT
    SETS = STEPS // 4
    ITEMS = STEPS // 2
    NORM = (6, 10, 14, 18)
    M_B, BACK, PROJECT, V, XT, Q, M_A, QR, K, KR = 1, 22, 26, 29, 32, 35, 38, 41, 45, 49
    with ExitStack() as ctx:
        sb = lambda n, s, d=F32: ctx.enter_context(nc.sbuf_tensor(f"{name}_{n}", s, d))
        ps = lambda n, s: ctx.enter_context(nc.psum_tensor(f"{name}_{n}", s, F32))
        sem = lambda n: ctx.enter_context(nc.semaphore(f"{name}_{n}"))
        misc_ps = ps("misc_ps", [P, T])
        norm = Norm(nc, ctx, name, src, const, misc_ps)
        xt = sb("xt", [P, T])
        res = [sb(f"res{k}", [P, NT, D]) for k in range(2)]
        by_cos, by_sin, rotated = sb("by_cos", [P, T]), sb("by_sin", [P, T]), sb("rotated", [P, T])
        hi = [sb(f"hi{n}", [P, T], F32R) for n in range(2)]
        lo = [sb(f"lo{n}", [P, T], F32R) for n in range(2)]
        qx = [sb(f"qx{k}", [P, SLOTS, T], F32R) for k in range(2)]
        kx = [sb(f"kx{k}", [P, SLOTS, T], F32R) for k in range(2)]
        vx = [sb(f"vx{k}", [P, NT, H, 32]) for k in range(2)]
        zero_row = sb("zero_row", [1, HALF, T])
        row_max = sb("row_max", [P, 2, 2, HALF, NT])
        neg_max = [sb(f"neg_max{k}", [32, P], F32R) for k in range(2)]
        prob = [sb(f"prob{k}", [P, T]) for k in range(8)]
        ot = [sb(f"ot{g}", [P, T]) for g in range(4)]
        inv_sum = sb("inv_sum", [P, NT, H])
        o = [sb(f"o{i}", [P, H, DH]) for i in range(NT)]
        oT = sb("oT", [P, T])
        y = [sb(f"y{k}", [P, NT, D]) for k in range(2)]
        max_ps = [ps(f"max_ps{k}", [P, 2, T]) for k in range(2)]
        score_ps = [ps(f"score_ps{k}", [P, T]) for k in range(2)]
        value_ps = ps("value_ps", [P, T])
        names = ("xt_copied qk_done cos_done sin_done rope_done hi_done lo_done v_done v_copied "
                 "max_done row_max_done m_turned m_negated score_done exp_done value_done ot_copied "
                 "turned inv_done o_done back_done back_copied project_done set_up")
        (xt_copied, qk_done, cos_done, sin_done, rope_done, hi_done, lo_done, v_done, v_copied,
         max_done, row_max_done, m_turned, m_negated, score_done, exp_done, value_done, ot_copied,
         turned, inv_done, o_done, back_done, back_copied, project_done, set_up) = [sem(n) for n in names.split()]
        set_done = [sem(f"set_done{k}") for k in range(2)]
        res_loaded = [sem(f"res_loaded{k}") for k in range(2)]
        res_done = [sem(f"res_done{k}") for k in range(2)]
        y_done = [sem(f"y_done{k}") for k in range(2)]
        y_stored = [sem(f"y_stored{k}") for k in range(2)]
        expanded = [[sem(f"expanded{k}{half}") for half in range(2)] for k in range(2)]
        m_placed = [[sem(f"m_placed{k}{half}") for half in range(2)] for k in range(2)]
        src_v = src.rearrange("b (i p) d -> b p i d", p=P)
        dst_v = dst.rearrange("b (i p) d -> b p i d", p=P)
        spill_done = [sem(f"spill_done{k}") for k in range(2)]
        spilled = nc.dram_tensor(f"{name}_spilled", [2, 2, 2, 3, DH, SLOTS, T], F32).ap()
        max_spill_done = [sem(f"max_spill_done{half}") for half in range(2)]
        max_spilled = nc.dram_tensor(f"{name}_max_spilled", [2, 2, 2, HALF, NT, P], F32).ap()
        SPILLS, EXPANDS = 5 * 16, 10 * 16

        def rows(buf, head):
            at = 64 * (head % 2)
            return buf[at:at + KROWS, head // 2, :]


        with nc.Block() as block:
            @block.sync
            def _(sp):
                def place_max(at, half):
                    sp.wait_ge(m_negated, at.u * 2 + half + 1)
                    sp.dma_start(max_spilled[at.par, half].rearrange("a s i q -> (a s i) q"),
                                 neg_max[half][:].bitcast(F32)).then_inc(max_spill_done[half], 16)
                    sp.wait_ge(max_spill_done[half], 16 * (at.u + 1))
                    for par in range(2):
                        row = 64 * par + MAX_ROW
                        sp.dma_start(qx[at.par][row:row + 1, half * HALF:(half + 1) * HALF, :].bitcast(F32),
                                     max_spilled[at.par, half, par].rearrange("s i q -> s (i q)").unsqueeze(0)
                                     ).then_inc(m_placed[at.par][half], 16)

                def spill(at):
                    for n in range(2):
                        sp.wait_ge(lo_done, at.u * 2 + n + 1)
                        for half in range(2):
                            sp.wait_ge(expanded[at.par][half], EXPANDS * at.pair)
                        for part, source in enumerate((hi[n], lo[n], hi[n])[:2 + n]):
                            sp.dma_start(spilled[at.par, n, :, part].rearrange("a d s t -> a (d s) t"),
                                         source[:].bitcast(F32)).then_inc(spill_done[at.par], 16)

                def expand(at, half):
                    slots = slice(half * HALF, (half + 1) * HALF)
                    for n, wide in ((0, qx), (1, kx)):
                        for par in range(2):
                            for pair in range(2):
                                to = 64 * par + 2 * DH * pair
                                start = pair if n else 0
                                sp.dma_start(wide[at.par][to:to + 2 * DH, slots, :].bitcast(F32),
                                             spilled[at.par, n, par, start:start + 2, :, slots, :]
                                             .rearrange("l d s t -> (l d) s t")).then_inc(expanded[at.par][half], 16)
                    for par in range(2):
                        row = 64 * par + MAX_ROW
                        sp.dma_start(qx[at.par][row:row + 1, slots, :].bitcast(F32),
                                     zero_row[:]).then_inc(expanded[at.par][half], 16)

                def iteration(t):
                    if at := t.after(3):
                        norm.load(sp, at, norm.xn_done)
                    if at := t.after(0):
                        sp.wait_ge(y_done[at.par], at.pair)
                        sp.dma_start(res[at.par][:], src_v[at.u]).then_inc(res_loaded[at.par], 16)
                    if at := t.after(0):
                        place_max(at, 1)
                    if at := t.after(-1):
                        sp.wait_ge(y_done[at.par], at.pair + 1)
                        sp.dma_start(dst_v[at.u], y[at.par][:]).then_inc(y_stored[at.par], 16)
                    if at := t.after(1):
                        place_max(at, 0)
                    if at := t.after(2):
                        spill(at)
                        sp.wait_ge(spill_done[at.par], SPILLS * (at.pair + 1))
                        if now := t.after(0):
                            sp.wait_ge(score_done, now.u * STEPS + STEPS // 2)
                        expand(at, 0)
                        if now:
                            sp.wait_ge(score_done, (now.u + 1) * STEPS)
                        expand(at, 1)

                sp.wait_ge(set_up, 2)
                skewed(sp, iteration, lead=3, lag=1)
                for par in range(2):
                    sp.wait_ge(y_stored[par], 16 * (B // 2))

            @block.gpsimd
            def _(pool):
                def iteration(t):
                    if at := t.after(0):
                        pool.wait_ge(res_loaded[at.par], 16 * (at.pair + 1))
                        nc.gpsimd.tensor_tensor(res[at.par][:], res[at.par][:],
                                                w["bo"][:].unsqueeze(1).to_broadcast([P, NT, D]),
                                                ALU.add).then_inc(res_done[at.par], 1)
                    if at := t.after(2):
                        norm.root(pool, at)
                        for n in range(2):
                            pool.wait_ge(sin_done, at.u * 2 + n + 1)
                            pool.wait_ge(lo_done, at.u * 2 + n)
                            nc.gpsimd.tensor_tensor(rotated[:], by_cos[:], by_sin[:], ALU.add).then_inc(rope_done, 1)
                            pool.wait_ge(hi_done, at.u * 2 + n + 1)
                            nc.gpsimd.tensor_tensor(lo[n][:], rotated[:], hi[n][:].bitcast(F32),
                                                    ALU.subtract).then_inc(lo_done, 1)

                skewed(pool, iteration, lead=2, lag=1)

            @block.tensor
            def _(pe):
                def values(at, s):
                    g, c = s // NT, s % NT
                    pe.wait_ge(exp_done, at.u * STEPS + 4 * s + 4)
                    if s == 0:
                        pe.wait_ge(v_copied, at.u + 1)
                    if c == 0:
                        pe.wait_ge(ot_copied, at.u * 4 + g)
                    for j in range(4):
                        last = nc.tensor.matmul(value_ps[32 * j:32 * j + 32, :], vx[at.par][:, c, 4 * g + j, :],
                                                prob[4 * (s % 2) + j][:], start=(c == 0), stop=(c == NT - 1))
                    last.then_inc(set_done[s % 2], 1)

                def score(at, k):
                    head, c = 4 * (k // 16) + k % 4, k // 4 % NT
                    pe.wait_ge(exp_done, at.u * STEPS + max(k - 1, 0))
                    if k % (STEPS // 2) == 0:
                        pe.wait_ge(m_placed[at.par][k // (STEPS // 2)], 32 * (at.pair + 1))
                    nc.tensor.matmul(score_ps[k % 2][:], rows(kx[at.par], head)[:, c * P:(c + 1) * P],
                                     rows(qx[at.par], head), start=True, stop=True).then_inc(score_done, 1)

                def score_for_max(at, n):
                    head = n // 2
                    if n % (ITEMS // 2) == 0:
                        pe.wait_ge(expanded[at.par][n // (ITEMS // 2)], EXPANDS * (at.pair + 1))
                    pe.wait_ge(row_max_done, at.u * ITEMS + max(n - 1, 0))
                    for i in range(2):
                        tile = 2 * (n % 2) + i
                        last = nc.tensor.matmul(
                            max_ps[n % 2][:, i, :], rows(qx[at.par], head)[:, tile * P:(tile + 1) * P],
                            rows(kx[at.par], head), start=True, stop=True)
                    last.then_inc(max_done, 1)

                def turn_max(at, half):
                    pe.wait_ge(row_max_done, at.u * ITEMS + (half + 1) * ITEMS // 2)
                    nc.tensor.transpose(misc_ps[0:32, 0:P], row_max[:, half].rearrange("p a s i -> p (a s i)"),
                                        const["ident"][:]).then_inc(m_turned, 1)

                def product(at, weights, done):
                    nc.tensor.matmul(misc_ps[:], weights, xt[:], start=True, stop=True).then_inc(done, 1)

                def iteration(t):
                    prev, now, nxt, ahead = t.after(-1), t.after(0), t.after(1), t.after(2)
                    for k in range(STEPS):
                        if k % 4 == 2:
                            s = k // 4 - 1
                            if s < 0 and prev:
                                values(prev, SETS - 1)
                            if s >= 0 and now:
                                values(now, s)
                        if now:
                            score(now, k)
                        if nxt and k % 2:
                            score_for_max(nxt, k // 2)
                        if now and k == M_B:
                            if nxt:
                                pe.wait_ge(sin_done, (nxt.u + 1) * 2)
                            pe.wait_ge(m_negated, now.u * 2 + 1)
                            turn_max(now, 1)
                        if prev and k in NORM:
                            i = NORM.index(k)
                            pe.wait_ge(ot_copied, (prev.u + 1) * 4)
                            if now:
                                pe.wait_ge(m_negated, now.u * 2 + 2)
                            else:
                                pe.wait_ge(y_done[1 - prev.par], prev.pair + prev.par)
                            pe.wait_ge(o_done, prev.u * NT + i)
                            for g in range(4):
                                last = nc.tensor.transpose(misc_ps[:, g * P:(g + 1) * P], ot[g][:, i * P:(i + 1) * P],
                                                           const["ident"][:])
                            last.then_inc(turned, 1)
                        if prev and k == BACK:
                            pe.wait_ge(o_done, (prev.u + 1) * NT)
                            for i in range(NT):
                                last = nc.tensor.transpose(misc_ps[:, i * P:(i + 1) * P],
                                                           o[i][:].rearrange("p h d -> p (h d)"), const["ident"][:])
                            last.then_inc(back_done, 1)
                        if prev and k == PROJECT:
                            pe.wait_ge(back_copied, prev.u + 1)
                            for i in range(NT):
                                last = nc.tensor.matmul(misc_ps[:, i * P:(i + 1) * P], oT[:, i * P:(i + 1) * P],
                                                        w["o"][:], start=True, stop=True)
                            last.then_inc(project_done, 1)
                        if nxt and k == V:
                            if prev:
                                pe.wait_ge(y_done[prev.par], prev.pair + 1)
                            if now:
                                pe.wait_ge(m_negated, now.u * 2 + 2)
                            pe.wait_ge(sin_done, (nxt.u + 1) * 2)
                            for i in range(NT):
                                last = nc.tensor.matmul(misc_ps[:, i * P:(i + 1) * P], xt[:, i * P:(i + 1) * P],
                                                        w["v"][:], start=True, stop=True)
                            last.then_inc(v_done, 1)
                        if ahead and k == XT:
                            if nxt:
                                pe.wait_ge(v_copied, nxt.u + 1)
                            norm.transpose(pe, ahead)
                        if ahead and k == Q:
                            pe.wait_ge(xt_copied, ahead.u + 1)
                            product(ahead, w["qk"][:, 0, :], qk_done)
                        if nxt and k == M_A:
                            if ahead:
                                pe.wait_ge(cos_done, ahead.u * 2 + 1)
                            else:
                                pe.wait_ge(v_copied, nxt.u + 1)
                            turn_max(nxt, 0)
                        if ahead and k == QR:
                            pe.wait_ge(cos_done, ahead.u * 2 + 1)
                            if nxt:
                                pe.wait_ge(m_negated, nxt.u * 2 + 1)
                            product(ahead, w["rot"][:, 0, :], qk_done)
                        if ahead and k == K:
                            pe.wait_ge(sin_done, ahead.u * 2 + 1)
                            product(ahead, w["qk"][:, 1, :], qk_done)
                        if ahead and k == KR:
                            pe.wait_ge(cos_done, ahead.u * 2 + 2)
                            product(ahead, w["rot"][:, 1, :], qk_done)

                pe.wait_ge(set_up, 2)
                skewed(pe, iteration, lead=2, lag=1)

            @block.scalar
            def _(act):
                def iteration(t):
                    prev, now, nxt, ahead = t.after(-1), t.after(0), t.after(1), t.after(2)
                    for k in range(STEPS):
                        if now:
                            s = k // 4
                            act.wait_ge(score_done, now.u * STEPS + k + 1)
                            if k % 4 == 0:
                                act.wait_ge(set_done[s % 2], now.u * (SETS // 2) + s // 2)
                            nc.scalar.activation(prob[k % 8][:], score_ps[k % 2][:], ACT.Exp,
                                                 scale=float(DH) ** -0.5).then_inc(exp_done, 1)
                        if k % 16 == 3:
                            g = k // 16 - 1
                            at = now if g >= 0 else prev
                            if at:
                                g %= 4
                                act.wait_ge(set_done[1], at.u * (SETS // 2) + 2 * g + 2)
                                act.wait_ge(turned, at.u * NT)
                                nc.scalar.copy(ot[g][:], value_ps[:]).then_inc(ot_copied, 1)
                        if prev and k == BACK + 1:
                            act.wait_ge(back_done, prev.u + 1)
                            nc.scalar.copy(oT[:], misc_ps[:]).then_inc(back_copied, 1)
                        if ahead and k == XT + 1:
                            act.wait_ge(norm.xt_done[ahead.par], ahead.pair + 1)
                            if nxt:
                                act.wait_ge(v_done, nxt.u + 1)
                            nc.scalar.copy(xt[:], misc_ps[:]).then_inc(xt_copied, 1)
                        for n, at_step in ((0, QR + 5), (1, KR + 5)):
                            if ahead and k == at_step:
                                act.wait_ge(rope_done, ahead.u * 2 + n + 1)
                                act.wait_ge(spill_done[1 - ahead.par], SPILLS * (ahead.pair + ahead.par))
                                nc.scalar.copy(hi[n][:], rotated[:]).then_inc(hi_done, 1)

                skewed(act, iteration, lead=2, lag=1)

            @block.vector
            def _(dve):
                def negate(at, half):
                    dve.wait_ge(m_turned, at.u * 2 + half + 1)
                    dve.wait_ge(max_spill_done[half], 16 * at.u)
                    nc.vector.tensor_scalar_mul(neg_max[half][:], misc_ps[0:32, 0:P], -1.0).then_inc(m_negated, 1)

                def iteration(t):
                    prev, now, nxt, ahead = t.after(-1), t.after(0), t.after(1), t.after(2)
                    for k in range(STEPS):
                        if nxt and k % 2:
                            n = k // 2
                            half, head, tile = n // (ITEMS // 2), n // 2, 2 * (n % 2)
                            dve.wait_ge(max_done, nxt.u * ITEMS + n + 1)
                            if n % (ITEMS // 2) == 0:
                                dve.wait_ge(m_turned, nxt.u * 2 - 1 + half if half else nxt.u * 2)
                            nc.vector.tensor_reduce(row_max[:, half, head % 2, head // 2 % HALF, tile:tile + 2],
                                                    max_ps[n % 2][:], AX_X, ALU.max).then_inc(row_max_done, 1)
                        if now and k == M_B + 1:
                            negate(now, 1)
                        if prev and k - 1 in NORM:
                            i = NORM.index(k - 1)
                            dve.wait_ge(turned, prev.u * NT + i + 1)
                            wide = misc_ps[:].rearrange("p (h c) -> p h c", c=32)
                            nc.vector.reciprocal(inv_sum[:, i, :], wide[:, :, DH]).then_inc(inv_done, 1)
                            dve.wait_ge(inv_done, prev.u * NT + i + 1)
                            dve.wait_ge(back_done, prev.u)
                            nc.vector.tensor_tensor(o[i][:], wide[:, :, 0:DH],
                                                    inv_sum[:, i, :].unsqueeze(2).to_broadcast([P, H, DH]),
                                                    ALU.mult).then_inc(o_done, 1)
                        if ahead and k == 21:
                            norm.statistics(dve, ahead)
                        if ahead and k == 27:
                            norm.normalise(dve, ahead)
                        if prev and k == PROJECT + 1:
                            dve.wait_ge(project_done, prev.u + 1)
                            dve.wait_ge(y_stored[prev.par], 16 * prev.pair)
                            dve.wait_ge(res_done[prev.par], prev.pair + 1)
                            nc.vector.tensor_tensor(y[prev.par][:], misc_ps[:].rearrange("p (i d) -> p i d", i=NT),
                                                    res[prev.par][:], ALU.add).then_inc(y_done[prev.par], 1)
                        for n, at_step in ((0, Q + 1), (1, K + 1)):
                            if ahead and k == at_step:
                                dve.wait_ge(qk_done, ahead.u * 4 + 2 * n + 1)
                                dve.wait_ge(rope_done, ahead.u * 2 + n)
                                nc.vector.tensor_tensor(by_cos[:], misc_ps[:], w["cos"][:], ALU.mult).then_inc(cos_done, 1)
                        for n, at_step in ((0, QR + 1), (1, KR + 1)):
                            if ahead and k == at_step:
                                dve.wait_ge(qk_done, ahead.u * 4 + 2 * n + 2)
                                nc.vector.tensor_tensor(by_sin[:], misc_ps[:], w["sin"][:], ALU.mult).then_inc(sin_done, 1)
                        if nxt and k == M_A + 1:
                            negate(nxt, 0)
                        if nxt and k == V + 1:
                            dve.wait_ge(v_done, nxt.u + 1)
                            if prev:
                                dve.wait_ge(set_done[1], (prev.u + 1) * (SETS // 2))
                            nc.vector.tensor_copy(vx[nxt.par][:, :, :, 0:DH],
                                                  misc_ps[:].rearrange("p (i h d) -> p i h d", i=NT, h=H)
                                                  ).then_inc(v_copied, 1)

                nc.vector.memset(zero_row[:], 0.0)
                for k in range(2):
                    nc.vector.memset(vx[k][:, :, :, DH:32], 0.0)
                    for par in range(2):
                        row = 64 * par + MAX_ROW
                        nc.vector.memset(qx[k][row:row + 32, :, :].bitcast(F32), 0.0)
                        last = nc.vector.memset(kx[k][row:row + 32, :, :].bitcast(F32), 0.0)
                last.then_inc(set_up, 1)
                dve.wait_ge(set_up, 1)
                for k in range(2):
                    for par in range(2):
                        row = 64 * par + MAX_ROW
                        nc.vector.memset(kx[k][row:row + 1, :, :].bitcast(F32), 1.0)
                    last = nc.vector.memset(vx[k][:, :, :, DH:DH + 1], 1.0)
                last.then_inc(set_up, 1)
                skewed(dve, iteration, lead=2, lag=1)


E = 8
HID = 256
BF16 = mybir.dt.bfloat16
REGION = B * T + P
TILES = 2 * B * T // P + E
LOWEST = -3.0e38
X_ROWS = E * REGION
Y_ROWS = TILES * P


def load_moe_weights(nc, ctx, name, router, w_gate, w_up, w_down):
    sb = lambda n, s, d=F32: ctx.enter_context(nc.sbuf_tensor(f"{name}_{n}", s, d))
    w = dict(router=sb("router", [P, E]), hi=sb("hi", [P, E, 2 * HID], F32R), lo=sb("lo", [P, E, 2 * HID], F32R),
             down=sb("down", [P, 2 * E, D]), below=sb("below", [P, P], BF16), ones=sb("ones", [P, P], BF16),
             prefer=sb("prefer", [P, NT, E]), base=sb("base", [P, E]), row=sb("row", [P, E]),
             tile=sb("tile", [P, TILES]), zero=sb("zero", [P, D]), steps=sb("steps", [P, E]))
    loaded = ctx.enter_context(nc.semaphore(f"{name}_weights_loaded"))
    split = ctx.enter_context(nc.semaphore(f"{name}_weights_split"))
    filled = ctx.enter_context(nc.semaphore(f"{name}_constants_filled"))
    with nc.sbuf_tensor(f"{name}_plain", [P, E, 2 * HID], F32) as plain, nc.Block() as block:
        @block.sync
        def _(sp):
            sp.dma_start(w["router"][:], router).then_inc(loaded, 16)
            sp.dma_start(plain[:, :, 0:HID], w_gate.rearrange("e d h -> d e h")).then_inc(loaded, 16)
            sp.dma_start(plain[:, :, HID:], w_up.rearrange("e d h -> d e h")).then_inc(loaded, 16)
            sp.dma_start(w["down"][:], w_down.rearrange("e (c p) d -> p (e c) d", p=P)).then_inc(loaded, 16)

        @block.vector
        def _(dve):
            dve.wait_ge(loaded, 4 * 16)
            nc.vector.tensor_copy(w["hi"][:], plain[:]).then_inc(split, 1)
            dve.wait_ge(split, 1)
            nc.vector.tensor_tensor(w["lo"][:], plain[:], w["hi"][:].bitcast(F32), ALU.subtract)

        @block.gpsimd
        def _(pool):
            nc.gpsimd.memset(w["zero"][:], 0.0)
            nc.gpsimd.memset(w["ones"][:], 1.0).then_inc(filled, 1)
            pool.wait_ge(filled, 1)
            nc.gpsimd.affine_select(out=w["below"][:], in_=w["ones"][:], compare_op=ALU.is_gt, fill=0.0, base=0,
                                    pattern=[[1, P]], channel_multiplier=-1)
            iota = dict(channel_multiplier=0, allow_small_or_imprecise_dtypes=True)
            nc.gpsimd.iota(w["prefer"][:], pattern=[[0, NT], [-1, E]], base=E, **iota)
            nc.gpsimd.iota(w["base"][:], pattern=[[REGION, E]], base=0, **iota)
            nc.gpsimd.iota(w["tile"][:], pattern=[[1, TILES]], base=0, **iota)
            nc.gpsimd.iota(w["row"][:], pattern=[[0, E]], base=0, channel_multiplier=1,
                           allow_small_or_imprecise_dtypes=True)
            nc.gpsimd.memset(w["steps"][:], 1.0).then_inc(filled, 1)
            pool.wait_ge(filled, 2)
            nc.gpsimd.memset(w["steps"][:, 0:1], 0.0)
    return w


def route_stage(nc, ctx, name, src, const, w, slots):
    sb = lambda n, s, d=F32: ctx.enter_context(nc.sbuf_tensor(f"{name}_{n}", s, d))
    sem = lambda n: ctx.enter_context(nc.semaphore(f"{name}_{n}"))
    r = dict(at=sb("at", [P, B * NT, 2], U32), gate=sb("gate", [P, B * NT, 2]),
             expert=sb("expert", [1, TILES], I32), start=sb("start", [1, TILES], I32))
    with ExitStack() as inner:
        sb = lambda n, s, d=F32: inner.enter_context(nc.sbuf_tensor(f"{name}_{n}", s, d))
        ps = lambda n, s: inner.enter_context(nc.psum_tensor(f"{name}_{n}", s, F32))
        xt_ps = ps("xt_ps", [P, T])
        norm = Norm(nc, inner, name, src, const, xt_ps)
        xt = [sb(f"xt{k}", [P, T]) for k in range(2)]
        logit_ps = ps("logit_ps", [P, NT, E])
        ahead_ps = ps("ahead_ps", [P, NT, E])
        total_ps = ps("total_ps", [P, E])
        logit, rest, same, rank = [sb(n, [P, NT, E]) for n in ("logit", "rest", "same", "rank")]
        best = sb("best", [P, NT, 1])
        chosen = sb("chosen", [P, NT, 2, E])
        both = sb("both", [P, NT, E], BF16)
        top, clamped, power, sigma = [sb(n, [P, NT, 2]) for n in ("top", "clamped", "power", "sigma")]
        gate_sum = sb("gate_sum", [P, NT, 1])
        place = sb("place", [P, NT, E])
        mine = sb("mine", [P, NT, 2, E])
        spot = sb("spot", [P, NT, 2])
        count = sb("count", [P, E])
        pad, pad_at = sb("pad", [P, E]), sb("pad_at", [P, E], U32)
        filled, tiles, jump = sb("filled", [P, E]), sb("tiles", [P, E]), sb("jump", [P, E])
        whole = sb("whole", [P, E], I32)
        ends = sb("ends", [P, E])
        tile = sb("tile", [P, TILES])
        behind = sb("behind", [P, TILES, E - 1])
        jumped = sb("jumped", [P, TILES, E - 1])
        summed = sb("summed", [P, TILES])
        sent = sb("sent", [P, B * NT * 2])
        passed, skipped = [sb(n, [P, B * NT * 2, E - 1]) for n in ("passed", "skipped")]
        xt_copied, logit_done, logit_copied, both_done, ahead_done, top_clamped, power_done, at_done, count_done, \
            pads_ready, step = [sem(n) for n in (
                "xt_copied", "logit_done", "logit_copied", "both_done", "ahead_done", "top_clamped", "power_done",
                "at_done", "count_done", "pads_ready", "step")]
        scattered, padded = slots["scattered"], slots["padded"]
        scattering = sem("scattering")
        at_now = [sb(f"at_now{k}", [P, NT, 2], U32) for k in range(2)]
        count_ready = sem("count_ready")
        STEPS = 19

        with nc.Block() as block:
            @block.sync
            def _(sp):
                def iteration(t):
                    if at := t.after(2):
                        norm.load(sp, at, norm.xn_done)

                skewed(sp, iteration, lead=2)

            @block.gpsimd
            def _(pool):
                def iteration(t):
                    if at := t.after(1):
                        norm.root(pool, at)
                    if at := t.after(0):
                        pool.wait_ge(at_done, at.u + 1)
                        pool.sem_inc(scattering, 1)
                        for i in range(NT):
                            for j in range(2):
                                nc.gpsimd.indirect_dma_start(
                                    slots["x"], bass.IndirectOffsetOnAxis(ap=at_now[at.par][:, i, j:j + 1], axis=0),
                                    norm.xn[at.par][:, i, :], None).then_inc(scattered[at.par], 16)

                skewed(pool, iteration, lead=1)
                pool.wait_ge(pads_ready, 1)
                for e in range(E):
                    nc.gpsimd.indirect_dma_start(slots["x"], bass.IndirectOffsetOnAxis(ap=pad_at[:, e:e + 1], axis=0),
                                                 w["zero"][:], None).then_inc(padded, 16)
                pool.wait_ge(padded, 16 * E)
                for par in range(2):
                    pool.wait_ge(scattered[par], 16 * 2 * NT * (B // 2))

            @block.tensor
            def _(pe):
                def iteration(t):
                    if at := t.after(0):
                        pe.wait_ge(xt_copied, at.u + 1)
                        pe.wait_ge(logit_copied, at.u)
                        for i in range(NT):
                            last = nc.tensor.matmul(logit_ps[:, i, :], xt[at.par][:, i * P:(i + 1) * P],
                                                    w["router"][:], start=True, stop=True)
                        last.then_inc(logit_done, 1)
                        pe.wait_ge(both_done, at.u + 1)
                        pe.wait_ge(count_done, at.u)
                        nc.tensor.matmul(ahead_ps[:], w["below"][:], both[:], start=True, stop=False)
                        for i in range(NT - 1):
                            nc.tensor.matmul(ahead_ps[:, i + 1:, :], w["ones"][:],
                                             both[:, i:i + 1, :].to_broadcast([P, NT - 1 - i, E]),
                                             start=False, stop=(i == NT - 2))
                        for i in range(NT):
                            last = nc.tensor.matmul(total_ps[:], w["ones"][:], both[:, i, :], start=(i == 0),
                                                    stop=(i == NT - 1))
                        last.then_inc(ahead_done, 1)
                    if at := t.after(1):
                        norm.transpose(pe, at)

                skewed(pe, iteration, lead=1)

            @block.scalar
            def _(act):
                def iteration(t):
                    if at := t.after(0):
                        act.wait_ge(top_clamped, at.u + 1)
                        nc.scalar.activation(power[:], clamped[:], ACT.Exp, scale=-1.0).then_inc(power_done, 1)
                    if at := t.after(1):
                        act.wait_ge(norm.xt_done[at.par], at.pair + 1)
                        nc.scalar.copy(xt[at.par][:], xt_ps[:]).then_inc(xt_copied, 1)

                skewed(act, iteration, lead=1)

            @block.vector
            def _(dve):
                V = nc.vector

                def iteration(t):
                    if at := t.after(0):
                        done = [0]

                        def then(ins):
                            done[0] += 1
                            ins.then_inc(step, 1)
                            dve.wait_ge(step, at.u * STEPS + done[0])

                        def wide(ap):
                            return ap.to_broadcast([P, NT, E])

                        def choose(j, values):
                            then(V.tensor_reduce(top[:, :, j:j + 1], values[:], AX_X, ALU.max))
                            then(V.tensor_tensor(same[:], values[:], wide(top[:, :, j:j + 1]), ALU.is_equal))
                            then(V.tensor_tensor(rank[:], same[:], w["prefer"][:], ALU.mult))
                            then(V.tensor_reduce(best[:], rank[:], AX_X, ALU.max))
                            then(V.tensor_tensor(chosen[:, :, j, :], rank[:], wide(best[:]), ALU.is_equal))

                        dve.wait_ge(logit_done, at.u + 1)
                        V.tensor_copy(logit[:], logit_ps[:]).then_inc(logit_copied, 1)
                        dve.wait_ge(logit_copied, at.u + 1)
                        choose(0, logit)
                        then(V.scalar_tensor_tensor(rest[:], chosen[:, :, 0, :], LOWEST, logit[:], ALU.mult, ALU.add))
                        choose(1, rest)
                        V.tensor_tensor(both[:], chosen[:, :, 0, :], chosen[:, :, 1, :], ALU.add).then_inc(both_done, 1)
                        V.tensor_scalar_max(clamped[:], top[:], -87.0).then_inc(top_clamped, 1)
                        if nxt := t.after(1):
                            norm.statistics(dve, nxt)
                        dve.wait_ge(ahead_done, at.u + 1)
                        then(V.tensor_tensor(place[:], ahead_ps[:], count[:].unsqueeze(1).to_broadcast([P, NT, E]),
                                             ALU.add))
                        V.tensor_tensor(count[:], count[:], total_ps[:], ALU.add).then_inc(count_done, 1)
                        then(V.tensor_tensor(mine[:], chosen[:], place[:].unsqueeze(2).to_broadcast([P, NT, 2, E]),
                                             ALU.mult))
                        then(V.tensor_reduce(spot[:], mine[:], AX_X, ALU.add))
                        V.tensor_copy(sent[:].rearrange("p (i j) -> p i j", j=2)[:, bass.ds(at.u * NT, NT), :], spot[:])
                        dve.wait_ge(scattered[at.par], 16 * 2 * NT * at.pair)
                        V.tensor_copy(at_now[at.par][:], spot[:]).then_inc(at_done, 1)
                        dve.wait_ge(power_done, at.u + 1)
                        then(V.tensor_scalar_add(sigma[:], power[:], 1.0))
                        then(V.reciprocal(power[:], sigma[:]))
                        then(V.tensor_tensor(gate_sum[:], power[:, :, 0:1], power[:, :, 1:2], ALU.add))
                        then(V.tensor_scalar(best[:], gate_sum[:], 1e-10, 2.0, ALU.add, ALU.mult))
                        then(V.reciprocal(gate_sum[:], best[:]))
                        V.tensor_tensor(r["gate"][:, bass.ds(at.u * NT, NT), :], power[:],
                                        gate_sum[:].to_broadcast([P, NT, 2]), ALU.mult)
                        assert done[0] == STEPS, done
                    elif nxt := t.after(1):
                        norm.statistics(dve, nxt)
                    if nxt := t.after(1):
                        if at:
                            dve.wait_ge(scattered[nxt.par], 16 * 2 * NT * nxt.pair)
                        norm.normalise(dve, nxt)

                V.tensor_copy(count[:], w["base"][:]).then_inc(count_ready, 1)
                dve.wait_ge(count_ready, 1)
                skewed(dve, iteration, lead=1)
                done = [0]

                def then(ins):
                    done[0] += 1
                    ins.then_inc(step, 1)
                    dve.wait_ge(step, B * STEPS + done[0])

                dve.wait_ge(count_done, B)
                then(V.tensor_tensor(pad[:], count[:], w["row"][:], ALU.add))
                V.tensor_copy(pad_at[:], pad[:]).then_inc(pads_ready, 1)
                then(V.tensor_tensor(filled[:], count[:], w["base"][:], ALU.subtract))
                then(V.tensor_scalar_add(tiles[:], filled[:], float(P - 1)))
                then(V.tensor_copy(whole[:], tiles[:]))
                then(V.tensor_scalar(whole[:], whole[:], P.bit_length() - 1, None, ALU.logical_shift_right))
                then(V.tensor_copy(tiles[:], whole[:]))
                for e in range(E):
                    then(V.tensor_reduce(ends[:, e:e + 1], tiles[:, 0:e + 1], AX_X, ALU.add))
                then(V.tensor_scalar(jump[:], tiles[:], -float(P), float(REGION), ALU.mult, ALU.add))
                then(V.tensor_scalar(tile[:], w["tile"][:], 1.0, ends[:, E - 1:E], ALU.add, ALU.min))
                then(V.tensor_scalar_add(tile[:], tile[:], -1.0))
                then(V.tensor_tensor(behind[:], tile[:].unsqueeze(2).to_broadcast([P, TILES, E - 1]),
                                     ends[:, 0:E - 1].unsqueeze(1).to_broadcast([P, TILES, E - 1]), ALU.is_ge))
                then(V.tensor_tensor(jumped[:], behind[:], jump[:, 0:E - 1].unsqueeze(1).to_broadcast([P, TILES, E - 1]),
                                     ALU.mult))
                then(V.tensor_reduce(summed[:], jumped[:], AX_X, ALU.add))
                then(V.scalar_tensor_tensor(tile[:], tile[:], float(P), summed[:], ALU.mult, ALU.add))
                V.tensor_copy(r["start"][:], tile[0:1, :])
                then(V.tensor_reduce(summed[:], behind[:], AX_X, ALU.add))
                V.tensor_copy(r["expert"][:], summed[0:1, :])
                wide = [P, B * NT * 2, E - 1]
                then(V.tensor_tensor(passed[:], sent[:].unsqueeze(2).to_broadcast(wide),
                                     w["base"][:, 1:].unsqueeze(1).to_broadcast(wide), ALU.is_ge))
                then(V.tensor_tensor(skipped[:], passed[:], jump[:, 0:E - 1].unsqueeze(1).to_broadcast(wide), ALU.mult))
                then(V.tensor_reduce(passed[:, :, 0], skipped[:], AX_X, ALU.add))
                V.tensor_tensor(r["at"][:].rearrange("p i j -> p (i j)"), sent[:], passed[:, :, 0], ALU.subtract)

    return r


def expert_stage(nc, name, const, w, r, slots):
    WAYS = 4
    with ExitStack() as ctx:
        sb = lambda n, s, d=F32: ctx.enter_context(nc.sbuf_tensor(f"{name}_{n}", s, d))
        ps = lambda n, s: ctx.enter_context(nc.psum_tensor(f"{name}_{n}", s, F32))
        sem = lambda n: ctx.enter_context(nc.semaphore(f"{name}_{n}"))
        x = [sb(f"x{k}", [P, D]) for k in range(WAYS)]
        hi = [sb(f"hi{k}", [P, P], F32R) for k in range(2)]
        lo = [sb(f"lo{k}", [P, P], F32R) for k in range(2)]
        silu = [sb(f"silu{k}", [P, HID]) for k in range(2)]
        h = [sb(f"h{k}", [P, 2, P]) for k in range(2)]
        ht = [sb(f"ht{k}", [P, 2, P]) for k in range(2)]
        y = [sb(f"y{k}", [P, D]) for k in range(WAYS)]
        xt_ps = [ps(f"xt_ps{k}", [P, P]) for k in range(2)]
        up_ps = [ps(f"up_ps{k}", [P, 2 * HID]) for k in range(2)]
        ht_ps = [ps(f"ht_ps{k}", [P, 2, P]) for k in range(2)]
        y_ps = [ps(f"y_ps{k}", [P, D]) for k in range(2)]
        x_loaded = [sem(f"x_loaded{k}") for k in range(WAYS)]
        y_stored = [sem(f"y_stored{k}") for k in range(WAYS)]
        xt_done, hi_done, lo_done, up_done, silu_done, h_done, ht_done, ht_copied, y_done, y_copied = [
            sem(n) for n in ("xt_done", "hi_done", "lo_done", "up_done", "silu_done", "h_done", "ht_done",
                             "ht_copied", "y_done", "y_copied")]

        with nc.Block() as block:
            @block.sync
            def _(sp):
                def iteration(t):
                    if at := t.after(4):
                        if t.after(0):
                            sp.wait_ge(xt_done, t.u + 1)
                        row = sp.value_load(r["start"][0:1, bass.ds(at.u, 1)], min_val=0, max_val=X_ROWS - P)
                        sp.dma_start(x[at.par][:], slots["x"][bass.ds(row, P), :]).then_inc(x_loaded[at.par], 16)
                    if at := t.after(-2):
                        sp.wait_ge(y_copied, at.u + 1)
                        sp.dma_start(slots["y"][bass.ds(at.u * P, P), :], y[at.par][:]).then_inc(y_stored[at.par], 16)

                skewed(sp, iteration, lead=4, lag=2, n=TILES, ways=WAYS)
                for k in range(WAYS):
                    sp.wait_ge(y_stored[k], 16 * TILES // WAYS)

            @block.tensor
            def _(pe):
                def iteration(t):
                    if at := t.after(0):
                        expert = pe.value_load(r["expert"][0:1, bass.ds(at.u, 1)], min_val=0, max_val=E - 1)
                        pe.wait_ge(lo_done, at.u + 1)
                        if t.after(-2):
                            pe.wait_ge(h_done, at.u - 1)
                        k = at.par % 2
                        one = bass.ds(expert, 1)
                        nc.tensor.matmul(up_ps[k][:], hi[k][:], w["hi"][:, one, :], start=True, stop=False)
                        nc.tensor.matmul(up_ps[k][:], lo[k][:], w["hi"][:, one, :], start=False, stop=False)
                        nc.tensor.matmul(up_ps[k][:], hi[k][:], w["lo"][:, one, :], start=False,
                                         stop=True).then_inc(up_done, 1)
                    if at := t.after(-1):
                        pe.wait_ge(h_done, at.u + 1)
                        for c in range(2):
                            last = nc.tensor.transpose(ht_ps[at.par % 2][:, c, :], h[at.par % 2][:, c, :],
                                                       const["ident"][:])
                        last.then_inc(ht_done, 1)
                    if at := t.after(2):
                        pe.wait_ge(x_loaded[at.par], 16 * (at.pair + 1))
                        nc.tensor.transpose(xt_ps[at.par % 2][:], x[at.par][:], const["ident"][:]).then_inc(xt_done, 1)
                    if at := t.after(-2):
                        expert = pe.value_load(r["expert"][0:1, bass.ds(at.u, 1)], min_val=0, max_val=E - 1)
                        pe.wait_ge(ht_copied, at.u + 1)
                        if at.after(-2):
                            pe.wait_ge(y_copied, at.u - 1)
                        for c in range(2):
                            last = nc.tensor.matmul(y_ps[at.par % 2][:], ht[at.par % 2][:, c, :],
                                                    w["down"][:, bass.ds(expert * 2 + c, 1), :],
                                                    start=(c == 0), stop=(c == 1))
                        last.then_inc(y_done, 1)

                skewed(pe, iteration, lead=2, lag=2, n=TILES, ways=WAYS)

            @block.scalar
            def _(act):
                def iteration(t):
                    if at := t.after(0):
                        act.wait_ge(up_done, at.u + 1)
                        if t.after(-2):
                            act.wait_ge(h_done, at.u - 1)
                        nc.scalar.activation(silu[at.par % 2][:], up_ps[at.par % 2][:, 0:HID],
                                             ACT.Silu).then_inc(silu_done, 1)
                    if at := t.after(-1):
                        act.wait_ge(ht_done, at.u + 1)
                        if at.after(-2):
                            act.wait_ge(y_done, at.u - 1)
                        nc.scalar.copy(ht[at.par % 2][:], ht_ps[at.par % 2][:]).then_inc(ht_copied, 1)
                    if at := t.after(2):
                        act.wait_ge(xt_done, at.u + 1)
                        nc.scalar.copy(hi[at.par % 2][:], xt_ps[at.par % 2][:]).then_inc(hi_done, 1)

                skewed(act, iteration, lead=2, lag=1, n=TILES, ways=WAYS)

            @block.vector
            def _(dve):
                def iteration(t):
                    if at := t.after(0):
                        dve.wait_ge(silu_done, at.u + 1)
                        if t.after(-2):
                            dve.wait_ge(ht_done, at.u - 1)
                        nc.vector.tensor_tensor(h[at.par % 2][:], silu[at.par % 2][:].rearrange("p (c h) -> p c h", c=2),
                                                up_ps[at.par % 2][:, HID:].rearrange("p (c h) -> p c h", c=2),
                                                ALU.mult).then_inc(h_done, 1)
                    if at := t.after(2):
                        dve.wait_ge(hi_done, at.u + 1)
                        nc.vector.tensor_tensor(lo[at.par % 2][:], xt_ps[at.par % 2][:], hi[at.par % 2][:].bitcast(F32),
                                                ALU.subtract).then_inc(lo_done, 1)
                    if at := t.after(-2):
                        dve.wait_ge(y_done, at.u + 1)
                        dve.wait_ge(y_stored[at.par], 16 * at.pair)
                        nc.vector.tensor_copy(y[at.par][:], y_ps[at.par % 2][:]).then_inc(y_copied, 1)

                skewed(dve, iteration, lead=2, lag=2, n=TILES, ways=WAYS)


def combine_stage(nc, name, src, dst, w, r, slots):
    with ExitStack() as ctx:
        sb = lambda n, s, d=F32: ctx.enter_context(nc.sbuf_tensor(f"{name}_{n}", s, d))
        sem = lambda n: ctx.enter_context(nc.semaphore(f"{name}_{n}"))
        x = [sb(f"x{k}", [P, NT, D]) for k in range(2)]
        z = [sb(f"z{k}", [P, NT, 2, D]) for k in range(2)]
        half = [sb(f"half{k}", [P, NT, D]) for k in range(2)]
        y = [sb(f"y{k}", [P, NT, D]) for k in range(2)]
        gate = [sb(f"gate{k}", [P, NT, 2]) for k in range(2)]
        place = [sb(f"place{k}", [P, NT, 2], U32) for k in range(2)]
        x_loaded, y_done, y_stored = [[sem(f"{n}{k}") for k in range(2)] for n in (
            "x_loaded", "y_done", "y_stored")]
        gathered = slots["gathered"]
        taken, half_done, gathering = sem("taken"), sem("half_done"), sem("gathering")
        src_v, dst_v = [a.rearrange("b (i p) d -> b p i d", p=P) for a in (src, dst)]

        with nc.Block() as block:
            @block.sync
            def _(sp):
                def iteration(t):
                    if at := t.after(2):
                        sp.wait_ge(y_done[at.par], at.pair)
                        sp.dma_start(x[at.par][:], src_v[at.u]).then_inc(x_loaded[at.par], 16)
                    if at := t.after(0):
                        sp.wait_ge(y_done[at.par], at.pair + 1)
                        sp.dma_start(dst_v[at.u], y[at.par][:]).then_inc(y_stored[at.par], 16)

                skewed(sp, iteration, lead=2)
                for par in range(2):
                    sp.wait_ge(y_stored[par], 16 * (B // 2))

            @block.gpsimd
            def _(pool):
                def iteration(t):
                    if at := t.after(1):
                        pool.wait_ge(taken, at.u + 1)
                        pool.wait_ge(y_done[at.par], at.pair)
                        pool.sem_inc(gathering, 1)
                        for i in range(NT):
                            for j in range(2):
                                nc.gpsimd.indirect_dma_start(
                                    z[at.par][:, i, j, :], None, slots["y"],
                                    bass.IndirectOffsetOnAxis(ap=place[at.par][:, i, j:j + 1], axis=0)).then_inc(
                                        gathered[at.par], 16)

                skewed(pool, iteration, lead=1)

            @block.vector
            def _(dve):
                def iteration(t):
                    if at := t.after(0):
                        dve.wait_ge(x_loaded[at.par], 16 * (at.pair + 1))
                        dve.wait_ge(gathered[at.par], 16 * 2 * NT * (at.pair + 1))
                        for i in range(NT):
                            last = nc.vector.scalar_tensor_tensor(half[at.par][:, i, :], z[at.par][:, i, 0, :],
                                                                  gate[at.par][:, i, 0:1], x[at.par][:, i, :],
                                                                  ALU.mult, ALU.add)
                        last.then_inc(half_done, 1)
                        dve.wait_ge(half_done, at.u + 1)
                        dve.wait_ge(y_stored[at.par], 16 * at.pair)
                        for i in range(NT):
                            last = nc.vector.scalar_tensor_tensor(y[at.par][:, i, :], z[at.par][:, i, 1, :],
                                                                  gate[at.par][:, i, 1:2], half[at.par][:, i, :],
                                                                  ALU.mult, ALU.add)
                        last.then_inc(y_done[at.par], 1)
                    if at := t.after(2):
                        dve.wait_ge(gathered[at.par], 16 * 2 * NT * at.pair)
                        dve.wait_ge(y_done[at.par], at.pair)
                        nc.vector.tensor_copy(gate[at.par][:], r["gate"][:, bass.ds(at.u * NT, NT), :])
                        nc.vector.tensor_copy(place[at.par][:], r["at"][:, bass.ds(at.u * NT, NT), :]).then_inc(taken, 1)

                skewed(dve, iteration, lead=2)


def macaron_kernel(nc, x, w_qk, w_v, w_out, b_out, cos, sin, router, w_gate, w_up, w_down, w_causal, b_causal,
                   u1, v1, b1, u2, v2, b2, out):
    dram = lambda n, s: nc.dram_tensor(n, s, F32).ap()
    between = [dram(f"between{k}", [B, T, D]) for k in range(5)]

    def moe_layer(name, src, dst, const, whole):
        sem = lambda n: whole.enter_context(nc.semaphore(f"{name}_{n}"))
        slots = dict(x=dram(f"{name}_sorted_x", [X_ROWS, D]), y=dram(f"{name}_sorted_y", [Y_ROWS, D]),
                     scattered=[sem(f"scattered{k}") for k in range(2)], padded=sem("padded"),
                     gathered=[sem(f"gathered{k}") for k in range(2)])
        with ExitStack() as ctx:
            w = load_moe_weights(nc, ctx, name, router, w_gate, w_up, w_down)
            r = route_stage(nc, ctx, f"{name}_route", src, const, w, slots)
            expert_stage(nc, f"{name}_expert", const, w, r, slots)
            combine_stage(nc, f"{name}_combine", src, dst, w, r, slots)

    with ExitStack() as whole:
        const = make_constants(nc, whole)
        moe_layer("moe_a", x, between[0], const, whole)
        with ExitStack() as ctx:
            w = load_heads_weights(nc, ctx, w_qk, w_v, w_out, b_out, cos, sin)
            heads_stage(nc, "heads", between[0], between[1], const, w)
        clear_semaphores(nc)
        moe_layer("moe_b", between[1], between[2], const, whole)
        w_ffn = load_ffn_weights(nc, whole, u1, v1, b1, u2, v2, b2)
        ffn_stage(nc, "ffn_a", between[2], between[3], const, w_ffn)
        clear_semaphores(nc)
        with ExitStack() as ctx:
            w = load_causal_weights(nc, ctx, w_causal, b_causal)
            causal_stage(nc, "causal", between[3], between[4], const, w)
        ffn_stage(nc, "ffn_b", between[4], out, const, w_ffn)


HEADS, D_HEAD = 16, 8


def _rope_tables():
    import numpy as np
    theta = (1.0 / np.float32(10000.0) ** (np.arange(0, D_HEAD, 2, dtype=np.float32) / np.float32(D_HEAD))).astype(np.float32)
    angles = np.outer(np.arange(T, dtype=np.float32), theta)
    angles = np.concatenate([angles, angles], axis=-1)
    sign = np.where(np.arange(D_HEAD) < D_HEAD // 2, -1, 1).astype(np.float32)
    rows = lambda tab: np.ascontiguousarray(np.broadcast_to(tab.T[None, :, None, :], (2, D_HEAD, HEADS // 2, T)).reshape(D, T))
    return rows(np.cos(angles).astype(np.float32)), rows(np.sin(angles).astype(np.float32) * sign)


def kernel(**inputs):
    import numpy as np
    import concourse.bacc as _bacc
    from concourse.bass_utils import run_bass_kernel_spmd as _run

    given = {k: np.asarray(v) for k, v in inputs.items()}
    w_qkv = given["L0_attn_w_qkv"]
    cos, sin = _rope_tables()
    laid = dict(
        x=given["L0_attn_x"],
        w_qk=w_qkv[:, :2 * D].reshape(D, 2, HEADS // 2, 2, D_HEAD).transpose(0, 1, 3, 4, 2).reshape(D, 2, D),
        w_v=w_qkv[:, 2 * D:], w_out=given["L0_attn_w_out"], b_out=given["L0_attn_b_out"], cos=cos, sin=sin,
        router=given["L0_ffn_router_w"].T, w_gate=given["L0_ffn_w_gate"], w_up=given["L0_ffn_w_up"],
        w_down=given["L0_ffn_w_down"], w_causal=given["L1_attn_W"], b_causal=given["L1_attn_b"],
        u1=given["L1_ffn_U1"], v1=given["L1_ffn_V1"], b1=given["L1_ffn_b1"], u2=given["L1_ffn_U2"],
        v2=given["L1_ffn_V2"], b2=given["L1_ffn_b2"])
    nc = _bacc.Bacc("TRN2", target_bir_lowering=False, num_devices=1)
    arrays, args = {}, []
    for name, a in laid.items():
        a = np.ascontiguousarray(a)
        arrays[f"in_{name}_dram"] = a
        args.append(nc.dram_tensor(f"in_{name}_dram", a.shape, mybir.dt.from_np(a.dtype), kind="ExternalInput").ap())
    args.append(nc.dram_tensor("out_0_dram", (B, T, D), F32, kind="ExternalOutput").ap())
    macaron_kernel(nc, *args)
    r = _run(nc, [arrays], core_ids=[0])
    return r.results[0]["out_0_dram"]
```

```python
from contextlib import ExitStack

import concourse.bass as bass
from concourse import mybir

F32 = mybir.dt.float32
F32R = mybir.dt.float32r
I32 = mybir.dt.int32
U32 = mybir.dt.uint32
ALU = mybir.AluOpType
ACT = mybir.ActivationFunctionType
AX_X = mybir.AxisListType.X

P = 128
B, T, D = 8, 512, 128
NT = T // P
EPS = 1e-5


class Norm:

    def __init__(self, nc, ctx, name, src, const, xt_ps, x=None):
        self.nc, self.src, self.const, self.xt_ps = nc, src, const, xt_ps
        sb = lambda n, s, d=F32: ctx.enter_context(nc.sbuf_tensor(f"{name}_{n}", s, d))
        sem = lambda n: ctx.enter_context(nc.semaphore(f"{name}_{n}"))
        self.x = x or [sb(f"x{k}", [P, NT, D]) for k in range(2)]
        self.xn = [sb(f"xn{k}", [P, NT, D]) for k in range(2)]
        self.stats = [sb(f"stats{k}", [P, NT, 6]) for k in range(2)]
        self.mv = [sb(f"mv{k}", [P, NT, 2]) for k in range(2)]
        self.var = [sb(f"var{k}", [P, NT]) for k in range(2)]
        self.rstd = [sb(f"rstd{k}", [P, NT]) for k in range(2)]
        self.x_loaded = [sem(f"x_loaded{k}") for k in range(2)]
        self.stats_done = sem("stats_done")
        self.aggregating = sem("aggregating")
        self.var_done = sem("var_done")
        self.eps_added = sem("eps_added")
        self.rstd_done = sem("rstd_done")
        self.xn_done = [sem(f"xn_done{k}") for k in range(2)]
        self.xt_done = [sem(f"xt_done{k}") for k in range(2)]

    def load(self, sp, at, x_free):
        u, pair, par = at.u, at.pair, at.par
        sp.wait_ge(x_free[par], pair)
        src = self.src.rearrange("b (i p) d -> b p i d", p=P)
        sp.dma_start(self.x[par][:], src[u]).then_inc(self.x_loaded[par], 16)

    def wait_for_x(self, dve, at):
        dve.wait_ge(self.x_loaded[at.par], 16 * (at.pair + 1))

    def statistics(self, dve, at):
        nc, u, pair, par = self.nc, at.u, at.pair, at.par
        self.wait_for_x(dve, at)
        for i in range(NT):
            last = nc.vector.bn_stats(self.stats[par][:, i, :], self.x[par][:, i, :])
        last.then_inc(self.stats_done, 1)
        dve.wait_ge(self.stats_done, u + 1)
        dve.sem_inc(self.aggregating, 1)
        for i in range(NT):
            last = nc.vector.bn_aggr(self.mv[par][:, i, :], self.stats[par][:, i, :])
        last.then_inc(self.var_done, 1)

    def root(self, pool, at):
        nc, u, pair, par = self.nc, at.u, at.pair, at.par
        pool.wait_ge(self.var_done, u + 1)
        nc.gpsimd.tensor_tensor(self.var[par][:], self.mv[par][:, :, 1], self.const["eps"][:, 0:NT],
                                ALU.add).then_inc(self.eps_added, 1)
        pool.wait_ge(self.eps_added, u + 1)
        nc.gpsimd.tensor_tensor(self.rstd[par][:], self.var[par][:], self.const["minus_half"][:, 0:NT],
                                ALU.pow).then_inc(self.rstd_done, 1)

    def normalise(self, dve, at):
        nc, u, pair, par = self.nc, at.u, at.pair, at.par
        dve.wait_ge(self.rstd_done, u + 1)
        dve.wait_ge(self.xt_done[par], pair)
        for i in range(NT):
            last = nc.vector.tensor_scalar(self.xn[par][:, i, :], self.x[par][:, i, :],
                                           self.mv[par][:, i, 0:1], self.rstd[par][:, i:i + 1],
                                           ALU.subtract, ALU.mult)
        last.then_inc(self.xn_done[par], 1)

    def transpose(self, pe, at):
        nc, u, pair, par = self.nc, at.u, at.pair, at.par
        pe.wait_ge(self.xn_done[par], pair + 1)
        for i in range(NT):
            last = nc.tensor.transpose(self.xt_ps[:, i * P:(i + 1) * P], self.xn[par][:, i, :],
                                       self.const["ident"][:])
        last.then_inc(self.xt_done[par], 1)


class Unit:

    def __init__(self, pair, par, n, ways=2):
        self.pair, self.par, self.n, self.ways, self.u = pair, par, n, ways, pair * ways + par

    def after(self, k):
        pair, par = self.pair + (self.par + k) // self.ways, (self.par + k) % self.ways
        if isinstance(pair, int) and not 0 <= pair < self.n // self.ways:
            return None
        return Unit(pair, par, self.n, self.ways)


def skewed(engine, iteration, lead, lag=0, n=B, ways=2):
    first, last = max((lag + ways - 1) // ways, 1), (n - lead) // ways
    for t in range(-lead, ways * first):
        iteration(Unit(t // ways, t % ways, n, ways))
    with engine.Fori(first, last) as pair:
        for k in range(ways):
            iteration(Unit(pair, k, n, ways))
    for t in range(ways * last, n + lag):
        iteration(Unit(t // ways, t % ways, n, ways))



def clear_semaphores(nc):
    given_back = sorted(nc.released_uncleared_semaphores)
    with nc.Block() as block:
        @block.gpsimd
        def _(pool):
            first = given_back[0]
            for number, following in zip(given_back, given_back[1:] + [None]):
                if following != number + 1:
                    pool.sem_clear(range(first, number + 1))
                    first = following


def make_constants(nc, ctx):
    sb = lambda n, s, d=F32: ctx.enter_context(nc.sbuf_tensor(n, s, d))
    const = dict(eps=sb("eps", [P, 8]), minus_half=sb("minus_half", [P, 8]), ident=sb("ident", [P, P]))
    zeroed = ctx.enter_context(nc.semaphore("ident_zeroed"))
    with nc.Block() as block:
        @block.gpsimd
        def _(pool):
            nc.gpsimd.memset(const["eps"][:], EPS)
            nc.gpsimd.memset(const["minus_half"][:], -0.5)
            nc.gpsimd.memset(const["ident"][:], 0.0).then_inc(zeroed, 1)
            pool.wait_ge(zeroed, 1)
            nc.gpsimd.affine_select(out=const["ident"][:], in_=const["ident"][:], compare_op=ALU.not_equal,
                                    fill=1.0, base=0, pattern=[[-1, P]], channel_multiplier=1)
    return const


R = 32
FF = 512
FC = FF // P


def load_ffn_weights(nc, ctx, U1, V1, b1, U2, V2, b2):
    sb = lambda n, s, d=F32: ctx.enter_context(nc.sbuf_tensor(f"ffn_{n}", s, d))
    w = dict(u1=sb("u1", [P, 4, R]), v1=sb("v1", [P, FF]), v1_hi=sb("v1_hi", [P, FF], F32R),
             v1_stack=sb("v1_stack", [P, FF], F32R), b1=sb("b1", [P, FC]), u2=sb("u2", [P, FC, R]),
             v2=sb("v2", [P, D]), v2_half=sb("v2_half", [P, D]), b2=sb("b2", [P, D]),
             b2_half=sb("b2_half", [P, D]))
    loaded = ctx.enter_context(nc.semaphore("ffn_weights_loaded"))
    split = ctx.enter_context(nc.semaphore("ffn_v1_split"))
    with nc.Block() as block:
        @block.sync
        def _(sp):
            for g in range(4):
                sp.dma_start(w["u1"][:, g, :], U1).then_inc(loaded, 16)
                sp.dma_start(w["v1"][g * R:(g + 1) * R, :], V1).then_inc(loaded, 16)
                sp.dma_start(w["v2"][g * R:(g + 1) * R, :], V2).then_inc(loaded, 16)
            sp.dma_start(w["b1"][:], b1.rearrange("(c p) -> p c", p=P),
                         allow_slow_non_contiguous=True).then_inc(loaded, 16)
            sp.dma_start(w["u2"][:], U2.rearrange("(c p) r -> p c r", p=P)).then_inc(loaded, 16)
            sp.dma_start(w["b2"][:], b2.partition_broadcast(P)).then_inc(loaded, 16)

        @block.vector
        def _(dve):
            dve.wait_ge(loaded, 15 * 16)
            nc.vector.tensor_scalar_mul(w["v2_half"][:], w["v2"][:], 0.5)
            nc.vector.tensor_scalar_mul(w["b2_half"][:], w["b2"][:], 0.5)
            nc.vector.tensor_copy(w["v1_hi"][:], w["v1"][:]).then_inc(split, 1)
            dve.wait_ge(split, 1)
            for g in (0, 2):
                rows = slice(g * R, (g + 1) * R)
                nc.vector.tensor_copy(w["v1_stack"][rows, :], w["v1"][rows, :])
            for g in (1, 3):
                rows = slice(g * R, (g + 1) * R)
                nc.vector.tensor_tensor(w["v1_stack"][rows, :], w["v1"][rows, :],
                                        w["v1_hi"][rows, :].bitcast(F32), ALU.subtract)
    return w


def ffn_stage(nc, name, src, dst, const, w, routed=None):
    with ExitStack() as ctx:
        sb = lambda n, s, d=F32: ctx.enter_context(nc.sbuf_tensor(f"{name}_{n}", s, d))
        ps = lambda n, s: ctx.enter_context(nc.psum_tensor(f"{name}_{n}", s, F32))
        sem = lambda n: ctx.enter_context(nc.semaphore(f"{name}_{n}"))
        xt_ps = ps("xt_ps", [P, T])
        norm = Combined(nc, ctx, name, src, const, xt_ps, *routed) if routed else \
            Norm(nc, ctx, name, src, const, xt_ps)
        xt = [sb(f"xt{k}", [P, T]) for k in range(2)]
        xb = [sb(f"xb{k}", [P, NT, D]) for k in range(2)]
        rank = [sb(f"rank{k}", [P, T], F32R) for k in range(2)]
        hid = [sb(f"hid{c}", [P, T]) for c in range(FC)]
        low = [sb(f"low{k}", [P, T]) for k in range(2)]
        y = [sb(f"y{k}", [P, NT, D]) for k in range(2)]
        rank_ps = ps("rank_ps", [P, T])
        hid_ps = [ps(f"hid_ps{k}", [P, T]) for k in range(3)]
        low_ps = ps("low_ps", [P, T])
        out_ps = [ps(f"out_ps{k}", [P, NT, D]) for k in range(2)]
        xt_copied, rank_done, rank_hi, rank_lo = [sem(n) for n in ("xt_copied", "rank_done", "rank_hi", "rank_lo")]
        hid_done, gelu_done, low_done, low_copied = [sem(n) for n in ("hid_done", "gelu_done", "low_done", "low_copied")]
        out_done = sem("out_done")
        xb_done = [sem(f"xb_done{k}") for k in range(2)]
        y_done = [sem(f"y_done{k}") for k in range(2)]
        y_stored = [sem(f"y_stored{k}") for k in range(2)]

        dst_v = dst.rearrange("b (i p) d -> b p i d", p=P)
        with nc.Block() as block:
            @block.sync
            def _(sp):
                def iteration(t):
                    if at := t.after(3):
                        if routed:
                            norm.load(sp, at)
                        else:
                            norm.load(sp, at, xb_done)
                    if at := t.after(0):
                        sp.wait_ge(y_done[at.par], at.pair + 1)
                        sp.dma_start(dst_v[at.u], y[at.par][:]).then_inc(y_stored[at.par], 16)

                skewed(sp, iteration, lead=3)
                for par in range(2):
                    sp.wait_ge(y_stored[par], 16 * (B // 2))

            @block.gpsimd
            def _(pool):
                def iteration(t):
                    if routed and (at := t.after(3)):
                        norm.gather(pool, at)
                    if at := t.after(2):
                        norm.root(pool, at)
                        pool.wait_ge(norm.xn_done[at.par], at.pair + 1)
                        pool.wait_ge(y_done[at.par], at.pair)
                        nc.gpsimd.tensor_tensor(xb[at.par][:], norm.x[at.par][:],
                                                w["b2_half"][:].unsqueeze(1).to_broadcast([P, NT, D]),
                                                ALU.add).then_inc(xb_done[at.par], 1)

                skewed(pool, iteration, lead=3 if routed else 2)

            @block.tensor
            def _(pe):
                def iteration(t):
                    if at := t.after(0):
                        pe.wait_ge(rank_lo, at.u + 1)
                        for c in range(FC):
                            pe.wait_ge(gelu_done, at.u * FC + max(c - 1, 0))
                            nc.tensor.matmul(hid_ps[c % 2][:], w["v1_stack"][:, c * P:(c + 1) * P],
                                             rank[at.par][:], start=True, stop=True).then_inc(hid_done, 1)
                    if at := t.after(1):
                        pe.wait_ge(xt_copied, at.u + 1)
                        nc.tensor.matmul(rank_ps[:], w["u1"][:].rearrange("p g r -> p (g r)"), xt[at.par][:],
                                         start=True, stop=True).then_inc(rank_done, 1)
                    if at := t.after(0):
                        pe.wait_ge(gelu_done, (at.u + 1) * FC)
                        for c in range(FC):
                            last = nc.tensor.matmul(low_ps[c * R:(c + 1) * R, :], w["u2"][:, c, :], hid[c][:],
                                                    start=True, stop=True)
                        last.then_inc(low_done, 1)
                        pe.wait_ge(low_copied, at.u + 1)
                        pe.wait_ge(y_done[at.par], at.pair)
                        for i in range(NT):
                            last = nc.tensor.matmul(out_ps[at.par][:, i, :], low[at.par][:, i * P:(i + 1) * P],
                                                    w["v2_half"][:], start=True, stop=True)
                        last.then_inc(out_done, 1)
                    if at := t.after(2):
                        norm.transpose(pe, at)

                skewed(pe, iteration, lead=2)

            @block.scalar
            def _(act):
                def iteration(t):
                    def gelu(at, c):
                        act.wait_ge(hid_done, at.u * FC + c + 1)
                        act.wait_ge(low_done, at.u)
                        nc.scalar.activation(hid[c][:], hid_ps[c % 2][:], ACT.Gelu_apprx_tanh,
                                             bias=w["b1"][:, c:c + 1]).then_inc(gelu_done, 1)

                    if at := t.after(0):
                        for c in range(FC):
                            gelu(at, c)
                    if at := t.after(1):
                        act.wait_ge(rank_done, at.u + 1)
                        nc.scalar.copy(rank[at.par][:], rank_ps[:]).then_inc(rank_hi, 1)
                    if at := t.after(0):
                        act.wait_ge(low_done, at.u + 1)
                        nc.scalar.copy(low[at.par][:], low_ps[:]).then_inc(low_copied, 1)
                    if at := t.after(2):
                        act.wait_ge(norm.xt_done[at.par], at.pair + 1)
                        nc.scalar.copy(xt[at.par][:], xt_ps[:]).then_inc(xt_copied, 1)

                skewed(act, iteration, lead=2)

            @block.vector
            def _(dve):
                def iteration(t):
                    if at := t.after(2):
                        if routed:
                            norm.combine(dve, at, xb_done, 1)
                        norm.statistics(dve, at)
                    if at := t.after(1):
                        dve.wait_ge(rank_hi, at.u + 1)
                        nc.vector.tensor_tensor(rank[at.par][64:P, :], rank_ps[64:P, :],
                                                rank[at.par][64:P, :].bitcast(F32),
                                                ALU.subtract).then_inc(rank_lo, 1)
                    if routed and (at := t.after(4)):
                        norm.take(dve, at)
                    if at := t.after(2):
                        norm.normalise(dve, at)
                    if at := t.after(0):
                        dve.wait_ge(out_done, at.u + 1)
                        dve.wait_ge(xb_done[at.par], at.pair + 1)
                        dve.wait_ge(y_stored[at.par], 16 * at.pair)
                        nc.vector.tensor_tensor(y[at.par][:], out_ps[at.par][:], xb[at.par][:],
                                                ALU.add).then_inc(y_done[at.par], 1)

                skewed(dve, iteration, lead=4 if routed else 2)


MASKED = -9000000000000000.0


def load_causal_weights(nc, ctx, W, bias):
    sb = lambda n, s, d=F32: ctx.enter_context(nc.sbuf_tensor(f"causal_{n}", s, d))
    w = dict(w=sb("w", [P, 3 * D]), bias=sb("bias", [P, 3]), bq=sb("bq", [P, 1]), bv=sb("bv", [P, D]),
             mask=sb("mask", [P, P]))
    loaded = ctx.enter_context(nc.semaphore("causal_weights_loaded"))
    zeroed = ctx.enter_context(nc.semaphore("causal_mask_zeroed"))
    with nc.Block() as block:
        @block.sync
        def _(sp):
            sp.dma_start(w["w"][:], W).then_inc(loaded, 16)
            sp.dma_start(w["bias"][:], bias.rearrange("(c p) -> p c", p=P),
                         allow_slow_non_contiguous=True).then_inc(loaded, 16)
            sp.dma_start(w["bv"][:], bias[2 * D:3 * D].partition_broadcast(P)).then_inc(loaded, 16)

        @block.vector
        def _(dve):
            dve.wait_ge(loaded, 3 * 16)
            nc.vector.tensor_scalar_mul(w["bq"][:], w["bias"][:, 0:1], float(D) ** -0.5)

        @block.gpsimd
        def _(pool):
            nc.gpsimd.memset(w["mask"][:], 0.0).then_inc(zeroed, 1)
            pool.wait_ge(zeroed, 1)
            nc.gpsimd.affine_select(out=w["mask"][:], in_=w["mask"][:], compare_op=ALU.is_ge, fill=MASKED,
                                    base=0, pattern=[[-1, P]], channel_multiplier=1)
    return w


def causal_stage(nc, name, src, dst, const, w):
    SCALE = float(D) ** -0.5
    with ExitStack() as ctx:
        sb = lambda n, s, d=F32: ctx.enter_context(nc.sbuf_tensor(f"{name}_{n}", s, d))
        ps = lambda n, s: ctx.enter_context(nc.psum_tensor(f"{name}_{n}", s, F32))
        sem = lambda n: ctx.enter_context(nc.semaphore(f"{name}_{n}"))
        xt_ps = ps("xt_ps", [P, T])
        norm = Norm(nc, ctx, name, src, const, xt_ps)
        xt = [sb(f"xt{k}", [P, T]) for k in range(2)]
        res = [sb(f"res{k}", [P, NT, D]) for k in range(2)]
        q = [sb(f"q{k}", [P, T]) for k in range(2)]
        k_ = [sb(f"k{k}", [P, T]) for k in range(2)]
        v = [sb(f"v{k}", [P, NT, D]) for k in range(2)]
        neg_max = [sb(f"neg_max{k}", [P, NT]) for k in range(2)]
        row_sum = [sb(f"row_sum{k}", [P, NT]) for k in range(2)]
        inv_sum = [sb(f"inv_sum{k}", [P, NT]) for k in range(2)]
        prob = [sb(f"prob{i}", [P, T]) for i in range(NT)]
        prob_t = [sb(f"prob_t{k}", [P, NT, P]) for k in range(2)]
        y = [sb(f"y{k}", [P, NT, D]) for k in range(2)]
        qv_ps, k_ps = ps("qv_ps", [P, T]), ps("k_ps", [P, T])
        score_ps = [ps(f"score_ps{k}", [P, T]) for k in range(2)]
        prob_t_ps = [ps(f"prob_t_ps{k}", [P, NT, P]) for k in range(2)]
        out_ps = ps("out_ps", [P, NT, D])
        (xt_copied, q_done, k_done, v_done, q_copied, k_copied, v_copied, res_done, score_done, mask_added,
         max_done, exp_done, prob_t_done, prob_t_copied, value_done, inv_done) = [
            sem(n) for n in ("xt_copied", "q_done", "k_done", "v_done", "q_copied", "k_copied", "v_copied",
                             "res_done", "score_done", "mask_added", "max_done", "exp_done", "prob_t_done",
                             "prob_t_copied", "value_done", "inv_done")]
        copying = sem("copying")
        res_copied = [sem(f"res_copied{k}") for k in range(2)]
        y_done = [sem(f"y_done{k}") for k in range(2)]
        y_stored = [sem(f"y_stored{k}") for k in range(2)]
        dst_v = dst.rearrange("b (i p) d -> b p i d", p=P)

        with nc.Block() as block:
            @block.sync
            def _(sp):
                def iteration(t):
                    if at := t.after(3):
                        norm.load(sp, at, res_copied)
                    if at := t.after(0):
                        sp.wait_ge(y_done[at.par], at.pair + 1)
                        sp.dma_start(dst_v[at.u], y[at.par][:]).then_inc(y_stored[at.par], 16)

                skewed(sp, iteration, lead=3)
                for par in range(2):
                    sp.wait_ge(y_stored[par], 16 * (B // 2))

            @block.gpsimd
            def _(pool):
                def iteration(t):
                    if at := t.after(2):
                        norm.root(pool, at)
                        pool.wait_ge(norm.xn_done[at.par], at.pair + 1)
                        pool.wait_ge(y_done[at.par], at.pair)
                        pool.sem_inc(copying, 1)
                        nc.gpsimd.tensor_copy(res[at.par][:], norm.x[at.par][:]).then_inc(res_copied[at.par], 1)

                skewed(pool, iteration, lead=2)

            @block.tensor
            def _(pe):
                def score(at, i):
                    pe.wait_ge(exp_done, at.u * NT + max(i - 1, 0))
                    n = (i + 1) * P
                    nc.tensor.matmul(score_ps[i % 2][:, 0:n], q[at.par][:, i * P:n], k_[at.par][:, 0:n],
                                     start=True, stop=True).then_inc(score_done, 1)

                def prob_transpose(at, i):
                    pe.wait_ge(exp_done, at.u * NT + i + 1)
                    pe.wait_ge(prob_t_copied, at.u * NT + max(i - 1, 0))
                    for j in range(i + 1):
                        last = nc.tensor.transpose(prob_t_ps[i % 2][:, j, :], prob[i][:, j * P:(j + 1) * P],
                                                   const["ident"][:])
                    last.then_inc(prob_t_done, 1)

                def values(at, i):
                    pe.wait_ge(prob_t_copied, at.u * NT + i + 1)
                    for j in range(i + 1):
                        last = nc.tensor.matmul(out_ps[:, i, :], prob_t[i % 2][:, j, :], v[at.par][:, j, :],
                                                start=(j == 0), stop=(j == i))
                    last.then_inc(value_done, 1)

                def iteration(t):
                    now, nxt = t.after(0), t.after(1)
                    if now:
                        pe.wait_ge(q_copied, now.u + 1)
                        pe.wait_ge(k_copied, now.u + 1)
                        score(now, 0)
                        score(now, 1)
                    if nxt:
                        pe.wait_ge(xt_copied, nxt.u + 1)
                        pe.wait_ge(v_copied, nxt.u)
                        nc.tensor.matmul(qv_ps[:], w["w"][:, 0:D], xt[nxt.par][:], start=True,
                                         stop=True).then_inc(q_done, 1)
                    if now:
                        score(now, 2)
                    if nxt:
                        pe.wait_ge(k_copied, nxt.u)
                        nc.tensor.matmul(k_ps[:], w["w"][:, D:2 * D], xt[nxt.par][:], start=True,
                                         stop=True).then_inc(k_done, 1)
                    if now:
                        score(now, 3)
                    if nxt:
                        pe.wait_ge(q_copied, nxt.u + 1)
                        for i in range(NT):
                            last = nc.tensor.matmul(qv_ps[:, i * P:(i + 1) * P], xt[nxt.par][:, i * P:(i + 1) * P],
                                                    w["w"][:, 2 * D:3 * D], start=True, stop=True)
                        last.then_inc(v_done, 1)
                    if now:
                        prob_transpose(now, 0)
                        prob_transpose(now, 1)
                        pe.wait_ge(v_copied, now.u + 1)
                        pe.wait_ge(y_done[1 - now.par], now.pair + now.par)
                        values(now, 0)
                        prob_transpose(now, 2)
                        values(now, 1)
                        prob_transpose(now, 3)
                        values(now, 2)
                        values(now, 3)
                    if ahead := t.after(2):
                        norm.transpose(pe, ahead)

                skewed(pe, iteration, lead=2)

            @block.scalar
            def _(act):
                def exponential(at, i):
                    n = (i + 1) * P
                    act.wait_ge(max_done, at.u * NT + i + 1)
                    act.wait_ge(prob_t_done, at.u * NT)
                    nc.scalar.activation(prob[i][:, 0:n], score_ps[i % 2][:, 0:n], ACT.Exp,
                                         bias=neg_max[at.par][:, i:i + 1],
                                         accum_out=row_sum[at.par][:, i:i + 1]).then_inc(exp_done, 1)

                def iteration(t):
                    now, nxt = t.after(0), t.after(1)
                    if now:
                        exponential(now, 0)
                        exponential(now, 1)
                    if nxt:
                        act.wait_ge(q_done, nxt.u + 1)
                        nc.scalar.activation(q[nxt.par][:], qv_ps[:], ACT.Identity, bias=w["bq"][:, 0:1],
                                             scale=SCALE).then_inc(q_copied, 1)
                    if now:
                        exponential(now, 2)
                        exponential(now, 3)
                        for i in (0, 1, 2, 3):
                            act.wait_ge(prob_t_done, now.u * NT + i + 1)
                            act.wait_ge(value_done, now.u * NT + max(i - 1, 0))
                            nc.scalar.copy(prob_t[i % 2][:, 0:i + 1, :],
                                           prob_t_ps[i % 2][:, 0:i + 1, :]).then_inc(prob_t_copied, 1)
                    if ahead := t.after(2):
                        act.wait_ge(norm.xt_done[ahead.par], ahead.pair + 1)
                        nc.scalar.copy(xt[ahead.par][:], xt_ps[:]).then_inc(xt_copied, 1)

                skewed(act, iteration, lead=2)

            @block.vector
            def _(dve):
                def row_max(at, i):
                    n = (i + 1) * P
                    dve.wait_ge(score_done, at.u * NT + i + 1)
                    nc.vector.tensor_tensor(score_ps[i % 2][:, i * P:n], score_ps[i % 2][:, i * P:n],
                                            w["mask"][:], ALU.add).then_inc(mask_added, 1)
                    dve.wait_ge(mask_added, at.u * NT + i + 1)
                    nc.vector.tensor_reduce(neg_max[at.par][:, i:i + 1], score_ps[i % 2][:, 0:n], AX_X, ALU.max,
                                            negate=True).then_inc(max_done, 1)

                def iteration(t):
                    now, nxt, ahead = t.after(0), t.after(1), t.after(2)
                    if now:
                        row_max(now, 0)
                        row_max(now, 1)
                    if ahead:
                        norm.statistics(dve, ahead)
                    if now:
                        row_max(now, 2)
                    if nxt:
                        dve.wait_ge(k_done, nxt.u + 1)
                        nc.vector.tensor_scalar(k_[nxt.par][:], k_ps[:], w["bias"][:, 1:2], None,
                                                ALU.add).then_inc(k_copied, 1)
                    if now:
                        row_max(now, 3)
                    if nxt:
                        dve.wait_ge(v_done, nxt.u + 1)
                        nc.vector.tensor_tensor(v[nxt.par][:], qv_ps[:].rearrange("p (i d) -> p i d", i=NT),
                                                w["bv"][:].unsqueeze(1).to_broadcast([P, NT, D]),
                                                ALU.add).then_inc(v_copied, 1)
                    if ahead:
                        norm.normalise(dve, ahead)
                    if now:
                        dve.wait_ge(exp_done, (now.u + 1) * NT)
                        nc.vector.reciprocal(inv_sum[now.par][:], row_sum[now.par][:]).then_inc(inv_done, 1)
                        dve.wait_ge(inv_done, now.u + 1)
                        dve.wait_ge(value_done, (now.u + 1) * NT)
                        dve.wait_ge(res_copied[now.par], now.pair + 1)
                        dve.wait_ge(y_stored[now.par], 16 * now.pair)
                        for i in range(NT):
                            last = nc.vector.scalar_tensor_tensor(
                                y[now.par][:, i, :], out_ps[:, i, :], inv_sum[now.par][:, i:i + 1],
                                res[now.par][:, i, :], ALU.mult, ALU.add)
                        last.then_inc(y_done[now.par], 1)

                skewed(dve, iteration, lead=2)


H = 16
DH = D // H
SLOTS = H // 2
PARTS = 4
MAX_ROW = PARTS * DH
KROWS = 64
HALF = SLOTS // 2


def load_heads_weights(nc, ctx, wqk, wv, wo, bo, cos, sin):
    sb = lambda n, s, d=F32: ctx.enter_context(nc.sbuf_tensor(f"heads_{n}", s, d))
    w = dict(qk=sb("qk", [P, 2, D]), rot=sb("rot", [P, 2, D]), v=sb("v", [P, D]), o=sb("o", [P, D]),
             bo=sb("bo", [P, D]), cos=sb("cos", [P, T]), sin=sb("sin", [P, T]), k_rest=sb("k_rest", [P, 1]))
    zeroed = ctx.enter_context(nc.semaphore("heads_k_rest_zeroed"))
    loaded = ctx.enter_context(nc.semaphore("heads_weights_loaded"))
    with nc.Block() as block:
        @block.sync
        def _(sp):
            sp.dma_start(w["qk"][:], wqk).then_inc(loaded, 16)
            for n in range(2):
                rot = w["rot"][:, n, :].rearrange("p (a e c) -> p a e c", e=2, c=DH // 2 * SLOTS)
                plain = wqk[:, n, :].rearrange("p (a e c) -> p a e c", e=2, c=DH // 2 * SLOTS)
                for e in range(2):
                    sp.dma_start(rot[:, :, e, :], plain[:, :, 1 - e, :]).then_inc(loaded, 16)
            sp.dma_start(w["v"][:], wv).then_inc(loaded, 16)
            sp.dma_start(w["o"][:], wo).then_inc(loaded, 16)
            sp.dma_start(w["bo"][:], bo.partition_broadcast(P)).then_inc(loaded, 16)
            sp.dma_start(w["cos"][:], cos).then_inc(loaded, 16)
            sp.dma_start(w["sin"][:], sin).then_inc(loaded, 16)
            sp.wait_ge(loaded, 10 * 16)

        @block.vector
        def _(dve):
            nc.vector.memset(w["k_rest"][:], 0.0).then_inc(zeroed, 1)
            dve.wait_ge(zeroed, 1)
            for low in range(2):
                row = 64 * low + MAX_ROW
                nc.vector.memset(w["k_rest"][row:row + 1, :], 1.0)
    return w


class Kept(Norm):

    def __init__(self, nc, ctx, name, const, xt_ps, x, given):
        super().__init__(nc, ctx, name, None, const, xt_ps, x)
        self.given = given

    def wait_for_x(self, dve, at):
        dve.wait_ge(self.given[at.par], at.pair + 1)


def heads_stage(nc, name, src, whole_src, dst, const, w, r, slots, w_route, r_next, slots_next):
    STEPS = H * NT
    SETS = STEPS // 4
    ITEMS = STEPS // 2
    M_B, V, XT, Q, QR, K, KR = 1, 3, 6, 9, 13, 17, 21
    NORM = (26, 29, 32, 35)
    M_A, BACK, PROJECT = 38, 42, 46
    TAKE, STATISTICS, NORMALISE = 1, 49, 58
    ROUTE_STATISTICS, ROUTE_NORMALISE, ROUTE_XT, LOGITS, COUNT, EXPONENT = 48, 53, 56, 60, 24, 5
    with ExitStack() as ctx:
        sb = lambda n, s, d=F32: ctx.enter_context(nc.sbuf_tensor(f"{name}_{n}", s, d))
        ps = lambda n, s: ctx.enter_context(nc.psum_tensor(f"{name}_{n}", s, F32))
        sem = lambda n: ctx.enter_context(nc.semaphore(f"{name}_{n}"))
        misc_ps = ps("misc_ps", [P, T])
        norm = Combined(nc, ctx, name, src, const, misc_ps, r, slots)
        xt = sb("xt", [P, T])
        res = [sb(f"res{k}", [P, NT, D]) for k in range(2)]
        by_cos, by_sin, rotated = sb("by_cos", [P, T]), sb("by_sin", [P, T]), sb("rotated", [P, T])
        hi = [sb(f"hi{n}", [P, T], F32R) for n in range(2)]
        lo = [sb(f"lo{n}", [P, T], F32R) for n in range(2)]
        qx = [sb(f"qx{k}", [P, SLOTS, T], F32R) for k in range(2)]
        kx = [sb(f"kx{k}", [P, SLOTS, T], F32R) for k in range(2)]
        vx = [sb(f"vx{k}", [P, NT, H, 32]) for k in range(2)]
        zero_row = sb("zero_row", [1, HALF, T])
        row_max = sb("row_max", [P, 2, 2, HALF, NT])
        neg_max = [sb(f"neg_max{k}", [32, P], F32R) for k in range(2)]
        prob = [sb(f"prob{k}", [P, T]) for k in range(8)]
        ot = [[sb(f"ot{k}{g}", [P, T]) for g in range(4)] for k in range(2)]
        inv_sum = sb("inv_sum", [P, NT, H])
        o = [sb(f"o{i}", [P, H, DH]) for i in range(NT)]
        oT = sb("oT", [P, T])
        y = [sb(f"y{k}", [P, NT, D]) for k in range(2)]
        max_ps = [ps(f"max_ps{k}", [P, 2, T]) for k in range(2)]
        score_ps = [ps(f"score_ps{k}", [P, T]) for k in range(2)]
        value_ps = ps("value_ps", [P, T])
        names = ("xt_copied qk_done cos_done sin_done rope_done hi_done lo_done v_done v_copied "
                 "max_done row_max_done m_turned m_negated score_done exp_done value_done ot_copied "
                 "turned inv_done o_done back_done back_copied project_done set_up k_filled")
        (xt_copied, qk_done, cos_done, sin_done, rope_done, hi_done, lo_done, v_done, v_copied,
         max_done, row_max_done, m_turned, m_negated, score_done, exp_done, value_done, ot_copied,
         turned, inv_done, o_done, back_done, back_copied, project_done, set_up, k_filled) = [sem(n) for n in names.split()]
        set_done = [sem(f"set_done{k}") for k in range(2)]
        res_loaded = [sem(f"res_loaded{k}") for k in range(2)]
        res_done = [sem(f"res_done{k}") for k in range(2)]
        y_done = [sem(f"y_done{k}") for k in range(2)]
        y_stored = [sem(f"y_stored{k}") for k in range(2)]
        expanded = [[sem(f"expanded{k}{half}") for half in range(2)] for k in range(2)]
        m_placed = [[sem(f"m_placed{k}{half}") for half in range(2)] for k in range(2)]
        kept = [sem(f"kept{k}") for k in range(2)]
        y_norm = Kept(nc, ctx, f"{name}_y_norm", const, misc_ps, y, y_done)
        router = Router(nc, ctx, f"{name}_router", y_norm, w_route, r_next, slots_next,
                        misc_ps[:, 0:NT * E].rearrange("p (i e) -> p i e", e=E),
                        misc_ps[:, NT * E:2 * NT * E].rearrange("p (i e) -> p i e", e=E),
                        misc_ps[:, 2 * NT * E:2 * NT * E + E])
        src_v = whole_src.rearrange("b (i p) d -> b p i d", p=P)
        dst_v = dst.rearrange("b (i p) d -> b p i d", p=P)
        spill_done = [sem(f"spill_done{k}") for k in range(2)]
        spilled = nc.dram_tensor(f"{name}_spilled", [2, 2, 2, 3, DH, SLOTS, T], F32).ap()
        max_spill_done = [sem(f"max_spill_done{half}") for half in range(2)]
        max_spilled = nc.dram_tensor(f"{name}_max_spilled", [2, 2, 2, HALF, NT, P], F32).ap()
        SPILLS, EXPANDS = 5 * 16, 10 * 16

        def rows(buf, head):
            at = 64 * (head % 2)
            return buf[at:at + KROWS, head // 2, :]


        with nc.Block() as block:
            @block.sync
            def _(sp):
                def place_max(at, half):
                    sp.wait_ge(m_negated, at.u * 2 + half + 1)
                    sp.dma_start(max_spilled[at.par, half].rearrange("a s i q -> (a s i) q"),
                                 neg_max[half][:].bitcast(F32)).then_inc(max_spill_done[half], 16)
                    sp.wait_ge(max_spill_done[half], 16 * (at.u + 1))
                    for par in range(2):
                        row = 64 * par + MAX_ROW
                        sp.dma_start(qx[at.par][row:row + 1, half * HALF:(half + 1) * HALF, :].bitcast(F32),
                                     max_spilled[at.par, half, par].rearrange("s i q -> s (i q)").unsqueeze(0)
                                     ).then_inc(m_placed[at.par][half], 16)

                def spill(at):
                    for n in range(2):
                        sp.wait_ge(lo_done, at.u * 2 + n + 1)
                        for half in range(2):
                            sp.wait_ge(expanded[at.par][half], EXPANDS * at.pair)
                        for part, source in enumerate((hi[n], lo[n], hi[n])[:2 + n]):
                            sp.dma_start(spilled[at.par, n, :, part].rearrange("a d s t -> a (d s) t"),
                                         source[:].bitcast(F32)).then_inc(spill_done[at.par], 16)

                def expand(at, half):
                    slots = slice(half * HALF, (half + 1) * HALF)
                    for n, wide in ((0, qx), (1, kx)):
                        for par in range(2):
                            for pair in range(2):
                                to = 64 * par + 2 * DH * pair
                                start = pair if n else 0
                                sp.dma_start(wide[at.par][to:to + 2 * DH, slots, :].bitcast(F32),
                                             spilled[at.par, n, par, start:start + 2, :, slots, :]
                                             .rearrange("l d s t -> (l d) s t")).then_inc(expanded[at.par][half], 16)
                    for par in range(2):
                        row = 64 * par + MAX_ROW
                        sp.dma_start(qx[at.par][row:row + 1, slots, :].bitcast(F32),
                                     zero_row[:]).then_inc(expanded[at.par][half], 16)

                def iteration(t):
                    if at := t.after(4):
                        norm.load(sp, at)
                    if at := t.after(0):
                        sp.wait_ge(y_done[at.par], at.pair)
                        sp.wait_ge(kept[at.par], 16 * (at.pair + 1))
                        sp.dma_start(res[at.par][:], src_v[at.u]).then_inc(res_loaded[at.par], 16)
                        place_max(at, 1)
                    if at := t.after(2):
                        spill(at)
                        sp.wait_ge(spill_done[at.par], SPILLS * (at.pair + 1))
                        if now := t.after(0):
                            sp.wait_ge(score_done, now.u * STEPS + STEPS // 2)
                        elif at.u == 0:
                            sp.wait_ge(set_up, 2)
                        expand(at, 0)
                    if at := t.after(1):
                        place_max(at, 0)
                    if at := t.after(-1):
                        sp.wait_ge(y_done[at.par], at.pair + 1)
                        sp.dma_start(dst_v[at.u], y[at.par][:]).then_inc(y_stored[at.par], 16)
                    if at := t.after(2):
                        if now := t.after(0):
                            sp.wait_ge(score_done, (now.u + 1) * STEPS)
                        expand(at, 1)
                    if at := t.after(3):
                        sp.wait_ge(norm.combined[at.par], at.pair + 1)
                        sp.dma_start(src_v[at.u], norm.x[at.par][:]).then_inc(kept[at.par], 16)

                skewed(sp, iteration, lead=4, lag=1)
                for par in range(2):
                    sp.wait_ge(y_stored[par], 16 * (B // 2))

            @block.gpsimd
            def _(pool):
                def iteration(t):
                    if at := t.after(0):
                        pool.wait_ge(res_loaded[at.par], 16 * (at.pair + 1))
                        nc.gpsimd.tensor_tensor(res[at.par][:], res[at.par][:],
                                                w["bo"][:].unsqueeze(1).to_broadcast([P, NT, D]),
                                                ALU.add).then_inc(res_done[at.par], 1)
                    if at := t.after(2):
                        for n in range(2):
                            pool.wait_ge(sin_done, at.u * 2 + n + 1)
                            pool.wait_ge(lo_done, at.u * 2 + n)
                            nc.gpsimd.tensor_tensor(rotated[:], by_cos[:], by_sin[:], ALU.add).then_inc(rope_done, 1)
                            pool.wait_ge(hi_done, at.u * 2 + n + 1)
                            nc.gpsimd.tensor_tensor(lo[n][:], rotated[:], hi[n][:].bitcast(F32),
                                                    ALU.subtract).then_inc(lo_done, 1)

                    if at := t.after(-2):
                        router.scatter(pool, at)
                    if at := t.after(-1):
                        y_norm.root(pool, at)
                    if at := t.after(3):
                        norm.root(pool, at)
                    if at := t.after(4):
                        norm.gather(pool, at)

                skewed(pool, iteration, lead=4, lag=2)

            @block.tensor
            def _(pe):
                def values(at, s):
                    g, c = s // NT, s % NT
                    pe.wait_ge(exp_done, at.u * STEPS + 4 * s + 4)
                    if s == 0:
                        pe.wait_ge(set_up, 2)
                        pe.wait_ge(v_copied, at.u + 1)
                    if c == 0:
                        pe.wait_ge(ot_copied, at.u * 4 + g)
                    for j in range(4):
                        last = nc.tensor.matmul(value_ps[32 * j:32 * j + 32, :], vx[at.par][:, c, 4 * g + j, :],
                                                prob[4 * (s % 2) + j][:], start=(c == 0), stop=(c == NT - 1))
                    last.then_inc(set_done[s % 2], 1)

                def score(at, k):
                    head, c = 4 * (k // 16) + k % 4, k // 4 % NT
                    pe.wait_ge(exp_done, at.u * STEPS + max(k - 1, 0))
                    if k % (STEPS // 2) == 0:
                        pe.wait_ge(m_placed[at.par][k // (STEPS // 2)], 32 * (at.pair + 1))
                    nc.tensor.matmul(score_ps[k % 2][:], rows(kx[at.par], head)[:, c * P:(c + 1) * P],
                                     rows(qx[at.par], head), start=True, stop=True).then_inc(score_done, 1)

                def score_for_max(at, n):
                    head = n // 2
                    if n == 0:
                        pe.wait_ge(set_up, 2)
                        pe.wait_ge(k_filled, 4)
                    if n % (ITEMS // 2) == 0:
                        pe.wait_ge(expanded[at.par][n // (ITEMS // 2)], EXPANDS * (at.pair + 1))
                    pe.wait_ge(row_max_done, at.u * ITEMS + max(n - 1, 0))
                    for i in range(2):
                        tile = 2 * (n % 2) + i
                        last = nc.tensor.matmul(
                            max_ps[n % 2][:, i, :], rows(qx[at.par], head)[:, tile * P:(tile + 1) * P],
                            rows(kx[at.par], head), start=True, stop=True)
                    last.then_inc(max_done, 1)

                def turn_max(at, half):
                    pe.wait_ge(row_max_done, at.u * ITEMS + (half + 1) * ITEMS // 2)
                    nc.tensor.transpose(misc_ps[0:32, 0:P], row_max[:, half].rearrange("p a s i -> p (a s i)"),
                                        const["ident"][:]).then_inc(m_turned, 1)

                def product(at, weights, done):
                    nc.tensor.matmul(misc_ps[:], weights, xt[:], start=True, stop=True).then_inc(done, 1)

                def iteration(t):
                    past, prev, now, nxt, ahead = [t.after(n) for n in range(-2, 3)]
                    for k in range(STEPS):
                        if k % 4 == 2:
                            s = k // 4 - 1
                            if s < 0 and prev:
                                values(prev, SETS - 1)
                            if s >= 0 and now:
                                values(now, s)
                        if now:
                            score(now, k)
                        if nxt and k % 2:
                            score_for_max(nxt, k // 2)
                        if now and k == M_B:
                            pe.wait_ge(m_negated, now.u * 2 + 1)
                            if now.after(-2):
                                pe.wait_ge(router.logit_copied, now.u - 1)
                            turn_max(now, 1)
                        if nxt and k == V:
                            if now:
                                pe.wait_ge(m_negated, now.u * 2 + 2)
                            pe.wait_ge(sin_done, (nxt.u + 1) * 2)
                            for i in range(NT):
                                last = nc.tensor.matmul(misc_ps[:, i * P:(i + 1) * P], xt[:, i * P:(i + 1) * P],
                                                        w["v"][:], start=True, stop=True)
                            last.then_inc(v_done, 1)
                        if ahead and k == XT:
                            if nxt:
                                pe.wait_ge(v_copied, nxt.u + 1)
                            norm.transpose(pe, ahead)
                        if ahead and k == Q:
                            pe.wait_ge(xt_copied, ahead.u + 1)
                            product(ahead, w["qk"][:, 0, :], qk_done)
                        if ahead and k == QR:
                            pe.wait_ge(cos_done, ahead.u * 2 + 1)
                            product(ahead, w["rot"][:, 0, :], qk_done)
                        if ahead and k == K:
                            pe.wait_ge(sin_done, ahead.u * 2 + 1)
                            product(ahead, w["qk"][:, 1, :], qk_done)
                        if ahead and k == KR:
                            pe.wait_ge(cos_done, ahead.u * 2 + 2)
                            product(ahead, w["rot"][:, 1, :], qk_done)
                        if past and k == COUNT:
                            if ahead:
                                pe.wait_ge(sin_done, (ahead.u + 1) * 2)
                            elif nxt:
                                pe.wait_ge(v_copied, nxt.u + 1)
                            elif now:
                                pe.wait_ge(m_negated, now.u * 2 + 2)
                            router.count(pe, past)
                        if prev and k in NORM:
                            i = NORM.index(k)
                            pe.wait_ge(ot_copied, (prev.u + 1) * 4)
                            if past:
                                pe.wait_ge(router.count_done, past.u + 1)
                            elif ahead:
                                pe.wait_ge(sin_done, (ahead.u + 1) * 2)
                            elif nxt:
                                pe.wait_ge(v_copied, nxt.u + 1)
                            elif now:
                                pe.wait_ge(m_negated, now.u * 2 + 2)
                            pe.wait_ge(o_done, prev.u * NT + i)
                            for g in range(4):
                                last = nc.tensor.transpose(misc_ps[:, g * P:(g + 1) * P],
                                                           ot[prev.par][g][:, i * P:(i + 1) * P], const["ident"][:])
                            last.then_inc(turned, 1)
                        if nxt and k == M_A:
                            if prev:
                                pe.wait_ge(o_done, (prev.u + 1) * NT)
                            elif ahead:
                                pe.wait_ge(sin_done, (ahead.u + 1) * 2)
                            turn_max(nxt, 0)
                        if prev and k == BACK:
                            if nxt:
                                pe.wait_ge(m_negated, nxt.u * 2 + 1)
                            pe.wait_ge(o_done, (prev.u + 1) * NT)
                            for i in range(NT):
                                last = nc.tensor.transpose(misc_ps[:, i * P:(i + 1) * P],
                                                           o[i][:].rearrange("p h d -> p (h d)"), const["ident"][:])
                            last.then_inc(back_done, 1)
                        if prev and k == PROJECT:
                            pe.wait_ge(back_copied, prev.u + 1)
                            for i in range(NT):
                                last = nc.tensor.matmul(misc_ps[:, i * P:(i + 1) * P], oT[:, i * P:(i + 1) * P],
                                                        w["o"][:], start=True, stop=True)
                            last.then_inc(project_done, 1)
                        if prev and k == ROUTE_XT:
                            y_norm.transpose(pe, prev)
                        if prev and k == LOGITS:
                            router.logits(pe, prev)

                skewed(pe, iteration, lead=2, lag=2)

            @block.scalar
            def _(act):
                def iteration(t):
                    past, prev, now, nxt, ahead = [t.after(n) for n in range(-2, 3)]
                    for k in range(STEPS):
                        if now:
                            s = k // 4
                            act.wait_ge(score_done, now.u * STEPS + k + 1)
                            if k % 4 == 0:
                                act.wait_ge(set_done[s % 2], now.u * (SETS // 2) + s // 2)
                            nc.scalar.activation(prob[k % 8][:], score_ps[k % 2][:], ACT.Exp,
                                                 scale=float(DH) ** -0.5).then_inc(exp_done, 1)
                        if k % 16 == 3:
                            g = k // 16 - 1
                            at = now if g >= 0 else prev
                            if at:
                                g %= 4
                                act.wait_ge(set_done[1], at.u * (SETS // 2) + 2 * g + 2)
                                if at.after(-2):
                                    act.wait_ge(turned, (at.u - 1) * NT)
                                nc.scalar.copy(ot[at.par][g][:], value_ps[:]).then_inc(ot_copied, 1)
                        if prev and k == BACK + 1:
                            act.wait_ge(back_done, prev.u + 1)
                            nc.scalar.copy(oT[:], misc_ps[:]).then_inc(back_copied, 1)
                        if past and k == EXPONENT:
                            router.exponent(act, past)
                        if prev and k == ROUTE_XT + 1:
                            router.copy_xt(act, prev)
                        if ahead and k == XT + 1:
                            act.wait_ge(norm.xt_done[ahead.par], ahead.pair + 1)
                            if nxt:
                                act.wait_ge(v_done, nxt.u + 1)
                            nc.scalar.copy(xt[:], misc_ps[:]).then_inc(xt_copied, 1)
                        for n, at_step in ((0, QR + 5), (1, KR + 5)):
                            if ahead and k == at_step:
                                act.wait_ge(rope_done, ahead.u * 2 + n + 1)
                                act.wait_ge(spill_done[1 - ahead.par], SPILLS * (ahead.pair + ahead.par))
                                nc.scalar.copy(hi[n][:], rotated[:]).then_inc(hi_done, 1)

                for par in range(2):
                    for low in range(2):
                        row = 64 * low + MAX_ROW
                        nc.scalar.copy(kx[par][row:row + 32, :, :].rearrange("p s t -> p (s t)"),
                                       w["k_rest"][row:row + 32, :].to_broadcast([32, SLOTS * T])).then_inc(k_filled, 1)
                skewed(act, iteration, lead=2, lag=2)

            @block.vector
            def _(dve):
                def negate(at, half):
                    dve.wait_ge(m_turned, at.u * 2 + half + 1)
                    dve.wait_ge(max_spill_done[half], 16 * at.u)
                    nc.vector.tensor_scalar_mul(neg_max[half][:], misc_ps[0:32, 0:P], -1.0).then_inc(m_negated, 1)

                def iteration(t):
                    past, prev, now, nxt, ahead, normed, fetched = [t.after(n) for n in range(-2, 5)]
                    for k in range(STEPS):
                        if nxt and k % 2:
                            n = k // 2
                            half, head, tile = n // (ITEMS // 2), n // 2, 2 * (n % 2)
                            dve.wait_ge(max_done, nxt.u * ITEMS + n + 1)
                            if n % (ITEMS // 2) == 0:
                                dve.wait_ge(m_turned, nxt.u * 2 - 1 + half if half else nxt.u * 2)
                            nc.vector.tensor_reduce(row_max[:, half, head % 2, head // 2 % HALF, tile:tile + 2],
                                                    max_ps[n % 2][:], AX_X, ALU.max).then_inc(row_max_done, 1)
                        if now and k == M_B + 1:
                            negate(now, 1)
                        if nxt and k == V + 1:
                            dve.wait_ge(v_done, nxt.u + 1)
                            if prev:
                                dve.wait_ge(set_done[1], (prev.u + 1) * (SETS // 2))
                            nc.vector.tensor_copy(vx[nxt.par][:, :, :, 0:DH],
                                                  misc_ps[:].rearrange("p (i h d) -> p i h d", i=NT, h=H)
                                                  ).then_inc(v_copied, 1)
                        for n, at_step in ((0, Q + 1), (1, K + 1)):
                            if ahead and k == at_step:
                                dve.wait_ge(qk_done, ahead.u * 4 + 2 * n + 1)
                                dve.wait_ge(rope_done, ahead.u * 2 + n)
                                nc.vector.tensor_tensor(by_cos[:], misc_ps[:], w["cos"][:], ALU.mult).then_inc(cos_done, 1)
                        for n, at_step in ((0, QR + 1), (1, KR + 1)):
                            if ahead and k == at_step:
                                dve.wait_ge(qk_done, ahead.u * 4 + 2 * n + 2)
                                nc.vector.tensor_tensor(by_sin[:], misc_ps[:], w["sin"][:], ALU.mult).then_inc(sin_done, 1)
                        if prev and k - 1 in NORM:
                            i = NORM.index(k - 1)
                            dve.wait_ge(turned, prev.u * NT + i + 1)
                            wide = misc_ps[:].rearrange("p (h c) -> p h c", c=32)
                            nc.vector.reciprocal(inv_sum[:, i, :], wide[:, :, DH]).then_inc(inv_done, 1)
                            dve.wait_ge(inv_done, prev.u * NT + i + 1)
                            dve.wait_ge(back_done, prev.u)
                            nc.vector.tensor_tensor(o[i][:], wide[:, :, 0:DH],
                                                    inv_sum[:, i, :].unsqueeze(2).to_broadcast([P, H, DH]),
                                                    ALU.mult).then_inc(o_done, 1)
                        if nxt and k == M_A + 1:
                            negate(nxt, 0)
                        if prev and k == PROJECT + 1:
                            dve.wait_ge(project_done, prev.u + 1)
                            dve.wait_ge(y_stored[prev.par], 16 * prev.pair)
                            dve.wait_ge(res_done[prev.par], prev.pair + 1)
                            nc.vector.tensor_tensor(y[prev.par][:], misc_ps[:].rearrange("p (i d) -> p i d", i=NT),
                                                    res[prev.par][:], ALU.add).then_inc(y_done[prev.par], 1)
                        if fetched and k == TAKE:
                            norm.take(dve, fetched)
                        if prev and k == ROUTE_STATISTICS:
                            y_norm.statistics(dve, prev)
                        if prev and k == ROUTE_NORMALISE:
                            router.normalise(dve, prev)
                        if prev and k == LOGITS + 1:
                            router.choose(dve, prev)
                        if past and k == COUNT + 1:
                            router.positions(dve, past)
                        if past and k == COUNT + 4:
                            router.gates(dve, past)
                        if fetched and not normed and k == TAKE + 1:
                            nc.vector.memset(zero_row[:], 0.0)
                            for par in range(2):
                                for low in range(2):
                                    row = 64 * low + MAX_ROW
                                    nc.vector.memset(qx[par][row:row + 32, :, :].bitcast(F32), 0.0)
                                nc.vector.memset(vx[par][:, :, :, DH + 1:32], 0.0)
                                nc.vector.memset(vx[par][:, :, :, DH:DH + 1], 1.0).then_inc(set_up, 1)
                        if normed and k == STATISTICS:
                            norm.combine(dve, normed, kept, 16)
                            norm.statistics(dve, normed)
                        if normed and k == NORMALISE:
                            norm.normalise(dve, normed)

                router.begin(dve)
                skewed(dve, iteration, lead=4, lag=2)


E = 8
HID = 256
BF16 = mybir.dt.bfloat16
REGION = B * T + P
TILES = 2 * B * T // P + E
LOWEST = -3.0e38
X_ROWS = E * REGION
Y_ROWS = TILES * P


def make_route_constants(nc, ctx, router):
    sb = lambda n, s, d=F32: ctx.enter_context(nc.sbuf_tensor(f"route_{n}", s, d))
    w = dict(router=sb("router", [P, E]), below=sb("below", [P, P], BF16), ones=sb("ones", [P, P], BF16),
             prefer=sb("prefer", [P, NT, E]), base=sb("base", [P, E]), row=sb("row", [P, E]),
             tile=sb("tile", [P, TILES]), zero=sb("zero", [P, D]))
    loaded = ctx.enter_context(nc.semaphore("router_loaded"))
    filled = ctx.enter_context(nc.semaphore("route_constants_filled"))
    with nc.Block() as block:
        @block.sync
        def _(sp):
            sp.dma_start(w["router"][:], router).then_inc(loaded, 16)
            sp.wait_ge(loaded, 16)

        @block.gpsimd
        def _(pool):
            nc.gpsimd.memset(w["zero"][:], 0.0)
            nc.gpsimd.memset(w["ones"][:], 1.0).then_inc(filled, 1)
            pool.wait_ge(filled, 1)
            nc.gpsimd.affine_select(out=w["below"][:], in_=w["ones"][:], compare_op=ALU.is_gt, fill=0.0, base=0,
                                    pattern=[[1, P]], channel_multiplier=-1)
            iota = dict(channel_multiplier=0, allow_small_or_imprecise_dtypes=True)
            nc.gpsimd.iota(w["prefer"][:], pattern=[[0, NT], [-1, E]], base=E, **iota)
            nc.gpsimd.iota(w["base"][:], pattern=[[REGION, E]], base=0, **iota)
            nc.gpsimd.iota(w["tile"][:], pattern=[[1, TILES]], base=0, **iota)
            nc.gpsimd.iota(w["row"][:], pattern=[[0, E]], base=0, channel_multiplier=1,
                           allow_small_or_imprecise_dtypes=True)
    return w


def make_tables(nc, ctx, name):
    sb = lambda n, s, d=F32: ctx.enter_context(nc.sbuf_tensor(f"{name}_{n}", s, d))
    return dict(sent=sb("sent", [P, B * NT, 2]), at=sb("at", [P, B * NT, 2], U32), gate=sb("gate", [P, B * NT, 2]),
                count=sb("count", [P, E]), expert=sb("expert", [1, TILES], I32), start=sb("start", [1, TILES], I32))


class Router:

    def __init__(self, nc, ctx, name, norm, w, r, slots, logit_ps, ahead_ps, total_ps):
        sb = lambda n, s, d=F32: ctx.enter_context(nc.sbuf_tensor(f"{name}_{n}", s, d))
        sem = lambda n: ctx.enter_context(nc.semaphore(f"{name}_{n}"))
        self.nc, self.norm, self.w, self.r, self.slots = nc, norm, w, r, slots
        self.logit_ps, self.ahead_ps, self.total_ps = logit_ps, ahead_ps, total_ps
        self.xt = sb("xt", [P, T])
        self.logit, self.rest, self.same, self.rank, self.place = [
            sb(n, [P, NT, E]) for n in ("logit", "rest", "same", "rank", "place")]
        self.best, self.gate_sum, self.twice = [sb(n, [P, NT, 1]) for n in ("best", "gate_sum", "twice")]
        self.chosen, self.mine = [sb(n, [P, NT, 2, E]) for n in ("chosen", "mine")]
        self.both = sb("both", [P, NT, E], BF16)
        self.top, self.clamped, self.power, self.sigma, self.spot = [
            sb(n, [P, NT, 2]) for n in ("top", "clamped", "power", "sigma", "spot")]
        self.at_now = [sb(f"at_now{k}", [P, NT, 2], U32) for k in range(2)]
        self.scattered = slots["scattered"]
        (self.xt_copied, self.logit_done, self.logit_copied, self.both_done, self.ahead_done, self.top_clamped,
         self.power_done, self.at_done, self.count_done, self.count_ready, self.scattering, self.choice,
         self.position, self.gating) = [sem(n) for n in (
             "xt_copied", "logit_done", "logit_copied", "both_done", "ahead_done", "top_clamped", "power_done",
             "at_done", "count_done", "count_ready", "scattering", "choice", "position", "gating")]

    def begin(self, dve):
        self.nc.vector.tensor_copy(self.r["count"][:], self.w["base"][:]).then_inc(self.count_ready, 1)
        dve.wait_ge(self.count_ready, 1)

    def normalise(self, dve, at):
        dve.wait_ge(self.scattered[at.par], 16 * 2 * NT * at.pair)
        self.norm.normalise(dve, at)

    def copy_xt(self, act, at):
        act.wait_ge(self.norm.xt_done[at.par], at.pair + 1)
        act.wait_ge(self.logit_done, at.u)
        self.nc.scalar.copy(self.xt[:], self.norm.xt_ps[:]).then_inc(self.xt_copied, 1)

    def logits(self, pe, at):
        nc = self.nc
        pe.wait_ge(self.xt_copied, at.u + 1)
        pe.wait_ge(self.logit_copied, at.u)
        for i in range(NT):
            last = nc.tensor.matmul(self.logit_ps[:, i, :], self.xt[:, i * P:(i + 1) * P], self.w["router"][:],
                                    start=True, stop=True)
        last.then_inc(self.logit_done, 1)

    def choose(self, dve, at):
        V, top, chosen = self.nc.vector, self.top, self.chosen
        wide = [P, NT, E]
        STEPS = 11
        dve.wait_ge(self.logit_done, at.u + 1)
        V.tensor_copy(self.logit[:], self.logit_ps).then_inc(self.logit_copied, 1)
        dve.wait_ge(self.logit_copied, at.u + 1)
        for j, values in enumerate((self.logit, self.rest)):
            done = at.u * STEPS + j * 6
            V.tensor_reduce(top[:, :, j:j + 1], values[:], AX_X, ALU.max).then_inc(self.choice, 1)
            dve.wait_ge(self.choice, done + 1)
            V.tensor_tensor(self.same[:], values[:], top[:, :, j:j + 1].to_broadcast(wide),
                            ALU.is_equal).then_inc(self.choice, 1)
            dve.wait_ge(self.choice, done + 2)
            V.tensor_tensor(self.rank[:], self.same[:], self.w["prefer"][:], ALU.mult).then_inc(self.choice, 1)
            dve.wait_ge(self.choice, done + 3)
            V.tensor_reduce(self.best[:], self.rank[:], AX_X, ALU.max).then_inc(self.choice, 1)
            dve.wait_ge(self.choice, done + 4)
            V.tensor_tensor(chosen[:, :, j, :], self.rank[:], self.best[:].to_broadcast(wide),
                            ALU.is_equal).then_inc(self.choice, 1)
            dve.wait_ge(self.choice, done + 5)
            if j == 0:
                V.scalar_tensor_tensor(self.rest[:], chosen[:, :, 0, :], LOWEST, self.logit[:], ALU.mult,
                                       ALU.add).then_inc(self.choice, 1)
                dve.wait_ge(self.choice, done + 6)
        V.tensor_tensor(self.both[:], chosen[:, :, 0, :], chosen[:, :, 1, :], ALU.add).then_inc(self.both_done, 1)
        V.tensor_scalar_max(self.clamped[:], top[:], -87.0).then_inc(self.top_clamped, 1)

    def count(self, pe, at):
        nc, both, ones = self.nc, self.both, self.w["ones"]
        pe.wait_ge(self.both_done, at.u + 1)
        pe.wait_ge(self.count_done, at.u)
        nc.tensor.matmul(self.ahead_ps, self.w["below"][:], both[:], start=True, stop=False)
        for i in range(NT - 1):
            nc.tensor.matmul(self.ahead_ps[:, i + 1:, :], ones[:],
                             both[:, i:i + 1, :].to_broadcast([P, NT - 1 - i, E]), start=False, stop=(i == NT - 2))
        for i in range(NT):
            last = nc.tensor.matmul(self.total_ps, ones[:], both[:, i, :], start=(i == 0), stop=(i == NT - 1))
        last.then_inc(self.ahead_done, 1)

    def positions(self, dve, at):
        V, r = self.nc.vector, self.r
        dve.wait_ge(self.ahead_done, at.u + 1)
        V.tensor_tensor(self.place[:], self.ahead_ps, r["count"][:].unsqueeze(1).to_broadcast([P, NT, E]),
                        ALU.add).then_inc(self.position, 1)
        dve.wait_ge(self.position, at.u * 3 + 1)
        V.tensor_tensor(r["count"][:], r["count"][:], self.total_ps, ALU.add).then_inc(self.count_done, 1)
        V.tensor_tensor(self.mine[:], self.chosen[:], self.place[:].unsqueeze(2).to_broadcast([P, NT, 2, E]),
                        ALU.mult).then_inc(self.position, 1)
        dve.wait_ge(self.position, at.u * 3 + 2)
        V.tensor_reduce(self.spot[:], self.mine[:], AX_X, ALU.add).then_inc(self.position, 1)
        dve.wait_ge(self.position, at.u * 3 + 3)
        V.tensor_copy(r["sent"][:, bass.ds(at.u * NT, NT), :], self.spot[:])
        dve.wait_ge(self.scattered[at.par], 16 * 2 * NT * at.pair)
        V.tensor_copy(self.at_now[at.par][:], self.spot[:]).then_inc(self.at_done, 1)

    def exponent(self, act, at):
        act.wait_ge(self.top_clamped, at.u + 1)
        self.nc.scalar.activation(self.power[:], self.clamped[:], ACT.Exp, scale=-1.0).then_inc(self.power_done, 1)

    def gates(self, dve, at):
        V = self.nc.vector
        dve.wait_ge(self.power_done, at.u + 1)
        V.tensor_scalar_add(self.sigma[:], self.power[:], 1.0).then_inc(self.gating, 1)
        dve.wait_ge(self.gating, at.u * 5 + 1)
        V.reciprocal(self.power[:], self.sigma[:]).then_inc(self.gating, 1)
        dve.wait_ge(self.gating, at.u * 5 + 2)
        V.tensor_tensor(self.gate_sum[:], self.power[:, :, 0:1], self.power[:, :, 1:2],
                        ALU.add).then_inc(self.gating, 1)
        dve.wait_ge(self.gating, at.u * 5 + 3)
        V.tensor_scalar(self.twice[:], self.gate_sum[:], 1e-10, 2.0, ALU.add, ALU.mult).then_inc(self.gating, 1)
        dve.wait_ge(self.gating, at.u * 5 + 4)
        V.reciprocal(self.gate_sum[:], self.twice[:]).then_inc(self.gating, 1)
        dve.wait_ge(self.gating, at.u * 5 + 5)
        V.tensor_tensor(self.r["gate"][:, bass.ds(at.u * NT, NT), :], self.power[:],
                        self.gate_sum[:].to_broadcast([P, NT, 2]), ALU.mult)

    def scatter(self, pool, at):
        pool.wait_ge(self.at_done, at.u + 1)
        pool.sem_inc(self.scattering, 1)
        for i in range(NT):
            for j in range(2):
                self.nc.gpsimd.indirect_dma_start(
                    self.slots["x"], bass.IndirectOffsetOnAxis(ap=self.at_now[at.par][:, i, j:j + 1], axis=0),
                    self.norm.xn[at.par][:, i, :], None).then_inc(self.scattered[at.par], 16)


def route_stage(nc, name, src, const, w, r, slots):
    with ExitStack() as ctx:
        ps = lambda n, s: ctx.enter_context(nc.psum_tensor(f"{name}_{n}", s, F32))
        norm = Norm(nc, ctx, f"{name}_norm", src, const, ps("xt_ps", [P, T]))
        router = Router(nc, ctx, name, norm, w, r, slots, ps("logit_ps", [P, NT, E])[:],
                        ps("ahead_ps", [P, NT, E])[:], ps("total_ps", [P, E])[:])
        with nc.Block() as block:
            @block.sync
            def _(sp):
                def iteration(t):
                    if at := t.after(2):
                        norm.load(sp, at, norm.xn_done)

                skewed(sp, iteration, lead=2)

            @block.gpsimd
            def _(pool):
                def iteration(t):
                    if at := t.after(1):
                        norm.root(pool, at)
                    if at := t.after(0):
                        router.scatter(pool, at)

                skewed(pool, iteration, lead=1)

            @block.tensor
            def _(pe):
                def iteration(t):
                    if at := t.after(0):
                        router.logits(pe, at)
                        router.count(pe, at)
                    if at := t.after(1):
                        norm.transpose(pe, at)

                skewed(pe, iteration, lead=1)

            @block.scalar
            def _(act):
                def iteration(t):
                    if at := t.after(0):
                        router.exponent(act, at)
                    if at := t.after(1):
                        router.copy_xt(act, at)

                skewed(act, iteration, lead=1)

            @block.vector
            def _(dve):
                def iteration(t):
                    if at := t.after(1):
                        norm.statistics(dve, at)
                    if at := t.after(0):
                        router.choose(dve, at)
                        router.positions(dve, at)
                        router.gates(dve, at)
                    if at := t.after(1):
                        router.normalise(dve, at)

                router.begin(dve)
                skewed(dve, iteration, lead=1)


def finish_routes(nc, ctx, name, w, r, slots, w_gate, w_up, w_down):
    sb = lambda n, s, d=F32: ctx.enter_context(nc.sbuf_tensor(f"{name}_{n}", s, d))
    experts = dict(hi=sb("hi", [P, E, 2 * HID], F32R), lo=sb("lo", [P, E, 2 * HID], F32R),
                   down=sb("down", [P, 2 * E, D]))
    scattered, padded = slots["scattered"], slots["padded"]
    CHUNKS = 4
    with ExitStack() as inner:
        sb = lambda n, s, d=F32: inner.enter_context(nc.sbuf_tensor(f"{name}_{n}", s, d))
        sem = lambda n: inner.enter_context(nc.semaphore(f"{name}_{n}"))
        plain = sb("plain", [P, E, 2 * HID])
        loaded, hi_done, pads_ready, step, down_loaded = [[sem(f"loaded{k}") for k in range(CHUNKS)]] + [
            sem(n) for n in ("hi_done", "pads_ready", "step", "down_loaded")]
        pad, pad_at = sb("pad", [P, E]), sb("pad_at", [P, E], U32)
        filled, tiles, jump, ends = [sb(n, [P, E]) for n in ("filled", "tiles", "jump", "ends")]
        full, whole = sb("full", [P, E], I32), sb("whole", [P, E], I32)
        tile, summed = sb("tile", [P, TILES]), sb("summed", [P, TILES])
        behind, jumped = [sb(n, [P, TILES, E - 1]) for n in ("behind", "jumped")]
        passed, skipped = [sb(n, [P, B * NT * 2, E - 1]) for n in ("passed", "skipped")]
        rests = sb("rests", [P, B * NT * 2])

        def chunk(k):
            return slice(k * E // CHUNKS, (k + 1) * E // CHUNKS)

        with nc.Block() as block:
            @block.sync
            def _(sp):
                for k in range(CHUNKS):
                    for side, source in enumerate((w_gate, w_up)):
                        sp.dma_start(plain[:, chunk(k), side * HID:(side + 1) * HID],
                                     source[chunk(k)].rearrange("e d h -> d e h")).then_inc(loaded[k], 16)
                sp.dma_start(experts["down"][:], w_down.rearrange("e (c p) d -> p (e c) d", p=P)).then_inc(
                    down_loaded, 16)
                sp.wait_ge(down_loaded, 16)

            @block.gpsimd
            def _(pool):
                pool.wait_ge(pads_ready, 1)
                for e in range(E):
                    nc.gpsimd.indirect_dma_start(slots["x"], bass.IndirectOffsetOnAxis(ap=pad_at[:, e:e + 1], axis=0),
                                                 w["zero"][:], None).then_inc(padded, 16)
                pool.wait_ge(padded, 16 * E)
                for par in range(2):
                    pool.wait_ge(scattered[par], 16 * 2 * NT * (B // 2))

            @block.scalar
            def _(act):
                for k in range(CHUNKS):
                    act.wait_ge(loaded[k], 2 * 16)
                    nc.scalar.copy(experts["hi"][:, chunk(k), :], plain[:, chunk(k), :]).then_inc(hi_done, 1)

            @block.vector
            def _(dve):
                V = nc.vector
                done = [0]

                def then(ins):
                    done[0] += 1
                    ins.then_inc(step, 1)
                    dve.wait_ge(step, done[0])

                then(V.tensor_tensor(pad[:], r["count"][:], w["row"][:], ALU.add))
                V.tensor_copy(pad_at[:], pad[:]).then_inc(pads_ready, 1)
                then(V.tensor_tensor(filled[:], r["count"][:], w["base"][:], ALU.subtract))
                then(V.tensor_scalar_add(filled[:], filled[:], float(P - 1)))
                then(V.tensor_copy(full[:], filled[:]))
                then(V.tensor_scalar(whole[:], full[:], P.bit_length() - 1, None, ALU.logical_shift_right))
                then(V.tensor_copy(tiles[:], whole[:]))
                for e in range(E):
                    last = V.tensor_reduce(ends[:, e:e + 1], tiles[:, 0:e + 1], AX_X, ALU.add)
                then(last)
                then(V.tensor_scalar(jump[:], tiles[:], -float(P), float(REGION), ALU.mult, ALU.add))
                then(V.tensor_scalar(tile[:], w["tile"][:], 1.0, ends[:, E - 1:E], ALU.add, ALU.min))
                then(V.tensor_scalar_add(tile[:], tile[:], -1.0))
                then(V.tensor_tensor(behind[:], tile[:].unsqueeze(2).to_broadcast([P, TILES, E - 1]),
                                     ends[:, 0:E - 1].unsqueeze(1).to_broadcast([P, TILES, E - 1]), ALU.is_ge))
                then(V.tensor_tensor(jumped[:], behind[:], jump[:, 0:E - 1].unsqueeze(1).to_broadcast([P, TILES, E - 1]),
                                     ALU.mult))
                then(V.tensor_reduce(summed[:], jumped[:], AX_X, ALU.add))
                then(V.scalar_tensor_tensor(tile[:], tile[:], float(P), summed[:], ALU.mult, ALU.add))
                V.tensor_copy(r["start"][:], tile[0:1, :])
                then(V.tensor_reduce(summed[:], behind[:], AX_X, ALU.add))
                V.tensor_copy(r["expert"][:], summed[0:1, :])
                wide = [P, B * NT * 2, E - 1]
                sent = r["sent"][:].rearrange("p i j -> p (i j)")
                then(V.tensor_tensor(passed[:], sent.unsqueeze(2).to_broadcast(wide),
                                     w["base"][:, 1:].unsqueeze(1).to_broadcast(wide), ALU.is_ge))
                then(V.tensor_tensor(skipped[:], passed[:], jump[:, 0:E - 1].unsqueeze(1).to_broadcast(wide), ALU.mult))
                then(V.tensor_reduce(rests[:], skipped[:], AX_X, ALU.add))
                V.tensor_tensor(r["at"][:].rearrange("p i j -> p (i j)"), sent, rests[:], ALU.subtract)
                for k in range(CHUNKS):
                    dve.wait_ge(hi_done, k + 1)
                    V.tensor_tensor(experts["lo"][:, chunk(k), :], plain[:, chunk(k), :],
                                    experts["hi"][:, chunk(k), :].bitcast(F32), ALU.subtract)
    return experts


def expert_stage(nc, name, const, w, r, slots):
    WAYS = 4
    with ExitStack() as ctx:
        sb = lambda n, s, d=F32: ctx.enter_context(nc.sbuf_tensor(f"{name}_{n}", s, d))
        ps = lambda n, s: ctx.enter_context(nc.psum_tensor(f"{name}_{n}", s, F32))
        sem = lambda n: ctx.enter_context(nc.semaphore(f"{name}_{n}"))
        x = [sb(f"x{k}", [P, D]) for k in range(WAYS)]
        hi = [sb(f"hi{k}", [P, P], F32R) for k in range(2)]
        lo = [sb(f"lo{k}", [P, P], F32R) for k in range(2)]
        silu = [sb(f"silu{k}", [P, HID]) for k in range(2)]
        h = [sb(f"h{k}", [P, 2, P]) for k in range(2)]
        ht = [sb(f"ht{k}", [P, 2, P]) for k in range(2)]
        y = [sb(f"y{k}", [P, 2, D]) for k in range(2)]
        xt_ps = [ps(f"xt_ps{k}", [P, P]) for k in range(2)]
        up_ps = [ps(f"up_ps{k}", [P, 2 * HID]) for k in range(2)]
        ht_ps = [ps(f"ht_ps{k}", [P, 2, P]) for k in range(2)]
        y_ps = [ps(f"y_ps{k}", [P, D]) for k in range(2)]
        x_loaded = [sem(f"x_loaded{k}") for k in range(WAYS)]
        y_stored = [sem(f"y_stored{k}") for k in range(2)]
        xt_done, hi_done, lo_done, up_done, silu_done, h_done, ht_done, ht_copied, y_done, y_copied = [
            sem(n) for n in ("xt_done", "hi_done", "lo_done", "up_done", "silu_done", "h_done", "ht_done",
                             "ht_copied", "y_done", "y_copied")]

        with nc.Block() as block:
            @block.sync
            def _(sp):
                def iteration(t):
                    if at := t.after(4):
                        if t.after(0):
                            sp.wait_ge(xt_done, t.u + 1)
                        row = sp.value_load(r["start"][0:1, bass.ds(at.u, 1)], min_val=0, max_val=X_ROWS - P)
                        sp.dma_start(x[at.par][:], slots["x"][bass.ds(row, P), :]).then_inc(x_loaded[at.par], 16)
                    if t.par % 2 and (at := t.after(-3)):
                        sp.wait_ge(y_copied, at.u + 2)
                        sp.dma_start(slots["y"][bass.ds(at.u * P, 2 * P), :].rearrange("(k p) d -> p k d", p=P),
                                     y[at.par // 2][:]).then_inc(y_stored[at.par // 2], 16)

                skewed(sp, iteration, lead=4, lag=4, n=TILES, ways=WAYS)
                for k in range(2):
                    sp.wait_ge(y_stored[k], 16 * TILES // WAYS)

            @block.tensor
            def _(pe):
                expert_of = [pe.alloc_register(f"{name}_expert{k}") for k in range(WAYS)]

                def iteration(t):
                    if at := t.after(0):
                        expert = pe.snap(expert_of[at.par], min_val=0, max_val=E - 1)
                        pe.wait_ge(lo_done, at.u + 1)
                        if t.after(-2):
                            pe.wait_ge(h_done, at.u - 1)
                        k = at.par % 2
                        one = bass.ds(expert, 1)
                        nc.tensor.matmul(up_ps[k][:], hi[k][:], w["hi"][:, one, :], start=True, stop=False)
                        nc.tensor.matmul(up_ps[k][:], lo[k][:], w["hi"][:, one, :], start=False, stop=False)
                        nc.tensor.matmul(up_ps[k][:], hi[k][:], w["lo"][:, one, :], start=False,
                                         stop=True).then_inc(up_done, 1)
                    if at := t.after(1):
                        pe.reg_load(expert_of[at.par], r["expert"][0:1, bass.ds(at.u, 1)])
                    if at := t.after(-1):
                        pe.wait_ge(h_done, at.u + 1)
                        for c in range(2):
                            last = nc.tensor.transpose(ht_ps[at.par % 2][:, c, :], h[at.par % 2][:, c, :],
                                                       const["ident"][:])
                        last.then_inc(ht_done, 1)
                    if at := t.after(2):
                        pe.wait_ge(x_loaded[at.par], 16 * (at.pair + 1))
                        nc.tensor.transpose(xt_ps[at.par % 2][:], x[at.par][:], const["ident"][:]).then_inc(xt_done, 1)
                    if at := t.after(-2):
                        expert = pe.snap(expert_of[at.par], min_val=0, max_val=E - 1)
                        pe.wait_ge(ht_copied, at.u + 1)
                        if at.after(-2):
                            pe.wait_ge(y_copied, at.u - 1)
                        for c in range(2):
                            last = nc.tensor.matmul(y_ps[at.par % 2][:], ht[at.par % 2][:, c, :],
                                                    w["down"][:, bass.ds(expert * 2 + c, 1), :],
                                                    start=(c == 0), stop=(c == 1))
                        last.then_inc(y_done, 1)

                skewed(pe, iteration, lead=2, lag=2, n=TILES, ways=WAYS)

            @block.scalar
            def _(act):
                def iteration(t):
                    if at := t.after(0):
                        act.wait_ge(up_done, at.u + 1)
                        if t.after(-2):
                            act.wait_ge(h_done, at.u - 1)
                        nc.scalar.activation(silu[at.par % 2][:], up_ps[at.par % 2][:, 0:HID],
                                             ACT.Silu).then_inc(silu_done, 1)
                    if at := t.after(-1):
                        act.wait_ge(ht_done, at.u + 1)
                        if at.after(-2):
                            act.wait_ge(y_done, at.u - 1)
                        nc.scalar.copy(ht[at.par % 2][:], ht_ps[at.par % 2][:]).then_inc(ht_copied, 1)
                    if at := t.after(2):
                        act.wait_ge(xt_done, at.u + 1)
                        nc.scalar.copy(hi[at.par % 2][:], xt_ps[at.par % 2][:]).then_inc(hi_done, 1)

                skewed(act, iteration, lead=2, lag=1, n=TILES, ways=WAYS)

            @block.vector
            def _(dve):
                def iteration(t):
                    if at := t.after(0):
                        dve.wait_ge(silu_done, at.u + 1)
                        if t.after(-2):
                            dve.wait_ge(ht_done, at.u - 1)
                        nc.vector.tensor_tensor(h[at.par % 2][:], silu[at.par % 2][:].rearrange("p (c h) -> p c h", c=2),
                                                up_ps[at.par % 2][:, HID:].rearrange("p (c h) -> p c h", c=2),
                                                ALU.mult).then_inc(h_done, 1)
                    if at := t.after(2):
                        dve.wait_ge(hi_done, at.u + 1)
                        nc.vector.tensor_tensor(lo[at.par % 2][:], xt_ps[at.par % 2][:], hi[at.par % 2][:].bitcast(F32),
                                                ALU.subtract).then_inc(lo_done, 1)
                    if at := t.after(-2):
                        dve.wait_ge(y_done, at.u + 1)
                        dve.wait_ge(y_stored[at.par // 2], 16 * at.pair)
                        nc.vector.tensor_copy(y[at.par // 2][:, at.par % 2, :], y_ps[at.par % 2][:]).then_inc(y_copied, 1)

                skewed(dve, iteration, lead=2, lag=2, n=TILES, ways=WAYS)




class Combined(Norm):

    def __init__(self, nc, ctx, name, src, const, xt_ps, r, slots):
        super().__init__(nc, ctx, name, src, const, xt_ps)
        sb = lambda n, s, d=F32: ctx.enter_context(nc.sbuf_tensor(f"{name}_{n}", s, d))
        sem = lambda n: ctx.enter_context(nc.semaphore(f"{name}_{n}"))
        self.r, self.slots, self.gathered = r, slots, slots["gathered"]
        self.before = [sb(f"before{k}", [P, NT, D]) for k in range(2)]
        self.result = [sb(f"result{k}", [P, NT, 2, D]) for k in range(2)]
        self.gate = [sb(f"gate{k}", [P, NT, 2]) for k in range(2)]
        self.place = [sb(f"place{k}", [P, NT, 2], U32) for k in range(2)]
        self.taken, self.half_combined, self.gathering = sem("taken"), sem("half_combined"), sem("gathering")
        self.combined = [sem(f"combined{k}") for k in range(2)]

    def load(self, sp, at):
        u, pair, par = at.u, at.pair, at.par
        sp.wait_ge(self.combined[par], pair)
        src = self.src.rearrange("b (i p) d -> b p i d", p=P)
        sp.dma_start(self.before[par][:], src[u]).then_inc(self.x_loaded[par], 16)

    def take(self, dve, at):
        nc, u, pair, par = self.nc, at.u, at.pair, at.par
        dve.wait_ge(self.gathered[par], 16 * 2 * NT * pair)
        dve.wait_ge(self.combined[par], pair)
        nc.vector.tensor_copy(self.gate[par][:], self.r["gate"][:, bass.ds(u * NT, NT), :])
        nc.vector.tensor_copy(self.place[par][:], self.r["at"][:, bass.ds(u * NT, NT), :]).then_inc(self.taken, 1)

    def gather(self, pool, at):
        nc, u, pair, par = self.nc, at.u, at.pair, at.par
        pool.wait_ge(self.taken, u + 1)
        pool.wait_ge(self.combined[par], pair)
        pool.sem_inc(self.gathering, 1)
        for i in range(NT):
            for j in range(2):
                nc.gpsimd.indirect_dma_start(
                    self.result[par][:, i, j, :], None, self.slots["y"],
                    bass.IndirectOffsetOnAxis(ap=self.place[par][:, i, j:j + 1], axis=0)).then_inc(
                        self.gathered[par], 16)

    def combine(self, dve, at, x_free, step):
        nc, u, pair, par = self.nc, at.u, at.pair, at.par
        dve.wait_ge(self.x_loaded[par], 16 * (pair + 1))
        dve.wait_ge(self.gathered[par], 16 * 2 * NT * (pair + 1))
        for i in range(NT):
            last = nc.vector.scalar_tensor_tensor(self.before[par][:, i, :], self.result[par][:, i, 0, :],
                                                  self.gate[par][:, i, 0:1], self.before[par][:, i, :],
                                                  ALU.mult, ALU.add)
        last.then_inc(self.half_combined, 1)
        dve.wait_ge(self.half_combined, u + 1)
        dve.wait_ge(x_free[par], step * pair)
        for i in range(NT):
            last = nc.vector.scalar_tensor_tensor(self.x[par][:, i, :], self.result[par][:, i, 1, :],
                                                  self.gate[par][:, i, 1:2], self.before[par][:, i, :],
                                                  ALU.mult, ALU.add)
        last.then_inc(self.combined[par], 1)

    def wait_for_x(self, dve, at):
        dve.wait_ge(self.combined[at.par], at.pair + 1)


def macaron_kernel(nc, x, w_qk, w_v, w_out, b_out, cos, sin, router, w_gate, w_up, w_down, w_causal, b_causal,
                   u1, v1, b1, u2, v2, b2, out):
    dram = lambda n, s: nc.dram_tensor(n, s, F32).ap()
    between = [dram(f"between{k}", [B, T, D]) for k in range(4)]

    def make_slots(name):
        sem = lambda n: whole.enter_context(nc.semaphore(f"{name}_{n}"))
        return dict(x=dram(f"{name}_sorted_x", [X_ROWS, D]), y=dram(f"{name}_sorted_y", [Y_ROWS, D]),
                    scattered=[sem(f"scattered{k}") for k in range(2)], padded=sem("padded"),
                    gathered=[sem(f"gathered{k}") for k in range(2)])

    def run_experts(name, r, slots):
        with ExitStack() as ctx:
            w = finish_routes(nc, ctx, f"{name}_finish", w_route, r, slots, w_gate, w_up, w_down)
            expert_stage(nc, f"{name}_expert", const, w, r, slots)

    with ExitStack() as whole:
        const = make_constants(nc, whole)
        w_route = make_route_constants(nc, whole, router)
        slots_a, slots_b = make_slots("moe_a"), make_slots("moe_b")
        r_b = make_tables(nc, whole, "moe_b_tables")
        with ExitStack() as first:
            r_a = make_tables(nc, first, "moe_a_tables")
            route_stage(nc, "route_a", x, const, w_route, r_a, slots_a)
            run_experts("moe_a", r_a, slots_a)
            w = load_heads_weights(nc, first, w_qk, w_v, w_out, b_out, cos, sin)
            heads_stage(nc, "heads", x, between[0], between[1], const, w, r_a, slots_a, w_route, r_b, slots_b)
        clear_semaphores(nc)
        run_experts("moe_b", r_b, slots_b)
        w_ffn = load_ffn_weights(nc, whole, u1, v1, b1, u2, v2, b2)
        ffn_stage(nc, "ffn_a", between[1], between[2], const, w_ffn, (r_b, slots_b))
        clear_semaphores(nc)
        with ExitStack() as ctx:
            w = load_causal_weights(nc, ctx, w_causal, b_causal)
            causal_stage(nc, "causal", between[2], between[3], const, w)
        ffn_stage(nc, "ffn_b", between[3], out, const, w_ffn)


HEADS, D_HEAD = 16, 8


def _rope_tables():
    import numpy as np
    theta = (1.0 / np.float32(10000.0) ** (np.arange(0, D_HEAD, 2, dtype=np.float32) / np.float32(D_HEAD))).astype(np.float32)
    angles = np.outer(np.arange(T, dtype=np.float32), theta)
    angles = np.concatenate([angles, angles], axis=-1)
    sign = np.where(np.arange(D_HEAD) < D_HEAD // 2, -1, 1).astype(np.float32)
    rows = lambda tab: np.ascontiguousarray(np.broadcast_to(tab.T[None, :, None, :], (2, D_HEAD, HEADS // 2, T)).reshape(D, T))
    return rows(np.cos(angles).astype(np.float32)), rows(np.sin(angles).astype(np.float32) * sign)


def kernel(**inputs):
    import numpy as np
    import concourse.bacc as _bacc
    from concourse.bass_utils import run_bass_kernel_spmd as _run

    given = {k: np.asarray(v) for k, v in inputs.items()}
    w_qkv = given["L0_attn_w_qkv"]
    cos, sin = _rope_tables()
    laid = dict(
        x=given["L0_attn_x"],
        w_qk=w_qkv[:, :2 * D].reshape(D, 2, HEADS // 2, 2, D_HEAD).transpose(0, 1, 3, 4, 2).reshape(D, 2, D),
        w_v=w_qkv[:, 2 * D:], w_out=given["L0_attn_w_out"], b_out=given["L0_attn_b_out"], cos=cos, sin=sin,
        router=given["L0_ffn_router_w"].T, w_gate=given["L0_ffn_w_gate"], w_up=given["L0_ffn_w_up"],
        w_down=given["L0_ffn_w_down"], w_causal=given["L1_attn_W"], b_causal=given["L1_attn_b"],
        u1=given["L1_ffn_U1"], v1=given["L1_ffn_V1"], b1=given["L1_ffn_b1"], u2=given["L1_ffn_U2"],
        v2=given["L1_ffn_V2"], b2=given["L1_ffn_b2"])
    nc = _bacc.Bacc("TRN2", target_bir_lowering=False, num_devices=1)
    arrays, args = {}, []
    for name, a in laid.items():
        a = np.ascontiguousarray(a)
        arrays[f"in_{name}_dram"] = a
        args.append(nc.dram_tensor(f"in_{name}_dram", a.shape, mybir.dt.from_np(a.dtype), kind="ExternalInput").ap())
    args.append(nc.dram_tensor("out_0_dram", (B, T, D), F32, kind="ExternalOutput").ap())
    macaron_kernel(nc, *args)
    r = _run(nc, [arrays], core_ids=[0])
    return r.results[0]["out_0_dram"]
```

```python
from contextlib import ExitStack

import concourse.bass as bass
from concourse import mybir

F32 = mybir.dt.float32
F32R = mybir.dt.float32r
I32 = mybir.dt.int32
U32 = mybir.dt.uint32
ALU = mybir.AluOpType
ACT = mybir.ActivationFunctionType
AX_X = mybir.AxisListType.X

P = 128
B, T, D = 8, 512, 128
NT = T // P
EPS = 1e-5


class Norm:

    def __init__(self, nc, ctx, name, src, const, xt_ps, x=None):
        self.nc, self.src, self.const, self.xt_ps = nc, src, const, xt_ps
        sb = lambda n, s, d=F32: ctx.enter_context(nc.sbuf_tensor(f"{name}_{n}", s, d))
        sem = lambda n: ctx.enter_context(nc.semaphore(f"{name}_{n}"))
        self.x = x or [sb(f"x{k}", [P, NT, D]) for k in range(2)]
        self.xn = [sb(f"xn{k}", [P, NT, D]) for k in range(2)]
        self.stats = [sb(f"stats{k}", [P, NT, 6]) for k in range(2)]
        self.mv = [sb(f"mv{k}", [P, NT, 2]) for k in range(2)]
        self.var = [sb(f"var{k}", [P, NT]) for k in range(2)]
        self.rstd = [sb(f"rstd{k}", [P, NT]) for k in range(2)]
        self.x_loaded = [sem(f"x_loaded{k}") for k in range(2)]
        self.stats_done = sem("stats_done")
        self.aggregating = sem("aggregating")
        self.var_done = sem("var_done")
        self.eps_added = sem("eps_added")
        self.rstd_done = sem("rstd_done")
        self.xn_done = [sem(f"xn_done{k}") for k in range(2)]
        self.xt_done = [sem(f"xt_done{k}") for k in range(2)]

    def load(self, sp, at, x_free):
        u, pair, par = at.u, at.pair, at.par
        sp.wait_ge(x_free[par], pair)
        src = self.src.rearrange("b (i p) d -> b p i d", p=P)
        sp.dma_start(self.x[par][:], src[u]).then_inc(self.x_loaded[par], 16)

    def wait_for_x(self, dve, at):
        dve.wait_ge(self.x_loaded[at.par], 16 * (at.pair + 1))

    def statistics(self, dve, at):
        nc, u, pair, par = self.nc, at.u, at.pair, at.par
        self.wait_for_x(dve, at)
        for i in range(NT):
            last = nc.vector.bn_stats(self.stats[par][:, i, :], self.x[par][:, i, :])
        last.then_inc(self.stats_done, 1)
        dve.wait_ge(self.stats_done, u + 1)
        dve.sem_inc(self.aggregating, 1)
        for i in range(NT):
            last = nc.vector.bn_aggr(self.mv[par][:, i, :], self.stats[par][:, i, :])
        last.then_inc(self.var_done, 1)

    def root(self, pool, at):
        nc, u, pair, par = self.nc, at.u, at.pair, at.par
        pool.wait_ge(self.var_done, u + 1)
        nc.gpsimd.tensor_tensor(self.var[par][:], self.mv[par][:, :, 1], self.const["eps"][:, 0:NT],
                                ALU.add).then_inc(self.eps_added, 1)
        pool.wait_ge(self.eps_added, u + 1)
        nc.gpsimd.tensor_tensor(self.rstd[par][:], self.var[par][:], self.const["minus_half"][:, 0:NT],
                                ALU.pow).then_inc(self.rstd_done, 1)

    def normalise(self, dve, at):
        nc, u, pair, par = self.nc, at.u, at.pair, at.par
        dve.wait_ge(self.rstd_done, u + 1)
        dve.wait_ge(self.xt_done[par], pair)
        for i in range(NT):
            last = nc.vector.tensor_scalar(self.xn[par][:, i, :], self.x[par][:, i, :],
                                           self.mv[par][:, i, 0:1], self.rstd[par][:, i:i + 1],
                                           ALU.subtract, ALU.mult)
        last.then_inc(self.xn_done[par], 1)

    def transpose(self, pe, at):
        nc, u, pair, par = self.nc, at.u, at.pair, at.par
        pe.wait_ge(self.xn_done[par], pair + 1)
        for i in range(NT):
            last = nc.tensor.transpose(self.xt_ps[:, i * P:(i + 1) * P], self.xn[par][:, i, :],
                                       self.const["ident"][:])
        last.then_inc(self.xt_done[par], 1)


class Unit:

    def __init__(self, pair, par, n, ways=2):
        self.pair, self.par, self.n, self.ways, self.u = pair, par, n, ways, pair * ways + par

    def after(self, k):
        pair, par = self.pair + (self.par + k) // self.ways, (self.par + k) % self.ways
        if isinstance(pair, int) and not 0 <= pair < self.n // self.ways:
            return None
        return Unit(pair, par, self.n, self.ways)


def skewed(engine, iteration, lead, lag=0, n=B, ways=2):
    first, last = max((lag + ways - 1) // ways, 1), (n - lead) // ways
    for t in range(-lead, ways * first):
        iteration(Unit(t // ways, t % ways, n, ways))
    with engine.Fori(first, last) as pair:
        for k in range(ways):
            iteration(Unit(pair, k, n, ways))
    for t in range(ways * last, n + lag):
        iteration(Unit(t // ways, t % ways, n, ways))



def clearing(nc, cleared):
    given_back = sorted(set(nc.released_uncleared_semaphores) - cleared)
    cleared.update(given_back)

    def clear(pool):
        first = given_back[0]
        for number, following in zip(given_back, given_back[1:] + [None]):
            if following != number + 1:
                pool.sem_clear(range(first, number + 1))
                first = following

    return clear


def make_constants(nc, ctx):
    sb = lambda n, s, d=F32: ctx.enter_context(nc.sbuf_tensor(n, s, d))
    const = dict(eps=sb("eps", [P, 8]), minus_half=sb("minus_half", [P, 8]), ident=sb("ident", [P, P]))
    zeroed = ctx.enter_context(nc.semaphore("ident_zeroed"))
    with nc.Block() as block:
        @block.gpsimd
        def _(pool):
            nc.gpsimd.memset(const["eps"][:], EPS)
            nc.gpsimd.memset(const["minus_half"][:], -0.5)
            nc.gpsimd.memset(const["ident"][:], 0.0).then_inc(zeroed, 1)
            pool.wait_ge(zeroed, 1)
            nc.gpsimd.affine_select(out=const["ident"][:], in_=const["ident"][:], compare_op=ALU.not_equal,
                                    fill=1.0, base=0, pattern=[[-1, P]], channel_multiplier=1)
    return const


R = 32
FF = 512
FC = FF // P


def make_ffn_weights(nc, ctx, U1, V1, b1, U2, V2, b2):
    sb = lambda n, s, d=F32: ctx.enter_context(nc.sbuf_tensor(f"ffn_{n}", s, d))
    w = dict(u1=sb("u1", [P, 4, R]), v1=sb("v1", [P, FF]), v1_hi=sb("v1_hi", [P, FF], F32R),
             v1_stack=sb("v1_stack", [P, FF], F32R), b1=sb("b1", [P, FC]), u2=sb("u2", [P, FC, R]),
             v2=sb("v2", [P, D]), v2_half=sb("v2_half", [P, D]), b2=sb("b2", [P, D]),
             b2_half=sb("b2_half", [P, D]))
    loaded = ctx.enter_context(nc.semaphore("ffn_weights_loaded"))
    split = ctx.enter_context(nc.semaphore("ffn_v1_split"))

    def load(pool):
        for g in range(4):
            pool.dma_start(w["u1"][:, g, :], U1).then_inc(loaded, 16)
            pool.dma_start(w["v1"][g * R:(g + 1) * R, :], V1).then_inc(loaded, 16)
            pool.dma_start(w["v2"][g * R:(g + 1) * R, :], V2).then_inc(loaded, 16)
        pool.dma_start(w["b1"][:], b1.rearrange("(c p) -> p c", p=P),
                       allow_slow_non_contiguous=True).then_inc(loaded, 16)
        pool.dma_start(w["u2"][:], U2.rearrange("(c p) r -> p c r", p=P)).then_inc(loaded, 16)
        pool.dma_start(w["b2"][:], b2.partition_broadcast(P)).then_inc(loaded, 16)
        pool.wait_ge(loaded, 15 * 16)
        nc.gpsimd.tensor_scalar_mul(w["v2_half"][:], w["v2"][:], 0.5).then_inc(split, 1)
        pool.wait_ge(split, 1)
        nc.gpsimd.tensor_scalar_mul(w["b2_half"][:], w["b2"][:], 0.5).then_inc(split, 1)
        pool.wait_ge(split, 2)
        nc.gpsimd.tensor_copy(w["v1_hi"][:], w["v1"][:]).then_inc(split, 1)
        pool.wait_ge(split, 3)
        for g in range(4):
            rows = slice(g * R, (g + 1) * R)
            if g % 2:
                last = nc.gpsimd.tensor_tensor(w["v1_stack"][rows, :], w["v1"][rows, :],
                                               w["v1_hi"][rows, :].bitcast(F32), ALU.subtract)
            else:
                last = nc.gpsimd.tensor_copy(w["v1_stack"][rows, :], w["v1"][rows, :])
            last.then_inc(split, 1)
            pool.wait_ge(split, 4 + g)

    return w, load


def ffn_stage(nc, name, src, dst, const, w, routed=None):
    with ExitStack() as ctx:
        sb = lambda n, s, d=F32: ctx.enter_context(nc.sbuf_tensor(f"{name}_{n}", s, d))
        ps = lambda n, s: ctx.enter_context(nc.psum_tensor(f"{name}_{n}", s, F32))
        sem = lambda n: ctx.enter_context(nc.semaphore(f"{name}_{n}"))
        xt_ps = ps("xt_ps", [P, T])
        norm = Combined(nc, ctx, name, src, const, xt_ps, *routed) if routed else \
            Norm(nc, ctx, name, src, const, xt_ps)
        xt = [sb(f"xt{k}", [P, T]) for k in range(2)]
        xb = [sb(f"xb{k}", [P, NT, D]) for k in range(2)]
        rank = [sb(f"rank{k}", [P, T], F32R) for k in range(2)]
        hid = [sb(f"hid{c}", [P, T]) for c in range(FC)]
        low = [sb(f"low{k}", [P, T]) for k in range(2)]
        y = [sb(f"y{k}", [P, NT, D]) for k in range(2)]
        rank_ps = ps("rank_ps", [P, T])
        hid_ps = [ps(f"hid_ps{c}", [P, T]) for c in range(FC)]
        low_ps = ps("low_ps", [P, T])
        out_ps = ps("out_ps", [P, NT, D])
        xt_copied, rank_done, rank_hi, rank_lo = [sem(n) for n in ("xt_copied", "rank_done", "rank_hi", "rank_lo")]
        hid_done, gelu_done, low_done, low_copied = [sem(n) for n in ("hid_done", "gelu_done", "low_done", "low_copied")]
        out_done = sem("out_done")
        xb_done = [sem(f"xb_done{k}") for k in range(2)]
        y_done = [sem(f"y_done{k}") for k in range(2)]
        y_stored = [sem(f"y_stored{k}") for k in range(2)]

        xb_loaded = [sem(f"xb_loaded{k}") for k in range(2)]
        bias = w["b2_half"][:].unsqueeze(1).to_broadcast([P, NT, D])
        src_v = src.rearrange("b (i p) d -> b p i d", p=P)
        dst_v = dst.rearrange("b (i p) d -> b p i d", p=P)

        with nc.Block() as block:
            @block.sync
            def _(sp):
                def iteration(t):
                    if at := t.after(3):
                        if routed:
                            norm.load(sp, at)
                        else:
                            norm.load(sp, at, norm.xn_done)
                    if not routed and (at := t.after(1)):
                        sp.wait_ge(y_done[at.par], at.pair)
                        sp.dma_start(xb[at.par][:], src_v[at.u]).then_inc(xb_loaded[at.par], 16)
                    if at := t.after(-1):
                        sp.wait_ge(y_done[at.par], at.pair + 1)
                        sp.dma_start(dst_v[at.u], y[at.par][:]).then_inc(y_stored[at.par], 16)

                skewed(sp, iteration, lead=3, lag=1)
                for par in range(2):
                    sp.wait_ge(y_stored[par], 16 * (B // 2))

            @block.gpsimd
            def _(pool):
                def iteration(t):
                    if routed and (at := t.after(3)):
                        norm.gather(pool, at)
                    if at := t.after(2):
                        norm.root(pool, at)
                    if not routed and (at := t.after(1)):
                        pool.wait_ge(xb_loaded[at.par], 16 * (at.pair + 1))
                        nc.gpsimd.tensor_tensor(xb[at.par][:], xb[at.par][:], bias, ALU.add).then_inc(
                            xb_done[at.par], 1)

                skewed(pool, iteration, lead=3 if routed else 2)

            @block.tensor
            def _(pe):
                def iteration(t):
                    if at := t.after(0):
                        pe.wait_ge(rank_lo, at.u + 1)
                        for c in range(FC):
                            nc.tensor.matmul(hid_ps[c][:], w["v1_stack"][:, c * P:(c + 1) * P],
                                             rank[at.par][:], start=True, stop=True).then_inc(hid_done, 1)
                    if at := t.after(-1):
                        pe.wait_ge(low_copied, at.u + 1)
                        pe.wait_ge(y_done[1 - at.par], at.pair + at.par)
                        for i in range(NT):
                            last = nc.tensor.matmul(out_ps[:, i, :], low[at.par][:, i * P:(i + 1) * P],
                                                    w["v2_half"][:], start=True, stop=True)
                        last.then_inc(out_done, 1)
                    if at := t.after(1):
                        pe.wait_ge(xt_copied, at.u + 1)
                        nc.tensor.matmul(rank_ps[:], w["u1"][:].rearrange("p g r -> p (g r)"), xt[at.par][:],
                                         start=True, stop=True).then_inc(rank_done, 1)
                    if at := t.after(0):
                        pe.wait_ge(gelu_done, (at.u + 1) * FC)
                        for c in range(FC):
                            last = nc.tensor.matmul(low_ps[c * R:(c + 1) * R, :], w["u2"][:, c, :], hid[c][:],
                                                    start=True, stop=True)
                        last.then_inc(low_done, 1)
                    if at := t.after(2):
                        norm.transpose(pe, at)

                skewed(pe, iteration, lead=2, lag=1)

            @block.scalar
            def _(act):
                def iteration(t):
                    def gelu(at, c):
                        act.wait_ge(hid_done, at.u * FC + c + 1)
                        act.wait_ge(low_done, at.u)
                        nc.scalar.activation(hid[c][:], hid_ps[c][:], ACT.Gelu_apprx_tanh,
                                             bias=w["b1"][:, c:c + 1]).then_inc(gelu_done, 1)

                    if at := t.after(0):
                        for c in range(FC):
                            gelu(at, c)
                    if at := t.after(1):
                        act.wait_ge(rank_done, at.u + 1)
                        nc.scalar.copy(rank[at.par][:], rank_ps[:]).then_inc(rank_hi, 1)
                    if at := t.after(0):
                        act.wait_ge(low_done, at.u + 1)
                        nc.scalar.copy(low[at.par][:], low_ps[:]).then_inc(low_copied, 1)
                    if at := t.after(2):
                        act.wait_ge(norm.xt_done[at.par], at.pair + 1)
                        nc.scalar.copy(xt[at.par][:], xt_ps[:]).then_inc(xt_copied, 1)

                skewed(act, iteration, lead=2)

            @block.vector
            def _(dve):
                def iteration(t):
                    if at := t.after(2):
                        if routed:
                            norm.combine(dve, at, xb_done, 1)
                        norm.statistics(dve, at)
                    if at := t.after(-1):
                        dve.wait_ge(out_done, at.u + 1)
                        dve.wait_ge(xb_done[at.par], at.pair + 1)
                        dve.wait_ge(y_stored[at.par], 16 * at.pair)
                        nc.vector.tensor_tensor(y[at.par][:], out_ps[:], xb[at.par][:], ALU.add).then_inc(
                            y_done[at.par], 1)
                    if routed and (at := t.after(4)):
                        norm.take(dve, at)
                    if at := t.after(2):
                        norm.normalise(dve, at)
                    if routed and (at := t.after(1)):
                        dve.wait_ge(y_done[at.par], at.pair)
                        nc.vector.tensor_tensor(xb[at.par][:], norm.x[at.par][:], bias, ALU.add).then_inc(
                            xb_done[at.par], 1)
                    if at := t.after(1):
                        dve.wait_ge(rank_hi, at.u + 1)
                        nc.vector.tensor_tensor(rank[at.par][64:P, :], rank_ps[64:P, :],
                                                rank[at.par][64:P, :].bitcast(F32),
                                                ALU.subtract).then_inc(rank_lo, 1)

                skewed(dve, iteration, lead=4 if routed else 2, lag=1)


MASKED = -9000000000000000.0


def make_causal_weights(nc, ctx, W, bias):
    sb = lambda n, s, d=F32: ctx.enter_context(nc.sbuf_tensor(f"causal_{n}", s, d))
    w = dict(w=sb("w", [P, 3 * D]), bias=sb("bias", [P, 3]), bq=sb("bq", [P, 1]), bv=sb("bv", [P, D]),
             mask=sb("mask", [P, P]))
    loaded = ctx.enter_context(nc.semaphore("causal_weights_loaded"))
    made = ctx.enter_context(nc.semaphore("causal_constants_made"))

    def load(pool):
        pool.dma_start(w["w"][:], W).then_inc(loaded, 16)
        pool.dma_start(w["bias"][:], bias.rearrange("(c p) -> p c", p=P),
                       allow_slow_non_contiguous=True).then_inc(loaded, 16)
        pool.dma_start(w["bv"][:], bias[2 * D:3 * D].partition_broadcast(P)).then_inc(loaded, 16)
        nc.gpsimd.memset(w["mask"][:], 0.0).then_inc(made, 1)
        pool.wait_ge(made, 1)
        nc.gpsimd.affine_select(out=w["mask"][:], in_=w["mask"][:], compare_op=ALU.is_ge, fill=MASKED,
                                base=0, pattern=[[-1, P]], channel_multiplier=1).then_inc(made, 1)
        pool.wait_ge(made, 2)
        pool.wait_ge(loaded, 3 * 16)
        nc.gpsimd.tensor_scalar_mul(w["bq"][:], w["bias"][:, 0:1], float(D) ** -0.5).then_inc(made, 1)
        pool.wait_ge(made, 3)

    return w, load


def causal_stage(nc, name, src, dst, const, w):
    SCALE = float(D) ** -0.5
    with ExitStack() as ctx:
        sb = lambda n, s, d=F32: ctx.enter_context(nc.sbuf_tensor(f"{name}_{n}", s, d))
        ps = lambda n, s: ctx.enter_context(nc.psum_tensor(f"{name}_{n}", s, F32))
        sem = lambda n: ctx.enter_context(nc.semaphore(f"{name}_{n}"))
        xt_ps = ps("xt_ps", [P, T])
        norm = Norm(nc, ctx, name, src, const, xt_ps)
        xt = [sb(f"xt{k}", [P, T]) for k in range(2)]
        res = [sb(f"res{k}", [P, NT, D]) for k in range(2)]
        q = [sb(f"q{k}", [P, T]) for k in range(2)]
        k_ = [sb(f"k{k}", [P, T]) for k in range(2)]
        v = [sb(f"v{k}", [P, NT, D]) for k in range(2)]
        neg_max = [sb(f"neg_max{k}", [P, NT]) for k in range(2)]
        row_sum = [sb(f"row_sum{k}", [P, NT]) for k in range(2)]
        inv_sum = [sb(f"inv_sum{k}", [P, NT]) for k in range(2)]
        prob = [sb(f"prob{i}", [P, T]) for i in range(NT)]
        prob_t = [sb(f"prob_t{k}", [P, NT, P]) for k in range(2)]
        y = [sb(f"y{k}", [P, NT, D]) for k in range(2)]
        qv_ps, k_ps = ps("qv_ps", [P, T]), ps("k_ps", [P, T])
        score_ps = [ps(f"score_ps{k}", [P, T]) for k in range(2)]
        prob_t_ps = [ps(f"prob_t_ps{k}", [P, NT, P]) for k in range(2)]
        out_ps = ps("out_ps", [P, NT, D])
        (xt_copied, q_done, k_done, v_done, q_copied, k_copied, v_copied, res_done, score_done, mask_added,
         max_done, exp_done, prob_t_done, prob_t_copied, value_done, inv_done) = [
            sem(n) for n in ("xt_copied", "q_done", "k_done", "v_done", "q_copied", "k_copied", "v_copied",
                             "res_done", "score_done", "mask_added", "max_done", "exp_done", "prob_t_done",
                             "prob_t_copied", "value_done", "inv_done")]
        copying = sem("copying")
        res_copied = [sem(f"res_copied{k}") for k in range(2)]
        y_done = [sem(f"y_done{k}") for k in range(2)]
        y_stored = [sem(f"y_stored{k}") for k in range(2)]
        dst_v = dst.rearrange("b (i p) d -> b p i d", p=P)

        with nc.Block() as block:
            @block.sync
            def _(sp):
                def iteration(t):
                    if at := t.after(3):
                        norm.load(sp, at, res_copied)
                    if at := t.after(0):
                        sp.wait_ge(y_done[at.par], at.pair + 1)
                        sp.dma_start(dst_v[at.u], y[at.par][:]).then_inc(y_stored[at.par], 16)

                skewed(sp, iteration, lead=3)
                for par in range(2):
                    sp.wait_ge(y_stored[par], 16 * (B // 2))

            @block.gpsimd
            def _(pool):
                def iteration(t):
                    if at := t.after(2):
                        norm.root(pool, at)
                        pool.wait_ge(norm.xn_done[at.par], at.pair + 1)
                        pool.wait_ge(y_done[at.par], at.pair)
                        pool.sem_inc(copying, 1)
                        nc.gpsimd.tensor_copy(res[at.par][:], norm.x[at.par][:]).then_inc(res_copied[at.par], 1)

                skewed(pool, iteration, lead=2)

            @block.tensor
            def _(pe):
                def score(at, i):
                    pe.wait_ge(exp_done, at.u * NT + max(i - 1, 0))
                    n = (i + 1) * P
                    nc.tensor.matmul(score_ps[i % 2][:, 0:n], q[at.par][:, i * P:n], k_[at.par][:, 0:n],
                                     start=True, stop=True).then_inc(score_done, 1)

                def prob_transpose(at, i):
                    pe.wait_ge(exp_done, at.u * NT + i + 1)
                    pe.wait_ge(prob_t_copied, at.u * NT + max(i - 1, 0))
                    for j in range(i + 1):
                        last = nc.tensor.transpose(prob_t_ps[i % 2][:, j, :], prob[i][:, j * P:(j + 1) * P],
                                                   const["ident"][:])
                    last.then_inc(prob_t_done, 1)

                def values(at, i):
                    pe.wait_ge(prob_t_copied, at.u * NT + i + 1)
                    for j in range(i + 1):
                        last = nc.tensor.matmul(out_ps[:, i, :], prob_t[i % 2][:, j, :], v[at.par][:, j, :],
                                                start=(j == 0), stop=(j == i))
                    last.then_inc(value_done, 1)

                def iteration(t):
                    now, nxt = t.after(0), t.after(1)
                    if now:
                        pe.wait_ge(q_copied, now.u + 1)
                        pe.wait_ge(k_copied, now.u + 1)
                        score(now, 0)
                        score(now, 1)
                    if nxt:
                        pe.wait_ge(xt_copied, nxt.u + 1)
                        pe.wait_ge(v_copied, nxt.u)
                        nc.tensor.matmul(qv_ps[:], w["w"][:, 0:D], xt[nxt.par][:], start=True,
                                         stop=True).then_inc(q_done, 1)
                    if now:
                        score(now, 2)
                    if nxt:
                        pe.wait_ge(k_copied, nxt.u)
                        nc.tensor.matmul(k_ps[:], w["w"][:, D:2 * D], xt[nxt.par][:], start=True,
                                         stop=True).then_inc(k_done, 1)
                    if now:
                        score(now, 3)
                    if nxt:
                        pe.wait_ge(q_copied, nxt.u + 1)
                        for i in range(NT):
                            last = nc.tensor.matmul(qv_ps[:, i * P:(i + 1) * P], xt[nxt.par][:, i * P:(i + 1) * P],
                                                    w["w"][:, 2 * D:3 * D], start=True, stop=True)
                        last.then_inc(v_done, 1)
                    if now:
                        prob_transpose(now, 0)
                        prob_transpose(now, 1)
                        pe.wait_ge(v_copied, now.u + 1)
                        pe.wait_ge(y_done[1 - now.par], now.pair + now.par)
                        values(now, 0)
                        prob_transpose(now, 2)
                        values(now, 1)
                        prob_transpose(now, 3)
                        values(now, 2)
                        values(now, 3)
                    if ahead := t.after(2):
                        norm.transpose(pe, ahead)

                skewed(pe, iteration, lead=2)

            @block.scalar
            def _(act):
                def exponential(at, i):
                    n = (i + 1) * P
                    act.wait_ge(max_done, at.u * NT + i + 1)
                    act.wait_ge(prob_t_done, at.u * NT)
                    nc.scalar.activation(prob[i][:, 0:n], score_ps[i % 2][:, 0:n], ACT.Exp,
                                         bias=neg_max[at.par][:, i:i + 1],
                                         accum_out=row_sum[at.par][:, i:i + 1]).then_inc(exp_done, 1)

                def iteration(t):
                    now, nxt = t.after(0), t.after(1)
                    if now:
                        exponential(now, 0)
                        exponential(now, 1)
                    if nxt:
                        act.wait_ge(q_done, nxt.u + 1)
                        nc.scalar.activation(q[nxt.par][:], qv_ps[:], ACT.Identity, bias=w["bq"][:, 0:1],
                                             scale=SCALE).then_inc(q_copied, 1)
                    if now:
                        exponential(now, 2)
                        exponential(now, 3)
                        for i in (0, 1, 2, 3):
                            act.wait_ge(prob_t_done, now.u * NT + i + 1)
                            act.wait_ge(value_done, now.u * NT + max(i - 1, 0))
                            nc.scalar.copy(prob_t[i % 2][:, 0:i + 1, :],
                                           prob_t_ps[i % 2][:, 0:i + 1, :]).then_inc(prob_t_copied, 1)
                    if ahead := t.after(2):
                        act.wait_ge(norm.xt_done[ahead.par], ahead.pair + 1)
                        nc.scalar.copy(xt[ahead.par][:], xt_ps[:]).then_inc(xt_copied, 1)

                skewed(act, iteration, lead=2)

            @block.vector
            def _(dve):
                def row_max(at, i):
                    n = (i + 1) * P
                    dve.wait_ge(score_done, at.u * NT + i + 1)
                    nc.vector.tensor_tensor(score_ps[i % 2][:, i * P:n], score_ps[i % 2][:, i * P:n],
                                            w["mask"][:], ALU.add).then_inc(mask_added, 1)
                    dve.wait_ge(mask_added, at.u * NT + i + 1)
                    nc.vector.tensor_reduce(neg_max[at.par][:, i:i + 1], score_ps[i % 2][:, 0:n], AX_X, ALU.max,
                                            negate=True).then_inc(max_done, 1)

                def iteration(t):
                    now, nxt, ahead = t.after(0), t.after(1), t.after(2)
                    if now:
                        row_max(now, 0)
                        row_max(now, 1)
                    if ahead:
                        norm.statistics(dve, ahead)
                    if now:
                        row_max(now, 2)
                    if nxt:
                        dve.wait_ge(k_done, nxt.u + 1)
                        nc.vector.tensor_scalar(k_[nxt.par][:], k_ps[:], w["bias"][:, 1:2], None,
                                                ALU.add).then_inc(k_copied, 1)
                    if now:
                        row_max(now, 3)
                    if nxt:
                        dve.wait_ge(v_done, nxt.u + 1)
                        nc.vector.tensor_tensor(v[nxt.par][:], qv_ps[:].rearrange("p (i d) -> p i d", i=NT),
                                                w["bv"][:].unsqueeze(1).to_broadcast([P, NT, D]),
                                                ALU.add).then_inc(v_copied, 1)
                    if ahead:
                        norm.normalise(dve, ahead)
                    if now:
                        dve.wait_ge(exp_done, (now.u + 1) * NT)
                        nc.vector.reciprocal(inv_sum[now.par][:], row_sum[now.par][:]).then_inc(inv_done, 1)
                        dve.wait_ge(inv_done, now.u + 1)
                        dve.wait_ge(value_done, (now.u + 1) * NT)
                        dve.wait_ge(res_copied[now.par], now.pair + 1)
                        dve.wait_ge(y_stored[now.par], 16 * now.pair)
                        for i in range(NT):
                            last = nc.vector.scalar_tensor_tensor(
                                y[now.par][:, i, :], out_ps[:, i, :], inv_sum[now.par][:, i:i + 1],
                                res[now.par][:, i, :], ALU.mult, ALU.add)
                        last.then_inc(y_done[now.par], 1)

                skewed(dve, iteration, lead=2)


H = 16
DH = D // H
SLOTS = H // 2
PARTS = 4
MAX_ROW = PARTS * DH
KROWS = 64
HALF = SLOTS // 2


def make_heads_weights(nc, ctx, wqk, wv, wo, bo, cos, sin):
    sb = lambda n, s, d=F32: ctx.enter_context(nc.sbuf_tensor(f"heads_{n}", s, d))
    w = dict(qk=sb("qk", [P, 2, D]), rot=sb("rot", [P, 2, D]), v=sb("v", [P, D]), o=sb("o", [P, D]),
             bo=sb("bo", [P, D]), cos=sb("cos", [P, T]), sin=sb("sin", [P, T]), k_rest=sb("k_rest", [P, 1]), q_rest=sb("q_rest", [P, 1]))
    loaded = ctx.enter_context(nc.semaphore("heads_weights_loaded"))
    zeroed = ctx.enter_context(nc.semaphore("heads_k_rest_zeroed"))

    def load(pool):
        pool.dma_start(w["qk"][:], wqk).then_inc(loaded, 16)
        for n in range(2):
            rot = w["rot"][:, n, :].rearrange("p (a e c) -> p a e c", e=2, c=DH // 2 * SLOTS)
            plain = wqk[:, n, :].rearrange("p (a e c) -> p a e c", e=2, c=DH // 2 * SLOTS)
            for e in range(2):
                pool.dma_start(rot[:, :, e, :], plain[:, :, 1 - e, :]).then_inc(loaded, 16)
        pool.dma_start(w["v"][:], wv).then_inc(loaded, 16)
        pool.dma_start(w["o"][:], wo).then_inc(loaded, 16)
        pool.dma_start(w["bo"][:], bo.partition_broadcast(P)).then_inc(loaded, 16)
        pool.dma_start(w["cos"][:], cos).then_inc(loaded, 16)
        pool.dma_start(w["sin"][:], sin).then_inc(loaded, 16)
        nc.gpsimd.memset(w["k_rest"][:], 0.0).then_inc(zeroed, 1)
        for low in range(2):
            row = 64 * low + MAX_ROW
            pool.wait_ge(zeroed, low + 1)
            nc.gpsimd.memset(w["k_rest"][row:row + 1, :], 1.0).then_inc(zeroed, 1)
        pool.wait_ge(zeroed, 3)
        nc.gpsimd.memset(w["q_rest"][:], 0.0).then_inc(zeroed, 1)
        pool.wait_ge(zeroed, 4)
        pool.wait_ge(loaded, 10 * 16)

    return w, load


class Kept(Norm):

    def __init__(self, nc, ctx, name, const, xt_ps, x, given):
        super().__init__(nc, ctx, name, None, const, xt_ps, x)
        self.given = given

    def wait_for_x(self, dve, at):
        dve.wait_ge(self.given[at.par], at.pair + 1)


def heads_stage(nc, name, src, whole_src, dst, const, w, r, slots, w_route, r_next, slots_next):
    STEPS = H * NT
    SETS = STEPS // 4
    ITEMS = STEPS // 2
    M_B, V, XT, Q, QR, K, KR = 1, 3, 6, 9, 13, 17, 21
    NORM = (26, 29, 32, 35)
    M_A, BACK, PROJECT = 38, 42, 46
    TAKE, STATISTICS, NORMALISE = 1, 49, 58
    ROUTE_STATISTICS, ROUTE_NORMALISE, ROUTE_XT, LOGITS, COUNT, EXPONENT = 48, 53, 56, 60, 24, 5
    with ExitStack() as ctx:
        sb = lambda n, s, d=F32: ctx.enter_context(nc.sbuf_tensor(f"{name}_{n}", s, d))
        ps = lambda n, s: ctx.enter_context(nc.psum_tensor(f"{name}_{n}", s, F32))
        sem = lambda n: ctx.enter_context(nc.semaphore(f"{name}_{n}"))
        misc_ps = ps("misc_ps", [P, T])
        norm = Combined(nc, ctx, name, src, const, misc_ps, r, slots)
        xt = sb("xt", [P, T])
        res = [sb(f"res{k}", [P, NT, D]) for k in range(2)]
        by_cos, by_sin, rotated = sb("by_cos", [P, T]), sb("by_sin", [P, T]), sb("rotated", [P, T])
        hi = [sb(f"hi{n}", [P, T], F32R) for n in range(2)]
        lo = [sb(f"lo{n}", [P, T], F32R) for n in range(2)]
        qx = [sb(f"qx{k}", [P, SLOTS, T], F32R) for k in range(2)]
        kx = [sb(f"kx{k}", [P, SLOTS, T], F32R) for k in range(2)]
        vx = [sb(f"vx{k}", [P, NT, H, 32]) for k in range(2)]
        row_max = sb("row_max", [P, 2, 2, HALF, NT])
        neg_max = [sb(f"neg_max{k}", [32, P], F32R) for k in range(2)]
        prob = [sb(f"prob{k}", [P, T]) for k in range(8)]
        ot = [[sb(f"ot{k}{g}", [P, T]) for g in range(4)] for k in range(2)]
        inv_sum = sb("inv_sum", [P, NT, H])
        o = [sb(f"o{i}", [P, H, DH]) for i in range(NT)]
        oT = sb("oT", [P, T])
        y = [sb(f"y{k}", [P, NT, D]) for k in range(2)]
        max_ps = [ps(f"max_ps{k}", [P, 2, T]) for k in range(2)]
        score_ps = [ps(f"score_ps{k}", [P, T]) for k in range(2)]
        value_ps = ps("value_ps", [P, T])
        names = ("xt_copied qk_done cos_done sin_done rope_done hi_done lo_done v_done v_copied "
                 "max_done row_max_done m_turned m_negated score_done exp_done value_done ot_copied "
                 "turned inv_done o_done back_done back_copied project_done set_up k_filled q_filled")
        (xt_copied, qk_done, cos_done, sin_done, rope_done, hi_done, lo_done, v_done, v_copied,
         max_done, row_max_done, m_turned, m_negated, score_done, exp_done, value_done, ot_copied,
         turned, inv_done, o_done, back_done, back_copied, project_done, set_up, k_filled, q_filled) = [sem(n) for n in names.split()]
        set_done = [sem(f"set_done{k}") for k in range(2)]
        res_loaded = [sem(f"res_loaded{k}") for k in range(2)]
        res_done = [sem(f"res_done{k}") for k in range(2)]
        y_done = [sem(f"y_done{k}") for k in range(2)]
        y_stored = [sem(f"y_stored{k}") for k in range(2)]
        expanded = [[sem(f"expanded{k}{half}") for half in range(2)] for k in range(2)]
        m_placed = [[sem(f"m_placed{k}{half}") for half in range(2)] for k in range(2)]
        kept = [sem(f"kept{k}") for k in range(2)]
        y_norm = Kept(nc, ctx, f"{name}_y_norm", const, misc_ps, y, y_done)
        router = Router(nc, ctx, f"{name}_router", y_norm, w_route, r_next, slots_next,
                        misc_ps[:, 0:NT * E].rearrange("p (i e) -> p i e", e=E),
                        misc_ps[:, NT * E:2 * NT * E].rearrange("p (i e) -> p i e", e=E),
                        misc_ps[:, 2 * NT * E:2 * NT * E + E])
        src_v = whole_src.rearrange("b (i p) d -> b p i d", p=P)
        dst_v = dst.rearrange("b (i p) d -> b p i d", p=P)
        spill_done = [sem(f"spill_done{k}") for k in range(2)]
        spilled = nc.dram_tensor(f"{name}_spilled", [2, 2, 2, 3, DH, SLOTS, T], F32).ap()
        max_spill_done = [sem(f"max_spill_done{half}") for half in range(2)]
        max_spilled = nc.dram_tensor(f"{name}_max_spilled", [2, 2, 2, HALF, NT, P], F32).ap()
        SPILLS, EXPANDS = 5 * 16, 10 * 16

        def rows(buf, head):
            at = 64 * (head % 2)
            return buf[at:at + KROWS, head // 2, :]


        def score_places(at):
            return [score_ps[k][:] for k in range(2)] + [
                max_ps[k][:, i, :] for k in range(2) for i in range(2) if not at.after(1)]

        with nc.Block() as block:
            @block.sync
            def _(sp):
                def place_max(at, half):
                    sp.wait_ge(m_negated, at.u * 2 + half + 1)
                    sp.dma_start(max_spilled[at.par, half].rearrange("a s i q -> (a s i) q"),
                                 neg_max[half][:].bitcast(F32)).then_inc(max_spill_done[half], 16)
                    sp.wait_ge(max_spill_done[half], 16 * (at.u + 1))
                    for par in range(2):
                        row = 64 * par + MAX_ROW
                        sp.dma_start(qx[at.par][row:row + 1, half * HALF:(half + 1) * HALF, :].bitcast(F32),
                                     max_spilled[at.par, half, par].rearrange("s i q -> s (i q)").unsqueeze(0)
                                     ).then_inc(m_placed[at.par][half], 16)

                def spill(at):
                    for n in range(2):
                        sp.wait_ge(lo_done, at.u * 2 + n + 1)
                        for half in range(2):
                            sp.wait_ge(expanded[at.par][half], EXPANDS * at.pair)
                        for part, source in enumerate((hi[n], lo[n], hi[n])[:2 + n]):
                            sp.dma_start(spilled[at.par, n, :, part].rearrange("a d s t -> a (d s) t"),
                                         source[:].bitcast(F32)).then_inc(spill_done[at.par], 16)

                def expand(at, half):
                    if isinstance(at.u, int) and at.u == 0:
                        sp.wait_ge(set_up, 1)
                    if isinstance(at.u, int) and at.u == 1:
                        sp.wait_ge(q_filled, 2)
                    slots = slice(half * HALF, (half + 1) * HALF)
                    for n, wide in ((0, qx), (1, kx)):
                        for par in range(2):
                            for pair in range(2):
                                to = 64 * par + 2 * DH * pair
                                start = pair if n else 0
                                sp.dma_start(wide[at.par][to:to + 2 * DH, slots, :].bitcast(F32),
                                             spilled[at.par, n, par, start:start + 2, :, slots, :]
                                             .rearrange("l d s t -> (l d) s t")).then_inc(expanded[at.par][half], 16)
                    sp.wait_ge(k_filled, 1)
                    for par in range(2):
                        row = 64 * par + MAX_ROW
                        sp.dma_start(qx[at.par][row:row + 1, slots, :].bitcast(F32),
                                     kx[0][MAX_ROW + 1:MAX_ROW + 2, 0:HALF, :].bitcast(F32)).then_inc(expanded[at.par][half], 16)

                def iteration(t):
                    if at := t.after(4):
                        norm.load(sp, at)
                    if at := t.after(0):
                        sp.wait_ge(y_done[at.par], at.pair)
                        sp.wait_ge(kept[at.par], 16 * (at.pair + 1))
                        sp.dma_start(res[at.par][:], src_v[at.u]).then_inc(res_loaded[at.par], 16)
                        place_max(at, 1)
                    if at := t.after(2):
                        spill(at)
                        sp.wait_ge(spill_done[at.par], SPILLS * (at.pair + 1))
                        if now := t.after(0):
                            sp.wait_ge(score_done, now.u * STEPS + STEPS // 2)
                        expand(at, 0)
                    if at := t.after(1):
                        place_max(at, 0)
                    if at := t.after(-1):
                        sp.wait_ge(y_done[at.par], at.pair + 1)
                        sp.dma_start(dst_v[at.u], y[at.par][:]).then_inc(y_stored[at.par], 16)
                    if at := t.after(2):
                        if now := t.after(0):
                            sp.wait_ge(score_done, (now.u + 1) * STEPS)
                        expand(at, 1)
                    if at := t.after(3):
                        sp.wait_ge(norm.combined[at.par], at.pair + 1)
                        sp.dma_start(src_v[at.u], norm.x[at.par][:]).then_inc(kept[at.par], 16)

                skewed(sp, iteration, lead=4, lag=1)
                for par in range(2):
                    sp.wait_ge(y_stored[par], 16 * (B // 2))

            @block.gpsimd
            def _(pool):
                def iteration(t):
                    if at := t.after(0):
                        pool.wait_ge(res_loaded[at.par], 16 * (at.pair + 1))
                        nc.gpsimd.tensor_tensor(res[at.par][:], res[at.par][:],
                                                w["bo"][:].unsqueeze(1).to_broadcast([P, NT, D]),
                                                ALU.add).then_inc(res_done[at.par], 1)
                    if at := t.after(2):
                        for n in range(2):
                            pool.wait_ge(sin_done, at.u * 2 + n + 1)
                            pool.wait_ge(lo_done, at.u * 2 + n)
                            nc.gpsimd.tensor_tensor(rotated[:], by_cos[:], by_sin[:], ALU.add).then_inc(rope_done, 1)
                            pool.wait_ge(hi_done, at.u * 2 + n + 1)
                            nc.gpsimd.tensor_tensor(lo[n][:], rotated[:], hi[n][:].bitcast(F32),
                                                    ALU.subtract).then_inc(lo_done, 1)

                    if at := t.after(-2):
                        router.scatter(pool, at)
                    if at := t.after(-1):
                        y_norm.root(pool, at)
                    if at := t.after(3):
                        norm.root(pool, at)
                    if at := t.after(4):
                        norm.gather(pool, at)

                skewed(pool, iteration, lead=4, lag=2)

            @block.tensor
            def _(pe):
                def values(at, s):
                    g, c = s // NT, s % NT
                    pe.wait_ge(exp_done, at.u * STEPS + 4 * s + 4)
                    if s == 0:
                        pe.wait_ge(v_copied, at.u + 1)
                    if c == 0:
                        pe.wait_ge(ot_copied, at.u * 4 + g)
                    for j in range(4):
                        last = nc.tensor.matmul(value_ps[32 * j:32 * j + 32, :], vx[at.par][:, c, 4 * g + j, :],
                                                prob[4 * (s % 2) + j][:], start=(c == 0), stop=(c == NT - 1))
                    last.then_inc(set_done[s % 2], 1)

                def score(at, k):
                    head, c = 4 * (k // 16) + k % 4, k // 4 % NT
                    places = score_places(at)
                    pe.wait_ge(exp_done, at.u * STEPS + max(k - len(places) + 1, 0))
                    if k % (STEPS // 2) == 0:
                        pe.wait_ge(m_placed[at.par][k // (STEPS // 2)], 32 * (at.pair + 1))
                    nc.tensor.matmul(places[k % len(places)], rows(kx[at.par], head)[:, c * P:(c + 1) * P],
                                     rows(qx[at.par], head), start=True, stop=True).then_inc(score_done, 1)

                def score_for_max(at, n):
                    head = n // 2
                    if n == 0 and isinstance(at.u, int) and at.u < 2:
                        pe.wait_ge(set_up, 2)
                        pe.wait_ge(k_filled, 4)
                        pe.wait_ge(q_filled, 2 * at.u)
                    if n % (ITEMS // 2) == 0:
                        pe.wait_ge(expanded[at.par][n // (ITEMS // 2)], EXPANDS * (at.pair + 1))
                    pe.wait_ge(row_max_done, at.u * ITEMS + max(n - 1, 0))
                    for i in range(2):
                        tile = 2 * (n % 2) + i
                        last = nc.tensor.matmul(
                            max_ps[n % 2][:, i, :], rows(qx[at.par], head)[:, tile * P:(tile + 1) * P],
                            rows(kx[at.par], head), start=True, stop=True)
                    last.then_inc(max_done, 1)

                def turn_max(at, half):
                    pe.wait_ge(row_max_done, at.u * ITEMS + (half + 1) * ITEMS // 2)
                    nc.tensor.transpose(misc_ps[0:32, 0:P], row_max[:, half].rearrange("p a s i -> p (a s i)"),
                                        const["ident"][:]).then_inc(m_turned, 1)

                def product(at, weights, done):
                    nc.tensor.matmul(misc_ps[:], weights, xt[:], start=True, stop=True).then_inc(done, 1)

                def iteration(t):
                    past, prev, now, nxt, ahead = [t.after(n) for n in range(-2, 3)]
                    for k in range(STEPS):
                        if k % 4 == 2:
                            s = k // 4 - 1
                            if s < 0 and prev:
                                values(prev, SETS - 1)
                            if s >= 0 and now:
                                values(now, s)
                        if now:
                            score(now, k)
                        if nxt and k % 2:
                            score_for_max(nxt, k // 2)
                        if now and k == M_B:
                            pe.wait_ge(m_negated, now.u * 2 + 1)
                            if now.after(-2):
                                pe.wait_ge(router.logit_copied, now.u - 1)
                            turn_max(now, 1)
                        if nxt and k == V:
                            if now:
                                pe.wait_ge(m_negated, now.u * 2 + 2)
                            pe.wait_ge(sin_done, (nxt.u + 1) * 2)
                            for i in range(NT):
                                last = nc.tensor.matmul(misc_ps[:, i * P:(i + 1) * P], xt[:, i * P:(i + 1) * P],
                                                        w["v"][:], start=True, stop=True)
                            last.then_inc(v_done, 1)
                        if ahead and k == XT:
                            if nxt:
                                pe.wait_ge(v_copied, nxt.u + 1)
                            norm.transpose(pe, ahead)
                        if ahead and k == Q:
                            pe.wait_ge(xt_copied, ahead.u + 1)
                            product(ahead, w["qk"][:, 0, :], qk_done)
                        if ahead and k == QR:
                            pe.wait_ge(cos_done, ahead.u * 2 + 1)
                            product(ahead, w["rot"][:, 0, :], qk_done)
                        if ahead and k == K:
                            pe.wait_ge(sin_done, ahead.u * 2 + 1)
                            product(ahead, w["qk"][:, 1, :], qk_done)
                        if ahead and k == KR:
                            pe.wait_ge(cos_done, ahead.u * 2 + 2)
                            product(ahead, w["rot"][:, 1, :], qk_done)
                        if past and k == COUNT:
                            if ahead:
                                pe.wait_ge(sin_done, (ahead.u + 1) * 2)
                            elif nxt:
                                pe.wait_ge(v_copied, nxt.u + 1)
                            elif now:
                                pe.wait_ge(m_negated, now.u * 2 + 2)
                            router.count(pe, past)
                        if prev and k in NORM:
                            i = NORM.index(k)
                            pe.wait_ge(ot_copied, (prev.u + 1) * 4)
                            if past:
                                pe.wait_ge(router.count_done, past.u + 1)
                            elif ahead:
                                pe.wait_ge(sin_done, (ahead.u + 1) * 2)
                            elif nxt:
                                pe.wait_ge(v_copied, nxt.u + 1)
                            elif now:
                                pe.wait_ge(m_negated, now.u * 2 + 2)
                            pe.wait_ge(o_done, prev.u * NT + i)
                            for g in range(4):
                                last = nc.tensor.transpose(misc_ps[:, g * P:(g + 1) * P],
                                                           ot[prev.par][g][:, i * P:(i + 1) * P], const["ident"][:])
                            last.then_inc(turned, 1)
                        if nxt and k == M_A:
                            if prev:
                                pe.wait_ge(o_done, (prev.u + 1) * NT)
                            elif ahead:
                                pe.wait_ge(sin_done, (ahead.u + 1) * 2)
                            turn_max(nxt, 0)
                        if prev and k == BACK:
                            if nxt:
                                pe.wait_ge(m_negated, nxt.u * 2 + 1)
                            pe.wait_ge(o_done, (prev.u + 1) * NT)
                            for i in range(NT):
                                last = nc.tensor.transpose(misc_ps[:, i * P:(i + 1) * P],
                                                           o[i][:].rearrange("p h d -> p (h d)"), const["ident"][:])
                            last.then_inc(back_done, 1)
                        if prev and k == PROJECT:
                            pe.wait_ge(back_copied, prev.u + 1)
                            for i in range(NT):
                                last = nc.tensor.matmul(misc_ps[:, i * P:(i + 1) * P], oT[:, i * P:(i + 1) * P],
                                                        w["o"][:], start=True, stop=True)
                            last.then_inc(project_done, 1)
                        if prev and k == ROUTE_XT:
                            y_norm.transpose(pe, prev)
                        if prev and k == LOGITS:
                            router.logits(pe, prev)

                skewed(pe, iteration, lead=2, lag=2)

            @block.scalar
            def _(act):
                def iteration(t):
                    past, prev, now, nxt, ahead = [t.after(n) for n in range(-2, 3)]
                    for k in range(STEPS):
                        if now:
                            s = k // 4
                            act.wait_ge(score_done, now.u * STEPS + k + 1)
                            if k % 4 == 0:
                                act.wait_ge(set_done[s % 2], now.u * (SETS // 2) + s // 2)
                            places = score_places(now)
                            nc.scalar.activation(prob[k % 8][:], places[k % len(places)], ACT.Exp,
                                                 scale=float(DH) ** -0.5).then_inc(exp_done, 1)
                        if k % 16 == 3:
                            g = k // 16 - 1
                            at = now if g >= 0 else prev
                            if at:
                                g %= 4
                                act.wait_ge(set_done[1], at.u * (SETS // 2) + 2 * g + 2)
                                if at.after(-2):
                                    act.wait_ge(turned, (at.u - 1) * NT)
                                nc.scalar.copy(ot[at.par][g][:], value_ps[:]).then_inc(ot_copied, 1)
                        if prev and k == BACK + 1:
                            act.wait_ge(back_done, prev.u + 1)
                            nc.scalar.copy(oT[:], misc_ps[:]).then_inc(back_copied, 1)
                        if past and k == EXPONENT:
                            router.exponent(act, past)
                        if prev and k == ROUTE_XT + 1:
                            router.copy_xt(act, prev)
                        if ahead and k == XT + 1:
                            act.wait_ge(norm.xt_done[ahead.par], ahead.pair + 1)
                            if nxt:
                                act.wait_ge(v_done, nxt.u + 1)
                            nc.scalar.copy(xt[:], misc_ps[:]).then_inc(xt_copied, 1)
                            if not nxt:
                                for low in range(2):
                                    row = 64 * low + MAX_ROW
                                    nc.scalar.copy(qx[1][row:row + 32, :, :].rearrange("p s t -> p (s t)"),
                                                   w["q_rest"][row:row + 32, :].to_broadcast([32, SLOTS * T])
                                                   ).then_inc(q_filled, 1)
                        for n, at_step in ((0, QR + 5), (1, KR + 5)):
                            if ahead and k == at_step:
                                act.wait_ge(rope_done, ahead.u * 2 + n + 1)
                                act.wait_ge(spill_done[1 - ahead.par], SPILLS * (ahead.pair + ahead.par))
                                nc.scalar.copy(hi[n][:], rotated[:]).then_inc(hi_done, 1)

                for par in range(2):
                    for low in range(2):
                        row = 64 * low + MAX_ROW
                        nc.scalar.copy(kx[par][row:row + 32, :, :].rearrange("p s t -> p (s t)"),
                                       w["k_rest"][row:row + 32, :].to_broadcast([32, SLOTS * T])).then_inc(k_filled, 1)
                skewed(act, iteration, lead=2, lag=2)

            @block.vector
            def _(dve):
                def negate(at, half):
                    dve.wait_ge(m_turned, at.u * 2 + half + 1)
                    dve.wait_ge(max_spill_done[half], 16 * at.u)
                    nc.vector.tensor_scalar_mul(neg_max[half][:], misc_ps[0:32, 0:P], -1.0).then_inc(m_negated, 1)

                def iteration(t):
                    past, prev, now, nxt, ahead, normed, fetched = [t.after(n) for n in range(-2, 5)]
                    for k in range(STEPS):
                        if nxt and k % 2:
                            n = k // 2
                            half, head, tile = n // (ITEMS // 2), n // 2, 2 * (n % 2)
                            dve.wait_ge(max_done, nxt.u * ITEMS + n + 1)
                            if n % (ITEMS // 2) == 0:
                                dve.wait_ge(m_turned, nxt.u * 2 - 1 + half if half else nxt.u * 2)
                            nc.vector.tensor_reduce(row_max[:, half, head % 2, head // 2 % HALF, tile:tile + 2],
                                                    max_ps[n % 2][:], AX_X, ALU.max).then_inc(row_max_done, 1)
                        if now and k == M_B + 1:
                            negate(now, 1)
                        if nxt and k == V + 1:
                            dve.wait_ge(v_done, nxt.u + 1)
                            if prev:
                                dve.wait_ge(set_done[1], (prev.u + 1) * (SETS // 2))
                            nc.vector.tensor_copy(vx[nxt.par][:, :, :, 0:DH],
                                                  misc_ps[:].rearrange("p (i h d) -> p i h d", i=NT, h=H)
                                                  ).then_inc(v_copied, 1)
                        for n, at_step in ((0, Q + 1), (1, K + 1)):
                            if ahead and k == at_step:
                                dve.wait_ge(qk_done, ahead.u * 4 + 2 * n + 1)
                                dve.wait_ge(rope_done, ahead.u * 2 + n)
                                nc.vector.tensor_tensor(by_cos[:], misc_ps[:], w["cos"][:], ALU.mult).then_inc(cos_done, 1)
                        for n, at_step in ((0, QR + 1), (1, KR + 1)):
                            if ahead and k == at_step:
                                dve.wait_ge(qk_done, ahead.u * 4 + 2 * n + 2)
                                nc.vector.tensor_tensor(by_sin[:], misc_ps[:], w["sin"][:], ALU.mult).then_inc(sin_done, 1)
                        if prev and k - 1 in NORM:
                            i = NORM.index(k - 1)
                            dve.wait_ge(turned, prev.u * NT + i + 1)
                            wide = misc_ps[:].rearrange("p (h c) -> p h c", c=32)
                            nc.vector.reciprocal(inv_sum[:, i, :], wide[:, :, DH]).then_inc(inv_done, 1)
                            dve.wait_ge(inv_done, prev.u * NT + i + 1)
                            dve.wait_ge(back_done, prev.u)
                            nc.vector.tensor_tensor(o[i][:], wide[:, :, 0:DH],
                                                    inv_sum[:, i, :].unsqueeze(2).to_broadcast([P, H, DH]),
                                                    ALU.mult).then_inc(o_done, 1)
                        if nxt and k == M_A + 1:
                            negate(nxt, 0)
                        if prev and k == PROJECT + 1:
                            dve.wait_ge(project_done, prev.u + 1)
                            dve.wait_ge(y_stored[prev.par], 16 * prev.pair)
                            dve.wait_ge(res_done[prev.par], prev.pair + 1)
                            nc.vector.tensor_tensor(y[prev.par][:], misc_ps[:].rearrange("p (i d) -> p i d", i=NT),
                                                    res[prev.par][:], ALU.add).then_inc(y_done[prev.par], 1)
                        if fetched and k == TAKE:
                            norm.take(dve, fetched)
                        if prev and k == ROUTE_STATISTICS:
                            y_norm.statistics(dve, prev)
                        if prev and k == ROUTE_NORMALISE:
                            router.normalise(dve, prev)
                        if prev and k == LOGITS + 1:
                            router.choose(dve, prev)
                        if past and k == COUNT + 1:
                            router.positions(dve, past)
                        if past and k == COUNT + 4:
                            router.gates(dve, past)
                        if normed and k == STATISTICS:
                            norm.combine(dve, normed, kept, 16)
                            norm.statistics(dve, normed)
                        if normed and k == NORMALISE:
                            norm.normalise(dve, normed)
                        if fetched and not normed and k == TAKE + 1:
                            for low in range(2):
                                row = 64 * low + MAX_ROW
                                nc.vector.memset(qx[0][row:row + 32, :, :].bitcast(F32), 0.0)
                            nc.vector.memset(vx[0][:, :, :, DH + 1:32], 0.0).then_inc(set_up, 1)
                        if normed and not ahead and k == NORMALISE + 1:
                            nc.vector.memset(vx[0][:, :, :, DH:DH + 1], 1.0)
                            nc.vector.memset(vx[1][:, :, :, DH + 1:32], 0.0)
                            nc.vector.memset(vx[1][:, :, :, DH:DH + 1], 1.0).then_inc(set_up, 1)

                router.begin(dve)
                skewed(dve, iteration, lead=4, lag=2)


E = 8
HID = 256
BF16 = mybir.dt.bfloat16
REGION = P + B * T
TILES = 2 * B * T // P + E
LOWEST = -3.0e38
X_ROWS = E * REGION
Y_ROWS = TILES * P


def load_experts(nc, ctx, w_gate, w_up, w_down):
    w = dict(plain=ctx.enter_context(nc.sbuf_tensor("experts_plain", [P, E, 2 * HID], F32)),
             down=ctx.enter_context(nc.sbuf_tensor("experts_down", [P, 2 * E, D], F32)),
             loaded=ctx.enter_context(nc.semaphore("experts_loaded")))

    def load(sp):
        for side, source in enumerate((w_gate, w_up)):
            sp.dma_start(w["plain"][:, :, side * HID:(side + 1) * HID],
                         source.rearrange("e d h -> d e h")).then_inc(w["loaded"], 16)
        sp.dma_start(w["down"][:], w_down.rearrange("e (c p) d -> p (e c) d", p=P)).then_inc(w["loaded"], 16)

    return w, load


def make_route_constants(nc, ctx, router, slots):
    sb = lambda n, s, d=F32: ctx.enter_context(nc.sbuf_tensor(f"route_{n}", s, d))
    w = dict(router=sb("router", [P, E]), below=sb("below", [P, P], BF16), ones=sb("ones", [P, P], BF16),
             prefer=sb("prefer", [P, NT, E]), base=sb("base", [P, E]),
             tile=sb("tile", [P, TILES]), zero=sb("zero", [P, D]))
    loaded = ctx.enter_context(nc.semaphore("router_loaded"))
    filled = ctx.enter_context(nc.semaphore("route_constants_filled"))
    with nc.Block() as block:
        @block.sync
        def _(sp):
            sp.dma_start(w["router"][:], router).then_inc(loaded, 16)
            sp.wait_ge(filled, 1)
            for layer in slots:
                sp.dma_start(layer["x"].rearrange("(e r) d -> r e d", e=E)[0:P],
                             w["zero"][:].unsqueeze(1).to_broadcast([P, E, D])).then_inc(loaded, 16)
            sp.wait_ge(loaded, 3 * 16)

        @block.gpsimd
        def _(pool):
            nc.gpsimd.memset(w["zero"][:], 0.0).then_inc(filled, 1)
            nc.gpsimd.memset(w["ones"][:], 1.0).then_inc(filled, 1)
            pool.wait_ge(filled, 2)
            nc.gpsimd.affine_select(out=w["below"][:], in_=w["ones"][:], compare_op=ALU.is_gt, fill=0.0, base=0,
                                    pattern=[[1, P]], channel_multiplier=-1)
            iota = dict(channel_multiplier=0, allow_small_or_imprecise_dtypes=True)
            nc.gpsimd.iota(w["prefer"][:], pattern=[[0, NT], [-1, E]], base=E, **iota)
            nc.gpsimd.iota(w["base"][:], pattern=[[REGION, E]], base=P, **iota)
            nc.gpsimd.iota(w["tile"][:], pattern=[[1, TILES]], base=0, **iota)
    return w


def make_tables(nc, ctx, name):
    sb = lambda n, s, d=F32: ctx.enter_context(nc.sbuf_tensor(f"{name}_{n}", s, d))
    return dict(sent=sb("sent", [P, B * NT, 2]), at=sb("at", [P, B * NT, 2], U32), gate=sb("gate", [P, B * NT, 2]),
                count=sb("count", [P, E]), expert=sb("expert", [1, TILES], I32), start=sb("start", [1, TILES], I32))


class Router:

    def __init__(self, nc, ctx, name, norm, w, r, slots, logit_ps, ahead_ps, total_ps):
        sb = lambda n, s, d=F32: ctx.enter_context(nc.sbuf_tensor(f"{name}_{n}", s, d))
        sem = lambda n: ctx.enter_context(nc.semaphore(f"{name}_{n}"))
        self.nc, self.norm, self.w, self.r, self.slots = nc, norm, w, r, slots
        self.logit_ps, self.ahead_ps, self.total_ps = logit_ps, ahead_ps, total_ps
        self.xt = sb("xt", [P, T])
        self.logit, self.rest, self.same, self.rank, self.place = [
            sb(n, [P, NT, E]) for n in ("logit", "rest", "same", "rank", "place")]
        self.best, self.gate_sum, self.twice = [sb(n, [P, NT, 1]) for n in ("best", "gate_sum", "twice")]
        self.chosen, self.mine = [sb(n, [P, NT, 2, E]) for n in ("chosen", "mine")]
        self.both = sb("both", [P, NT, E], BF16)
        self.top, self.clamped, self.power, self.sigma, self.spot = [
            sb(n, [P, NT, 2]) for n in ("top", "clamped", "power", "sigma", "spot")]
        self.at_now = [sb(f"at_now{k}", [P, NT, 2], U32) for k in range(2)]
        self.scattered = slots["scattered"]
        (self.xt_copied, self.logit_done, self.logit_copied, self.both_done, self.ahead_done, self.top_clamped,
         self.power_done, self.at_done, self.count_done, self.count_ready, self.scattering, self.choice,
         self.position, self.gating) = [sem(n) for n in (
             "xt_copied", "logit_done", "logit_copied", "both_done", "ahead_done", "top_clamped", "power_done",
             "at_done", "count_done", "count_ready", "scattering", "choice", "position", "gating")]

    def begin(self, dve):
        self.nc.vector.tensor_copy(self.r["count"][:], self.w["base"][:]).then_inc(self.count_ready, 1)
        dve.wait_ge(self.count_ready, 1)

    def normalise(self, dve, at):
        dve.wait_ge(self.scattered[at.par], 16 * 2 * NT * at.pair)
        self.norm.normalise(dve, at)

    def copy_xt(self, act, at):
        act.wait_ge(self.norm.xt_done[at.par], at.pair + 1)
        act.wait_ge(self.logit_done, at.u)
        self.nc.scalar.copy(self.xt[:], self.norm.xt_ps[:]).then_inc(self.xt_copied, 1)

    def logits(self, pe, at):
        nc = self.nc
        pe.wait_ge(self.xt_copied, at.u + 1)
        pe.wait_ge(self.logit_copied, at.u)
        for i in range(NT):
            last = nc.tensor.matmul(self.logit_ps[:, i, :], self.xt[:, i * P:(i + 1) * P], self.w["router"][:],
                                    start=True, stop=True)
        last.then_inc(self.logit_done, 1)

    def choose(self, dve, at):
        V, top, chosen = self.nc.vector, self.top, self.chosen
        wide = [P, NT, E]
        STEPS = 11
        dve.wait_ge(self.logit_done, at.u + 1)
        V.tensor_copy(self.logit[:], self.logit_ps).then_inc(self.logit_copied, 1)
        dve.wait_ge(self.logit_copied, at.u + 1)
        for j, values in enumerate((self.logit, self.rest)):
            done = at.u * STEPS + j * 6
            V.tensor_reduce(top[:, :, j:j + 1], values[:], AX_X, ALU.max).then_inc(self.choice, 1)
            dve.wait_ge(self.choice, done + 1)
            V.tensor_tensor(self.same[:], values[:], top[:, :, j:j + 1].to_broadcast(wide),
                            ALU.is_equal).then_inc(self.choice, 1)
            dve.wait_ge(self.choice, done + 2)
            V.tensor_tensor(self.rank[:], self.same[:], self.w["prefer"][:], ALU.mult).then_inc(self.choice, 1)
            dve.wait_ge(self.choice, done + 3)
            V.tensor_reduce(self.best[:], self.rank[:], AX_X, ALU.max).then_inc(self.choice, 1)
            dve.wait_ge(self.choice, done + 4)
            V.tensor_tensor(chosen[:, :, j, :], self.rank[:], self.best[:].to_broadcast(wide),
                            ALU.is_equal).then_inc(self.choice, 1)
            dve.wait_ge(self.choice, done + 5)
            if j == 0:
                V.scalar_tensor_tensor(self.rest[:], chosen[:, :, 0, :], LOWEST, self.logit[:], ALU.mult,
                                       ALU.add).then_inc(self.choice, 1)
                dve.wait_ge(self.choice, done + 6)
        V.tensor_tensor(self.both[:], chosen[:, :, 0, :], chosen[:, :, 1, :], ALU.add).then_inc(self.both_done, 1)
        V.tensor_scalar_max(self.clamped[:], top[:], -87.0).then_inc(self.top_clamped, 1)

    def count(self, pe, at):
        nc, both, ones = self.nc, self.both, self.w["ones"]
        pe.wait_ge(self.both_done, at.u + 1)
        pe.wait_ge(self.count_done, at.u)
        nc.tensor.matmul(self.ahead_ps, self.w["below"][:], both[:], start=True, stop=False)
        for i in range(NT - 1):
            nc.tensor.matmul(self.ahead_ps[:, i + 1:, :], ones[:],
                             both[:, i:i + 1, :].to_broadcast([P, NT - 1 - i, E]), start=False, stop=(i == NT - 2))
        for i in range(NT):
            last = nc.tensor.matmul(self.total_ps, ones[:], both[:, i, :], start=(i == 0), stop=(i == NT - 1))
        last.then_inc(self.ahead_done, 1)

    def positions(self, dve, at):
        V, r = self.nc.vector, self.r
        dve.wait_ge(self.ahead_done, at.u + 1)
        V.tensor_tensor(self.place[:], self.ahead_ps, r["count"][:].unsqueeze(1).to_broadcast([P, NT, E]),
                        ALU.add).then_inc(self.position, 1)
        dve.wait_ge(self.position, at.u * 3 + 1)
        V.tensor_tensor(r["count"][:], r["count"][:], self.total_ps, ALU.add).then_inc(self.count_done, 1)
        V.tensor_tensor(self.mine[:], self.chosen[:], self.place[:].unsqueeze(2).to_broadcast([P, NT, 2, E]),
                        ALU.mult).then_inc(self.position, 1)
        dve.wait_ge(self.position, at.u * 3 + 2)
        V.tensor_reduce(self.spot[:], self.mine[:], AX_X, ALU.add).then_inc(self.position, 1)
        dve.wait_ge(self.position, at.u * 3 + 3)
        V.tensor_copy(r["sent"][:, bass.ds(at.u * NT, NT), :], self.spot[:])
        dve.wait_ge(self.scattered[at.par], 16 * 2 * NT * at.pair)
        V.tensor_copy(self.at_now[at.par][:], self.spot[:]).then_inc(self.at_done, 1)

    def exponent(self, act, at):
        act.wait_ge(self.top_clamped, at.u + 1)
        self.nc.scalar.activation(self.power[:], self.clamped[:], ACT.Exp, scale=-1.0).then_inc(self.power_done, 1)

    def gates(self, dve, at):
        V = self.nc.vector
        dve.wait_ge(self.power_done, at.u + 1)
        V.tensor_scalar_add(self.sigma[:], self.power[:], 1.0).then_inc(self.gating, 1)
        dve.wait_ge(self.gating, at.u * 5 + 1)
        V.reciprocal(self.power[:], self.sigma[:]).then_inc(self.gating, 1)
        dve.wait_ge(self.gating, at.u * 5 + 2)
        V.tensor_tensor(self.gate_sum[:], self.power[:, :, 0:1], self.power[:, :, 1:2],
                        ALU.add).then_inc(self.gating, 1)
        dve.wait_ge(self.gating, at.u * 5 + 3)
        V.tensor_scalar(self.twice[:], self.gate_sum[:], 1e-10, 2.0, ALU.add, ALU.mult).then_inc(self.gating, 1)
        dve.wait_ge(self.gating, at.u * 5 + 4)
        V.reciprocal(self.gate_sum[:], self.twice[:]).then_inc(self.gating, 1)
        dve.wait_ge(self.gating, at.u * 5 + 5)
        V.tensor_tensor(self.r["gate"][:, bass.ds(at.u * NT, NT), :], self.power[:],
                        self.gate_sum[:].to_broadcast([P, NT, 2]), ALU.mult)

    def scatter(self, pool, at):
        pool.wait_ge(self.at_done, at.u + 1)
        pool.sem_inc(self.scattering, 1)
        for i in range(NT):
            for j in range(2):
                self.nc.gpsimd.indirect_dma_start(
                    self.slots["x"], bass.IndirectOffsetOnAxis(ap=self.at_now[at.par][:, i, j:j + 1], axis=0),
                    self.norm.xn[at.par][:, i, :], None).then_inc(self.scattered[at.par], 16)


def route_stage(nc, name, src, const, w, r, slots, load):
    with ExitStack() as ctx:
        ps = lambda n, s: ctx.enter_context(nc.psum_tensor(f"{name}_{n}", s, F32))
        norm = Norm(nc, ctx, f"{name}_norm", src, const, ps("xt_ps", [P, T]))
        router = Router(nc, ctx, name, norm, w, r, slots, ps("logit_ps", [P, NT, E])[:],
                        ps("ahead_ps", [P, NT, E])[:], ps("total_ps", [P, E])[:])
        with nc.Block() as block:
            @block.sync
            def _(sp):
                def iteration(t):
                    if at := t.after(2):
                        norm.load(sp, at, norm.xn_done)

                skewed(sp, iteration, lead=2)
                load(sp)

            @block.gpsimd
            def _(pool):
                def iteration(t):
                    if at := t.after(1):
                        norm.root(pool, at)
                    if at := t.after(0):
                        router.scatter(pool, at)

                skewed(pool, iteration, lead=1)

            @block.tensor
            def _(pe):
                def iteration(t):
                    if at := t.after(0):
                        router.logits(pe, at)
                        router.count(pe, at)
                    if at := t.after(1):
                        norm.transpose(pe, at)

                skewed(pe, iteration, lead=1)

            @block.scalar
            def _(act):
                def iteration(t):
                    if at := t.after(0):
                        router.exponent(act, at)
                    if at := t.after(1):
                        router.copy_xt(act, at)

                skewed(act, iteration, lead=1)

            @block.vector
            def _(dve):
                def iteration(t):
                    if at := t.after(1):
                        norm.statistics(dve, at)
                    if at := t.after(0):
                        router.choose(dve, at)
                        router.positions(dve, at)
                    if at := t.after(1):
                        router.normalise(dve, at)
                    if at := t.after(0):
                        router.gates(dve, at)

                router.begin(dve)
                skewed(dve, iteration, lead=1)


def finish_routes(nc, ctx, name, w, r, slots, experts, clear):
    sb = lambda n, s, d=F32: ctx.enter_context(nc.sbuf_tensor(f"{name}_{n}", s, d))
    hi, lo = sb("hi", [P, E, 2 * HID], F32R), sb("lo", [P, E, 2 * HID], F32R)
    plain, scattered = experts["plain"], slots["scattered"]
    CHUNKS = 4
    with ExitStack() as inner:
        sb = lambda n, s, d=F32: inner.enter_context(nc.sbuf_tensor(f"{name}_{n}", s, d))
        sem = lambda n: inner.enter_context(nc.semaphore(f"{name}_{n}"))
        hi_done, step = sem("hi_done"), sem("step")
        filled, tiles, offset, ends = [sb(n, [P, E]) for n in ("filled", "tiles", "offset", "ends")]
        jump = sb("jump", [P, E - 1])
        full, whole = sb("full", [P, E], I32), sb("whole", [P, E], I32)
        tile, summed, start = sb("tile", [P, TILES]), sb("summed", [P, TILES]), sb("start", [P, TILES])
        behind, jumped = [sb(n, [P, TILES, E - 1]) for n in ("behind", "jumped")]
        passed, skipped = [sb(n, [P, B * NT * 2, E - 1]) for n in ("passed", "skipped")]
        rests = sb("rests", [P, B * NT * 2])

        def chunk(k):
            return slice(k * E // CHUNKS, (k + 1) * E // CHUNKS)

        with nc.Block() as block:
            @block.gpsimd
            def _(pool):
                clear(pool)
                for par in range(2):
                    pool.wait_ge(scattered[par], 16 * 2 * NT * (B // 2))

            @block.scalar
            def _(act):
                act.wait_ge(experts["loaded"], 3 * 16)
                for k in range(CHUNKS):
                    nc.scalar.copy(hi[:, chunk(k), :], plain[:, chunk(k), :]).then_inc(hi_done, 1)

            @block.vector
            def _(dve):
                V = nc.vector
                done = [0]

                def then(ins):
                    done[0] += 1
                    ins.then_inc(step, 1)
                    dve.wait_ge(step, done[0])

                then(V.tensor_tensor(filled[:], r["count"][:], w["base"][:], ALU.subtract))
                then(V.tensor_scalar_add(filled[:], filled[:], float(P - 1)))
                then(V.tensor_copy(full[:], filled[:]))
                then(V.tensor_scalar(whole[:], full[:], P.bit_length() - 1, None, ALU.logical_shift_right))
                then(V.tensor_copy(tiles[:], whole[:]))
                for e in range(E):
                    last = V.tensor_reduce(ends[:, e:e + 1], tiles[:, 0:e + 1], AX_X, ALU.add)
                then(last)
                then(V.scalar_tensor_tensor(offset[:], ends[:], -float(P), r["count"][:], ALU.mult, ALU.add))
                then(V.tensor_tensor(jump[:], offset[:, 1:], offset[:, 0:E - 1], ALU.subtract))
                then(V.tensor_scalar(tile[:], w["tile"][:], 1.0, ends[:, E - 1:E], ALU.add, ALU.min))
                then(V.tensor_scalar_add(tile[:], tile[:], -1.0))
                then(V.tensor_tensor(behind[:], tile[:].unsqueeze(2).to_broadcast([P, TILES, E - 1]),
                                     ends[:, 0:E - 1].unsqueeze(1).to_broadcast([P, TILES, E - 1]), ALU.is_ge))
                then(V.tensor_tensor(jumped[:], behind[:], jump[:].unsqueeze(1).to_broadcast([P, TILES, E - 1]),
                                     ALU.mult))
                then(V.tensor_reduce(summed[:], jumped[:], AX_X, ALU.add))
                then(V.scalar_tensor_tensor(start[:], tile[:], float(P), summed[:], ALU.mult, ALU.add))
                V.tensor_scalar_add(r["start"][:], start[0:1, :], offset[0:1, 0:1])
                then(V.tensor_reduce(tile[:], behind[:], AX_X, ALU.add))
                V.tensor_copy(r["expert"][:], tile[0:1, :])
                wide = [P, B * NT * 2, E - 1]
                sent = r["sent"][:].rearrange("p i j -> p (i j)")
                then(V.tensor_tensor(passed[:], sent.unsqueeze(2).to_broadcast(wide),
                                     w["base"][:, 1:].unsqueeze(1).to_broadcast(wide), ALU.is_ge))
                then(V.tensor_tensor(skipped[:], passed[:], jump[:].unsqueeze(1).to_broadcast(wide), ALU.mult))
                then(V.tensor_reduce(rests[:], skipped[:], AX_X, ALU.add))
                then(V.tensor_scalar_add(rests[:], rests[:], offset[:, 0:1]))
                V.tensor_tensor(r["at"][:].rearrange("p i j -> p (i j)"), sent, rests[:], ALU.subtract)
                for k in range(CHUNKS):
                    dve.wait_ge(hi_done, k + 1)
                    V.tensor_tensor(lo[:, chunk(k), :], plain[:, chunk(k), :], hi[:, chunk(k), :].bitcast(F32),
                                    ALU.subtract)
    return dict(hi=hi, lo=lo, down=experts["down"])


def expert_stage(nc, name, const, w, r, slots, beside):
    WAYS, AHEAD = 8, 6
    with ExitStack() as ctx:
        sb = lambda n, s, d=F32: ctx.enter_context(nc.sbuf_tensor(f"{name}_{n}", s, d))
        ps = lambda n, s: ctx.enter_context(nc.psum_tensor(f"{name}_{n}", s, F32))
        sem = lambda n: ctx.enter_context(nc.semaphore(f"{name}_{n}"))
        x = [sb(f"x{k}", [P, D]) for k in range(WAYS)]
        hi = [sb(f"hi{k}", [P, P], F32R) for k in range(2)]
        lo = [sb(f"lo{k}", [P, P], F32R) for k in range(2)]
        silu = [sb(f"silu{k}", [P, HID]) for k in range(2)]
        h = [sb(f"h{k}", [P, 2, P]) for k in range(2)]
        ht = [sb(f"ht{k}", [P, 2, P]) for k in range(2)]
        y = [sb(f"y{k}", [P, 2, D]) for k in range(WAYS // 2)]
        xt_ps = [ps(f"xt_ps{k}", [P, P]) for k in range(2)]
        up_ps = [ps(f"up_ps{k}", [P, 2 * HID]) for k in range(2)]
        ht_ps = [ps(f"ht_ps{k}", [P, 2, P]) for k in range(2)]
        y_ps = [ps(f"y_ps{k}", [P, D]) for k in range(2)]
        x_loaded = [sem(f"x_loaded{k}") for k in range(WAYS)]
        y_stored = [sem(f"y_stored{k}") for k in range(WAYS // 2)]
        xt_done, hi_done, lo_done, up_done, silu_done, h_done, ht_done, ht_copied, y_done, y_copied = [
            sem(n) for n in ("xt_done", "hi_done", "lo_done", "up_done", "silu_done", "h_done", "ht_done",
                             "ht_copied", "y_done", "y_copied")]

        with nc.Block() as block:
            @block.sync
            def _(sp):
                def iteration(t):
                    if at := t.after(AHEAD):
                        if t.after(AHEAD - WAYS):
                            sp.wait_ge(xt_done, t.u + AHEAD - WAYS + 1)
                        row = sp.value_load(r["start"][0:1, bass.ds(at.u, 1)], min_val=0, max_val=X_ROWS - P)
                        sp.dma_start(x[at.par][:], slots["x"][bass.ds(row, P), :]).then_inc(x_loaded[at.par], 16)
                    if t.par % 2 and (at := t.after(-3)):
                        sp.wait_ge(y_copied, at.u + 2)
                        sp.dma_start(slots["y"][bass.ds(at.u * P, 2 * P), :].rearrange("(k p) d -> p k d", p=P),
                                     y[at.par // 2][:]).then_inc(y_stored[at.par // 2], 16)

                skewed(sp, iteration, lead=AHEAD, lag=4, n=TILES, ways=WAYS)
                for k in range(WAYS // 2):
                    sp.wait_ge(y_stored[k], 16 * TILES // WAYS)

            @block.gpsimd
            def _(pool):
                for load in beside:
                    load(pool)

            @block.tensor
            def _(pe):
                expert_of = [pe.alloc_register(f"{name}_expert{k}") for k in range(WAYS)]

                def iteration(t):
                    if at := t.after(0):
                        expert = pe.snap(expert_of[at.par], min_val=0, max_val=E - 1)
                        pe.wait_ge(lo_done, at.u + 1)
                        if t.after(-2):
                            pe.wait_ge(h_done, at.u - 1)
                        k = at.par % 2
                        one = bass.ds(expert, 1)
                        nc.tensor.matmul(up_ps[k][:], hi[k][:], w["hi"][:, one, :], start=True, stop=False)
                        nc.tensor.matmul(up_ps[k][:], lo[k][:], w["hi"][:, one, :], start=False, stop=False)
                        nc.tensor.matmul(up_ps[k][:], hi[k][:], w["lo"][:, one, :], start=False,
                                         stop=True).then_inc(up_done, 1)
                    if at := t.after(1):
                        pe.reg_load(expert_of[at.par], r["expert"][0:1, bass.ds(at.u, 1)])
                    if at := t.after(-1):
                        pe.wait_ge(h_done, at.u + 1)
                        for c in range(2):
                            last = nc.tensor.transpose(ht_ps[at.par % 2][:, c, :], h[at.par % 2][:, c, :],
                                                       const["ident"][:])
                        last.then_inc(ht_done, 1)
                    if at := t.after(2):
                        pe.wait_ge(x_loaded[at.par], 16 * (at.pair + 1))
                        nc.tensor.transpose(xt_ps[at.par % 2][:], x[at.par][:], const["ident"][:]).then_inc(xt_done, 1)
                    if at := t.after(-2):
                        expert = pe.snap(expert_of[at.par], min_val=0, max_val=E - 1)
                        pe.wait_ge(ht_copied, at.u + 1)
                        if at.after(-2):
                            pe.wait_ge(y_copied, at.u - 1)
                        for c in range(2):
                            last = nc.tensor.matmul(y_ps[at.par % 2][:], ht[at.par % 2][:, c, :],
                                                    w["down"][:, bass.ds(expert * 2 + c, 1), :],
                                                    start=(c == 0), stop=(c == 1))
                        last.then_inc(y_done, 1)

                skewed(pe, iteration, lead=2, lag=2, n=TILES, ways=WAYS)

            @block.scalar
            def _(act):
                def iteration(t):
                    if at := t.after(0):
                        act.wait_ge(up_done, at.u + 1)
                        if t.after(-2):
                            act.wait_ge(h_done, at.u - 1)
                        nc.scalar.activation(silu[at.par % 2][:], up_ps[at.par % 2][:, 0:HID],
                                             ACT.Silu).then_inc(silu_done, 1)
                    if at := t.after(-1):
                        act.wait_ge(ht_done, at.u + 1)
                        if at.after(-2):
                            act.wait_ge(y_done, at.u - 1)
                        nc.scalar.copy(ht[at.par % 2][:], ht_ps[at.par % 2][:]).then_inc(ht_copied, 1)
                    if at := t.after(2):
                        act.wait_ge(xt_done, at.u + 1)
                        nc.scalar.copy(hi[at.par % 2][:], xt_ps[at.par % 2][:]).then_inc(hi_done, 1)

                skewed(act, iteration, lead=2, lag=1, n=TILES, ways=WAYS)

            @block.vector
            def _(dve):
                def iteration(t):
                    if at := t.after(0):
                        dve.wait_ge(silu_done, at.u + 1)
                        if t.after(-2):
                            dve.wait_ge(ht_done, at.u - 1)
                        nc.vector.tensor_tensor(h[at.par % 2][:], silu[at.par % 2][:].rearrange("p (c h) -> p c h", c=2),
                                                up_ps[at.par % 2][:, HID:].rearrange("p (c h) -> p c h", c=2),
                                                ALU.mult).then_inc(h_done, 1)
                    if at := t.after(2):
                        dve.wait_ge(hi_done, at.u + 1)
                        nc.vector.tensor_tensor(lo[at.par % 2][:], xt_ps[at.par % 2][:], hi[at.par % 2][:].bitcast(F32),
                                                ALU.subtract).then_inc(lo_done, 1)
                    if at := t.after(-2):
                        dve.wait_ge(y_done, at.u + 1)
                        dve.wait_ge(y_stored[at.par // 2], 16 * at.pair)
                        nc.vector.tensor_copy(y[at.par // 2][:, at.par % 2, :], y_ps[at.par % 2][:]).then_inc(y_copied, 1)

                skewed(dve, iteration, lead=2, lag=2, n=TILES, ways=WAYS)




class Combined(Norm):

    def __init__(self, nc, ctx, name, src, const, xt_ps, r, slots):
        super().__init__(nc, ctx, name, src, const, xt_ps)
        sb = lambda n, s, d=F32: ctx.enter_context(nc.sbuf_tensor(f"{name}_{n}", s, d))
        sem = lambda n: ctx.enter_context(nc.semaphore(f"{name}_{n}"))
        self.r, self.slots, self.gathered = r, slots, slots["gathered"]
        self.before = [sb(f"before{k}", [P, NT, D]) for k in range(2)]
        self.result = [sb(f"result{k}", [P, NT, 2, D]) for k in range(2)]
        self.gate = [sb(f"gate{k}", [P, NT, 2]) for k in range(2)]
        self.place = [sb(f"place{k}", [P, NT, 2], U32) for k in range(2)]
        self.taken, self.half_combined, self.gathering = sem("taken"), sem("half_combined"), sem("gathering")
        self.combined = [sem(f"combined{k}") for k in range(2)]

    def load(self, sp, at):
        u, pair, par = at.u, at.pair, at.par
        sp.wait_ge(self.combined[par], pair)
        src = self.src.rearrange("b (i p) d -> b p i d", p=P)
        sp.dma_start(self.before[par][:], src[u]).then_inc(self.x_loaded[par], 16)

    def take(self, dve, at):
        nc, u, pair, par = self.nc, at.u, at.pair, at.par
        dve.wait_ge(self.gathered[par], 16 * 2 * NT * pair)
        dve.wait_ge(self.combined[par], pair)
        nc.vector.tensor_copy(self.gate[par][:], self.r["gate"][:, bass.ds(u * NT, NT), :])
        nc.vector.tensor_copy(self.place[par][:], self.r["at"][:, bass.ds(u * NT, NT), :]).then_inc(self.taken, 1)

    def gather(self, pool, at):
        nc, u, pair, par = self.nc, at.u, at.pair, at.par
        pool.wait_ge(self.taken, u + 1)
        pool.wait_ge(self.combined[par], pair)
        pool.sem_inc(self.gathering, 1)
        for i in range(NT):
            for j in range(2):
                nc.gpsimd.indirect_dma_start(
                    self.result[par][:, i, j, :], None, self.slots["y"],
                    bass.IndirectOffsetOnAxis(ap=self.place[par][:, i, j:j + 1], axis=0)).then_inc(
                        self.gathered[par], 16)

    def combine(self, dve, at, x_free, step):
        nc, u, pair, par = self.nc, at.u, at.pair, at.par
        dve.wait_ge(self.x_loaded[par], 16 * (pair + 1))
        dve.wait_ge(self.gathered[par], 16 * 2 * NT * (pair + 1))
        for i in range(NT):
            last = nc.vector.scalar_tensor_tensor(self.before[par][:, i, :], self.result[par][:, i, 0, :],
                                                  self.gate[par][:, i, 0:1], self.before[par][:, i, :],
                                                  ALU.mult, ALU.add)
        last.then_inc(self.half_combined, 1)
        dve.wait_ge(self.half_combined, u + 1)
        dve.wait_ge(x_free[par], step * pair)
        for i in range(NT):
            last = nc.vector.scalar_tensor_tensor(self.x[par][:, i, :], self.result[par][:, i, 1, :],
                                                  self.gate[par][:, i, 1:2], self.before[par][:, i, :],
                                                  ALU.mult, ALU.add)
        last.then_inc(self.combined[par], 1)

    def wait_for_x(self, dve, at):
        dve.wait_ge(self.combined[at.par], at.pair + 1)


def macaron_kernel(nc, x, w_qk, w_v, w_out, b_out, cos, sin, router, w_gate, w_up, w_down, w_causal, b_causal,
                   u1, v1, b1, u2, v2, b2, out):
    dram = lambda n, s: nc.dram_tensor(n, s, F32).ap()
    between = [dram(f"between{k}", [B, T, D]) for k in range(4)]

    def make_slots(name):
        sem = lambda n: whole.enter_context(nc.semaphore(f"{name}_{n}"))
        return dict(x=dram(f"{name}_sorted_x", [X_ROWS, D]), y=dram(f"{name}_sorted_y", [Y_ROWS, D]),
                    scattered=[sem(f"scattered{k}") for k in range(2)],
                    gathered=[sem(f"gathered{k}") for k in range(2)])

    def run_experts(name, r, slots, beside):
        with ExitStack() as ctx:
            w = finish_routes(nc, ctx, f"{name}_finish", w_route, r, slots, experts, clearing(nc, cleared))
            expert_stage(nc, f"{name}_expert", const, w, r, slots, beside)

    cleared = set()
    with ExitStack() as whole:
        const = make_constants(nc, whole)
        slots_a, slots_b = make_slots("moe_a"), make_slots("moe_b")
        w_route = make_route_constants(nc, whole, router, (slots_a, slots_b))
        experts, load = load_experts(nc, whole, w_gate, w_up, w_down)
        r_b = make_tables(nc, whole, "moe_b_tables")
        with ExitStack() as first:
            r_a = make_tables(nc, first, "moe_a_tables")
            w_heads, load_heads = make_heads_weights(nc, first, w_qk, w_v, w_out, b_out, cos, sin)
            route_stage(nc, "route_a", x, const, w_route, r_a, slots_a, load)
            run_experts("moe_a", r_a, slots_a, [load_heads])
            heads_stage(nc, "heads", x, between[0], between[1], const, w_heads, r_a, slots_a, w_route, r_b, slots_b)
        w_ffn, load_ffn = make_ffn_weights(nc, whole, u1, v1, b1, u2, v2, b2)
        w_causal, load_causal = make_causal_weights(nc, whole, w_causal, b_causal)
        run_experts("moe_b", r_b, slots_b, [load_ffn, load_causal])
        clear = clearing(nc, set())
        with nc.Block() as block:
            @block.gpsimd
            def _(pool):
                clear(pool)
        ffn_stage(nc, "ffn_a", between[1], between[2], const, w_ffn, (r_b, slots_b))
        causal_stage(nc, "causal", between[2], between[3], const, w_causal)
        ffn_stage(nc, "ffn_b", between[3], out, const, w_ffn)


HEADS, D_HEAD = 16, 8


def _rope_tables():
    import numpy as np
    theta = (1.0 / np.float32(10000.0) ** (np.arange(0, D_HEAD, 2, dtype=np.float32) / np.float32(D_HEAD))).astype(np.float32)
    angles = np.outer(np.arange(T, dtype=np.float32), theta)
    angles = np.concatenate([angles, angles], axis=-1)
    sign = np.where(np.arange(D_HEAD) < D_HEAD // 2, -1, 1).astype(np.float32)
    rows = lambda tab: np.ascontiguousarray(np.broadcast_to(tab.T[None, :, None, :], (2, D_HEAD, HEADS // 2, T)).reshape(D, T))
    return rows(np.cos(angles).astype(np.float32)), rows(np.sin(angles).astype(np.float32) * sign)


def kernel(**inputs):
    import numpy as np
    import concourse.bacc as _bacc
    from concourse.bass_utils import run_bass_kernel_spmd as _run

    given = {k: np.asarray(v) for k, v in inputs.items()}
    w_qkv = given["L0_attn_w_qkv"]
    cos, sin = _rope_tables()
    laid = dict(
        x=given["L0_attn_x"],
        w_qk=w_qkv[:, :2 * D].reshape(D, 2, HEADS // 2, 2, D_HEAD).transpose(0, 1, 3, 4, 2).reshape(D, 2, D),
        w_v=w_qkv[:, 2 * D:], w_out=given["L0_attn_w_out"], b_out=given["L0_attn_b_out"], cos=cos, sin=sin,
        router=given["L0_ffn_router_w"].T, w_gate=given["L0_ffn_w_gate"], w_up=given["L0_ffn_w_up"],
        w_down=given["L0_ffn_w_down"], w_causal=given["L1_attn_W"], b_causal=given["L1_attn_b"],
        u1=given["L1_ffn_U1"], v1=given["L1_ffn_V1"], b1=given["L1_ffn_b1"], u2=given["L1_ffn_U2"],
        v2=given["L1_ffn_V2"], b2=given["L1_ffn_b2"])
    nc = _bacc.Bacc("TRN2", target_bir_lowering=False, num_devices=1)
    arrays, args = {}, []
    for name, a in laid.items():
        a = np.ascontiguousarray(a)
        arrays[f"in_{name}_dram"] = a
        args.append(nc.dram_tensor(f"in_{name}_dram", a.shape, mybir.dt.from_np(a.dtype), kind="ExternalInput").ap())
    args.append(nc.dram_tensor("out_0_dram", (B, T, D), F32, kind="ExternalOutput").ap())
    macaron_kernel(nc, *args)
    r = _run(nc, [arrays], core_ids=[0])
    return r.results[0]["out_0_dram"]
```
